# Optimizing a Trainium2 kernel written in Bass

```python
import numpy as np
import jax
import jax.numpy as jnp

def _softmax(x, axis=-1):
    return jax.nn.softmax(x, axis=axis)

def _gelu(x):
    return jax.nn.gelu(x, approximate=True)

def _silu(x):
    return jax.nn.silu(x)

def _sigmoid(x):
    return jax.nn.sigmoid(x)

def _layernorm(x, axis=-1, eps=1e-05):
    m = jnp.mean(x, axis=axis, keepdims=True)
    v = jnp.var(x, axis=axis, keepdims=True)
    return (x - m) / jnp.sqrt(v + eps)

def _scatter_add(tgt, idx, src, axis=0):
    return tgt.at[idx].add(src)

def _segment_sum(src, seg, n):
    return jax.ops.segment_sum(src, seg, n)
kernel_name = 'mk_xattn_ffn_d2_seqx_r4_c33dec'

def setup_inputs(seed: int=0):
    np.random.seed(seed)
    _w = jnp.asarray

    def _rec_inputs():
        import jax
        import jax.numpy as jnp
        _rk = jax.random.key(seed)
        x = -0.0002928 + 1 * jax.random.normal(jax.random.fold_in(_rk, 1), (8, 256, 256), jnp.float32)
        _lenS = 256 - jax.random.randint(jax.random.fold_in(_rk, 7), (8,), 0, max(1, 256 // 4) + 1, jnp.int32)
        _lenS2 = 256 - jax.random.randint(jax.random.fold_in(_rk, 8), (8,), 0, max(1, 256 // 4) + 1, jnp.int32)
        _ctx_1024P = jax.random.normal(jax.random.fold_in(_rk, 11), (8, 16, 256), jnp.float32)
        _ctx_1024c = jax.random.dirichlet(jax.random.fold_in(_rk, 511), 0.3 * jnp.ones((16,), jnp.float32), (8, 256))
        _ctx_1024t = jnp.einsum('bsk,bkd->bsd', _ctx_1024c, _ctx_1024P)
        _ctx_1024t = _ctx_1024t * jax.lax.rsqrt(jnp.mean(jnp.square(_ctx_1024t)) + 1e-12) * 0.953939
        ctx_1024 = -1.39393e-06 + 0.999914 * (_ctx_1024t + 0.3 * jax.random.normal(jax.random.fold_in(_rk, 611), (8, 256, 256), jnp.float32))
        _validS = jnp.arange(256)[None, :] < _lenS[:, None]
        _validS2 = jnp.arange(256)[None, :] < _lenS2[:, None]
        _causal = jnp.tril(jnp.ones((256, 256), dtype=bool))
        mask_1x1xSxS2_ik0 = jnp.where(jnp.broadcast_to(_validS2[0:1, None, None, :], (1, 1, 256, 256)), 0, 1).astype(jnp.int32)
        return (x, ctx_1024, mask_1x1xSxS2_ik0)
    x, ctx_1024, mask_1x1xSxS2_ik0 = _rec_inputs()

    def _L0_xattn_setup():
        import jax, jax.numpy as jnp
        import numpy as np
        D_MODEL = 256
        NUM_HEADS = 16
        D_K = D_MODEL // NUM_HEADS
        B, S = (2, 512)

        def _split_heads(x):
            b, s, _ = x.shape
            return x.reshape(b, s, NUM_HEADS, D_K).transpose(0, 2, 1, 3)
        key = jax.random.key(seed)
        ks = jax.random.split(key, 11)
        scale = 1.0 / np.sqrt(D_MODEL)
        inp = {'Q': jax.random.normal(ks[0], (B, S, D_MODEL), jnp.float32), 'K': jax.random.normal(ks[1], (B, S, D_MODEL), jnp.float32), 'V': jax.random.normal(ks[2], (B, S, D_MODEL), jnp.float32), 'mask': jnp.tril(jnp.ones((S, S), jnp.int32))[None, None, :, :], 'Wq': jax.random.normal(ks[3], (D_MODEL, D_MODEL), jnp.float32) * scale, 'bq': jax.random.normal(ks[4], (D_MODEL,), jnp.float32) * scale, 'Wk': jax.random.normal(ks[5], (D_MODEL, D_MODEL), jnp.float32) * scale, 'bk': jax.random.normal(ks[6], (D_MODEL,), jnp.float32) * scale, 'Wv': jax.random.normal(ks[7], (D_MODEL, D_MODEL), jnp.float32) * scale, 'bv': jax.random.normal(ks[8], (D_MODEL,), jnp.float32) * scale, 'Wo': jax.random.normal(ks[9], (D_MODEL, D_MODEL), jnp.float32) * scale, 'bo': jax.random.normal(ks[10], (D_MODEL,), jnp.float32) * scale}
        return inp
    _L0_xattn_all = _L0_xattn_setup()
    _L0_xattn_in = {k: v for k, v in _L0_xattn_all.items() if k in ('Wq', 'bq', 'Wk', 'bk', 'Wv', 'bv', 'Wo', 'bo')}
    del _L0_xattn_all

    def _L0_ffn_setup():
        import jax, jax.numpy as jnp
        import numpy as np
        DIM = 256
        E = 8
        K = 2
        EPS = 1e-05

        def _ln(x, g, b):
            mu = jnp.mean(x, axis=-1, keepdims=True)
            var = jnp.mean(jnp.square(x - mu), axis=-1, keepdims=True)
            return (x - mu) * jax.lax.rsqrt(var + EPS) * g + b
        key = jax.random.key(seed)
        ks = jax.random.split(key, 8)
        H = 2 * DIM
        s_in = 1.0 / np.sqrt(DIM)
        s_h = 1.0 / np.sqrt(H)
        return {'x': jax.random.normal(ks[0], (2, 512, DIM), dtype=jnp.float32), 'gate_w': jax.random.uniform(ks[1], (DIM, E), minval=-s_in, maxval=s_in, dtype=jnp.float32), 'w1': jax.random.uniform(ks[2], (E, DIM, H), minval=-s_in, maxval=s_in, dtype=jnp.float32), 'b1': jax.random.uniform(ks[3], (E, H), minval=-s_in, maxval=s_in, dtype=jnp.float32), 'ln1_g': jnp.ones((E, H), dtype=jnp.float32), 'ln1_b': jnp.zeros((E, H), dtype=jnp.float32), 'w2': jax.random.uniform(ks[4], (E, H, DIM), minval=-s_h, maxval=s_h, dtype=jnp.float32), 'b2': jax.random.uniform(ks[5], (E, DIM), minval=-s_h, maxval=s_h, dtype=jnp.float32), 'ln_g': jnp.ones((DIM,), dtype=jnp.float32), 'ln_b': jnp.zeros((DIM,), dtype=jnp.float32)}
    _L0_ffn_all = _L0_ffn_setup()
    _L0_ffn_in = {k: v for k, v in _L0_ffn_all.items() if k in ('gate_w', 'w1', 'b1', 'ln1_g', 'ln1_b', 'w2', 'b2', 'ln_g', 'ln_b')}
    del _L0_ffn_all

    def _L1_xattn_setup():
        import jax, jax.numpy as jnp
        import numpy as np
        HEADS = 16
        key = jax.random.key(seed)
        ks = jax.random.split(key, 8)
        b, t, k = (2, 512, 256)
        scale = 1.0 / np.sqrt(k)
        return {'Q': jax.random.normal(ks[0], (b, t, k), dtype=jnp.float32), 'K': jax.random.normal(ks[1], (b, t, k), dtype=jnp.float32), 'V': jax.random.normal(ks[2], (b, t, k), dtype=jnp.float32), 'Wq': jax.random.normal(ks[3], (k, k), dtype=jnp.float32) * scale, 'Wk': jax.random.normal(ks[4], (k, k), dtype=jnp.float32) * scale, 'Wv': jax.random.normal(ks[5], (k, k), dtype=jnp.float32) * scale, 'Wu': jax.random.normal(ks[6], (k, k), dtype=jnp.float32) * scale, 'bu': jax.random.normal(ks[7], (k,), dtype=jnp.float32) * 0.01}
    _L1_xattn_all = _L1_xattn_setup()
    _L1_xattn_in = {k: v for k, v in _L1_xattn_all.items() if k in ('Wq', 'Wk', 'Wv', 'Wu', 'bu')}
    del _L1_xattn_all

    def _L1_ffn_setup():
        import jax, jax.numpy as jnp
        import numpy as np
        DIM = 256
        INTER = 256
        E = 32
        K = 4
        G = 8
        LG = 4
        ROUTE_SCALE = 1.0
        CAP_FACTOR = 1.25
        B, S = (4, 512)

        def _gate(xf, wg):
            logits = xf @ wg.T
            scores = jax.nn.softmax(logits, axis=-1)
            sg = scores.reshape(-1, G, E // G)
            group_scores = sg.max(axis=-1)
            _, gtop = jax.lax.top_k(group_scores, LG)
            keep_g = jnp.sum(jax.nn.one_hot(gtop, G, dtype=jnp.float32), axis=1) > 0
            masked = jnp.where(keep_g[:, :, None], sg, -jnp.inf).reshape(-1, E)
            _, idx = jax.lax.top_k(masked, K)
            w = jnp.take_along_axis(scores, idx, axis=1)
            w = w / (w.sum(-1, keepdims=True) + 1e-09) * ROUTE_SCALE
            return (w.astype(xf.dtype), idx)

        def _forward(x, wg, w1, w2, w3, sw1, sw2, sw3):
            shape = x.shape
            xf = x.reshape(-1, DIM)
            N = xf.shape[0]
            cap = max(1, int(CAP_FACTOR * N * K / E))
            w, idx = _gate(xf, wg)
            fe = idx.reshape(-1)
            oh = jax.nn.one_hot(fe, E, dtype=jnp.int32)
            pos = (jnp.cumsum(oh, axis=0) * oh).sum(-1) - 1
            keep = pos < cap
            dest = jnp.where(keep, fe * cap + pos, E * cap)
            tok = jnp.arange(N * K, dtype=jnp.int32) // K
            buf_tok = jnp.full((E * cap + 1,), N, jnp.int32).at[dest].set(tok)[:-1]
            buf_w = jnp.zeros((E * cap + 1,), x.dtype).at[dest].set(w.reshape(-1))[:-1]
            xp = jnp.concatenate([xf, jnp.zeros((1, DIM), x.dtype)], axis=0)
            xe = xp[buf_tok].reshape(E, cap, DIM)
            h = jax.nn.silu(jnp.einsum('ecd,edh->ech', xe, w1)) * jnp.einsum('ecd,edh->ech', xe, w3)
            out = jnp.einsum('ech,ehd->ecd', h, w2) * buf_w.reshape(E, cap, 1)
            y = jnp.zeros((N + 1, DIM), x.dtype).at[buf_tok].add(out.reshape(E * cap, DIM))[:N]
            z = jax.nn.silu(xf @ sw1) * (xf @ sw3) @ sw2
            return (y + z).reshape(shape)
        key = jax.random.key(seed)
        ks = jax.random.split(key, 9)
        sd = DIM ** (-0.5)
        si = INTER ** (-0.5)
        x = jax.random.normal(ks[0], (B, S, DIM), jnp.float32)
        wg = jax.random.normal(ks[1], (E, DIM), jnp.float32) * sd
        w1 = jax.random.normal(ks[2], (E, DIM, INTER), jnp.float32) * sd
        w3 = jax.random.normal(ks[3], (E, DIM, INTER), jnp.float32) * sd
        w2 = jax.random.normal(ks[4], (E, INTER, DIM), jnp.float32) * si
        sw1 = jax.random.normal(ks[5], (DIM, INTER), jnp.float32) * sd
        sw3 = jax.random.normal(ks[6], (DIM, INTER), jnp.float32) * sd
        sw2 = jax.random.normal(ks[7], (INTER, DIM), jnp.float32) * si
        return dict(x=x, wg=wg, w1=w1, w2=w2, w3=w3, sw1=sw1, sw2=sw2, sw3=sw3)
    _L1_ffn_all = _L1_ffn_setup()
    _L1_ffn_in = {k: v for k, v in _L1_ffn_all.items() if k in ('wg', 'w1', 'w2', 'w3', 'sw1', 'sw2', 'sw3')}
    del _L1_ffn_all
    return {'x': x, 'ctx_1024': ctx_1024, 'mask_1x1xSxS2_ik0': mask_1x1xSxS2_ik0, 'L0_xattn_Wq': _L0_xattn_in['Wq'], 'L0_xattn_bq': _L0_xattn_in['bq'], 'L0_xattn_Wk': _L0_xattn_in['Wk'], 'L0_xattn_bk': _L0_xattn_in['bk'], 'L0_xattn_Wv': _L0_xattn_in['Wv'], 'L0_xattn_bv': _L0_xattn_in['bv'], 'L0_xattn_Wo': _L0_xattn_in['Wo'], 'L0_xattn_bo': _L0_xattn_in['bo'], 'L0_ffn_gate_w': _L0_ffn_in['gate_w'], 'L0_ffn_w1': _L0_ffn_in['w1'], 'L0_ffn_b1': _L0_ffn_in['b1'], 'L0_ffn_ln1_g': _L0_ffn_in['ln1_g'], 'L0_ffn_ln1_b': _L0_ffn_in['ln1_b'], 'L0_ffn_w2': _L0_ffn_in['w2'], 'L0_ffn_b2': _L0_ffn_in['b2'], 'L0_ffn_ln_g': _L0_ffn_in['ln_g'], 'L0_ffn_ln_b': _L0_ffn_in['ln_b'], 'L1_xattn_Wq': _L1_xattn_in['Wq'], 'L1_xattn_Wk': _L1_xattn_in['Wk'], 'L1_xattn_Wv': _L1_xattn_in['Wv'], 'L1_xattn_Wu': _L1_xattn_in['Wu'], 'L1_xattn_bu': _L1_xattn_in['bu'], 'L1_ffn_wg': _L1_ffn_in['wg'], 'L1_ffn_w1': _L1_ffn_in['w1'], 'L1_ffn_w2': _L1_ffn_in['w2'], 'L1_ffn_w3': _L1_ffn_in['w3'], 'L1_ffn_sw1': _L1_ffn_in['sw1'], 'L1_ffn_sw2': _L1_ffn_in['sw2'], 'L1_ffn_sw3': _L1_ffn_in['sw3']}

def reference(x, ctx_1024, mask_1x1xSxS2_ik0, L0_xattn_Wq, L0_xattn_bq, L0_xattn_Wk, L0_xattn_bk, L0_xattn_Wv, L0_xattn_bv, L0_xattn_Wo, L0_xattn_bo, L0_ffn_gate_w, L0_ffn_w1, L0_ffn_b1, L0_ffn_ln1_g, L0_ffn_ln1_b, L0_ffn_w2, L0_ffn_b2, L0_ffn_ln_g, L0_ffn_ln_b, L1_xattn_Wq, L1_xattn_Wk, L1_xattn_Wv, L1_xattn_Wu, L1_xattn_bu, L1_ffn_wg, L1_ffn_w1, L1_ffn_w2, L1_ffn_w3, L1_ffn_sw1, L1_ffn_sw2, L1_ffn_sw3):
    import jax
    import jax.numpy as jnp

    def _L0_xattn_ref(Q, K, V, mask, Wq, bq, Wk, bk, Wv, bv, Wo, bo):
        import jax, jax.numpy as jnp
        import numpy as np
        D_MODEL = 256
        NUM_HEADS = 16
        D_K = D_MODEL // NUM_HEADS
        B, S = (2, 512)

        def _split_heads(x):
            b, s, _ = x.shape
            return x.reshape(b, s, NUM_HEADS, D_K).transpose(0, 2, 1, 3)
        q = _split_heads(Q @ Wq.T + bq)
        k = _split_heads(K @ Wk.T + bk)
        v = _split_heads(V @ Wv.T + bv)
        scores = jnp.einsum('bhqd,bhkd->bhqk', q, k) / jnp.sqrt(jnp.float32(D_K))
        scores = jnp.where(mask == 0, jnp.float32(-1000000000.0), scores)
        probs = jax.nn.softmax(scores, axis=-1)
        attn = jnp.einsum('bhqk,bhkd->bhqd', probs, v)
        attn = attn.transpose(0, 2, 1, 3).reshape(Q.shape[0], Q.shape[1], D_MODEL)
        return attn @ Wo.T + bo

    def _L0_ffn_ref(x, gate_w, w1, b1, ln1_g, ln1_b, w2, b2, ln_g, ln_b):
        import jax, jax.numpy as jnp
        import numpy as np
        DIM = 256
        E = 8
        K = 2
        EPS = 1e-05

        def _ln(x, g, b):
            mu = jnp.mean(x, axis=-1, keepdims=True)
            var = jnp.mean(jnp.square(x - mu), axis=-1, keepdims=True)
            return (x - mu) * jax.lax.rsqrt(var + EPS) * g + b
        shape = x.shape
        xf = x.reshape(-1, shape[-1])
        gates = jax.nn.softmax(xf @ gate_w, axis=-1)
        topw, topi = jax.lax.top_k(gates, K)
        topw = topw / jnp.sum(topw, axis=-1, keepdims=True)
        combine = jnp.sum(topw[:, :, None] * jax.nn.one_hot(topi, E, dtype=xf.dtype), axis=1)
        h = jnp.einsum('td,edh->teh', xf, w1) + b1
        h = _ln(h, ln1_g, ln1_b)
        h = jax.nn.gelu(h, approximate=False)
        y = jnp.einsum('teh,ehd->ted', h, w2) + b2
        out = jnp.einsum('ted,te->td', y, combine)
        out = _ln(out + xf, ln_g, ln_b)
        return out.reshape(shape)

    def _L1_xattn_ref(Q, K, V, Wq, Wk, Wv, Wu, bu):
        import jax, jax.numpy as jnp
        import numpy as np
        HEADS = 16
        b, t, k = Q.shape
        h = HEADS
        s = k // h
        q = (Q @ Wq.T).reshape(b, t, h, s).transpose(0, 2, 1, 3)
        kk = (K @ Wk.T).reshape(b, t, h, s).transpose(0, 2, 1, 3)
        v = (V @ Wv.T).reshape(b, t, h, s).transpose(0, 2, 1, 3)
        scores = jnp.einsum('bhts,bhTs->bhtT', q, kk) / jnp.sqrt(jnp.float32(k))
        w = jax.nn.softmax(scores, axis=-1)
        attn = jnp.einsum('bhtT,bhTs->bhts', w, v)
        out = attn.transpose(0, 2, 1, 3).reshape(b, t, k)
        return out @ Wu.T + bu

    def _L1_ffn_ref(x, wg, w1, w2, w3, sw1, sw2, sw3):
        import jax, jax.numpy as jnp
        import numpy as np
        DIM = 256
        INTER = 256
        E = 32
        K = 4
        G = 8
        LG = 4
        ROUTE_SCALE = 1.0
        CAP_FACTOR = 1.25
        B, S = (4, 512)

        def _gate(xf, wg):
            logits = xf @ wg.T
            scores = jax.nn.softmax(logits, axis=-1)
            sg = scores.reshape(-1, G, E // G)
            group_scores = sg.max(axis=-1)
            _, gtop = jax.lax.top_k(group_scores, LG)
            keep_g = jnp.sum(jax.nn.one_hot(gtop, G, dtype=jnp.float32), axis=1) > 0
            masked = jnp.where(keep_g[:, :, None], sg, -jnp.inf).reshape(-1, E)
            _, idx = jax.lax.top_k(masked, K)
            w = jnp.take_along_axis(scores, idx, axis=1)
            w = w / (w.sum(-1, keepdims=True) + 1e-09) * ROUTE_SCALE
            return (w.astype(xf.dtype), idx)

        def _forward(x, wg, w1, w2, w3, sw1, sw2, sw3):
            shape = x.shape
            xf = x.reshape(-1, DIM)
            N = xf.shape[0]
            cap = max(1, int(CAP_FACTOR * N * K / E))
            w, idx = _gate(xf, wg)
            fe = idx.reshape(-1)
            oh = jax.nn.one_hot(fe, E, dtype=jnp.int32)
            pos = (jnp.cumsum(oh, axis=0) * oh).sum(-1) - 1
            keep = pos < cap
            dest = jnp.where(keep, fe * cap + pos, E * cap)
            tok = jnp.arange(N * K, dtype=jnp.int32) // K
            buf_tok = jnp.full((E * cap + 1,), N, jnp.int32).at[dest].set(tok)[:-1]
            buf_w = jnp.zeros((E * cap + 1,), x.dtype).at[dest].set(w.reshape(-1))[:-1]
            xp = jnp.concatenate([xf, jnp.zeros((1, DIM), x.dtype)], axis=0)
            xe = xp[buf_tok].reshape(E, cap, DIM)
            h = jax.nn.silu(jnp.einsum('ecd,edh->ech', xe, w1)) * jnp.einsum('ecd,edh->ech', xe, w3)
            out = jnp.einsum('ech,ehd->ecd', h, w2) * buf_w.reshape(E, cap, 1)
            y = jnp.zeros((N + 1, DIM), x.dtype).at[buf_tok].add(out.reshape(E * cap, DIM))[:N]
            z = jax.nn.silu(xf @ sw1) * (xf @ sw3) @ sw2
            return (y + z).reshape(shape)
        return _forward(x, wg, w1, w2, w3, sw1, sw2, sw3)
    x = x + _L0_xattn_ref(_layernorm(x, axis=-1), ctx_1024, ctx_1024, mask_1x1xSxS2_ik0, L0_xattn_Wq, L0_xattn_bq, L0_xattn_Wk, L0_xattn_bk, L0_xattn_Wv, L0_xattn_bv, L0_xattn_Wo, L0_xattn_bo)
    x = x + _L0_ffn_ref(_layernorm(x, axis=-1), L0_ffn_gate_w, L0_ffn_w1, L0_ffn_b1, L0_ffn_ln1_g, L0_ffn_ln1_b, L0_ffn_w2, L0_ffn_b2, L0_ffn_ln_g, L0_ffn_ln_b)
    x = x + _L1_xattn_ref(_layernorm(x, axis=-1), ctx_1024, ctx_1024, L1_xattn_Wq, L1_xattn_Wk, L1_xattn_Wv, L1_xattn_Wu, L1_xattn_bu)
    x = x + _L1_ffn_ref(_layernorm(x, axis=-1), L1_ffn_wg, L1_ffn_w1, L1_ffn_w2, L1_ffn_w3, L1_ffn_sw1, L1_ffn_sw2, L1_ffn_sw3)
    return x

_drawn_inputs = setup_inputs


def setup_inputs(seed=0):
    import zlib

    import numpy as np

    out = dict(_drawn_inputs(seed))
    spreads = {'L0_ffn_ln1_g': (1.0, 0.2),
     'L0_ffn_ln1_b': (0.0, 0.429),
     'L0_ffn_ln_g': (1.0, 0.2),
     'L0_ffn_ln_b': (0.0, 0.1)}
    factors = {'L0_xattn_bk': 8.0, 'L0_ffn_b1': 4.725, 'L0_ffn_b2': 3.937, 'L1_xattn_bu': 5.767}
    for name, (base, spread) in spreads.items():
        noise = np.random.default_rng([zlib.crc32(name.encode()), seed]).standard_normal(out[name].shape)
        drawn = base * np.exp(spread * noise) if base else spread * noise
        out[name] = jnp.asarray(drawn.astype(out[name].dtype))
    for name, factor in factors.items():
        out[name] = (out[name] * factor).astype(out[name].dtype)
    return out
```

```python
import numpy as np
import concourse.bass as bass
from concourse import mybir
from contextlib import ExitStack

fp32 = mybir.dt.float32
fp32r = mybir.dt.float32r
bf16 = mybir.dt.bfloat16
int32 = mybir.dt.int32
ALU = mybir.AluOpType
ACT = mybir.ActivationFunctionType
AX = mybir.AxisListType

P = 128
B, S, D = 8, 256, 256
N = B * S
NT = N // P
TB = S // P
KT = D // P
H, DH = 16, 16
HV = 32
HQ = P // HV
NEG = -float(2 ** 100)
EPS = 1e-5
ROW_MAX = 64
STACK = ROW_MAX + 2

E0, K0, H0 = 8, 2, 512
HT0 = H0 // P
TILES0 = N * K0 // P + E0 - 1 + 1
E1, K1, H1 = 32, 4, 256
G1, LG1 = 8, 4
GE1 = E1 // G1
HT1 = H1 // P
CAP = int(1.25 * N * K1 / E1)
SLOTS1 = E1 * CAP
SLOT_TILES = [(s, min(P, CAP - s)) for s in range(0, CAP, P)]


class Program:

    def __init__(self, nc, dram):
        self.nc = nc
        self.dram = dram
        self.sems = {}
        self.stack = ExitStack()
        self.lasting = ExitStack()
        self.top = 16640
        self.limit = 229344

    def sem(self, name):
        if name not in self.sems:
            self.sems[name] = self.stack.enter_context(self.nc.semaphore(name))
        return self.sems[name]

    def pool_dma_sem(self, name):
        return self.lasting.enter_context(self.nc.semaphore(name))

    def renew_semaphores(self):
        with self.nc.Block() as block:
            @block.gpsimd
            def _(pool):
                for sem in self.sems.values():
                    pool.sem_clear(sem)
        self.stack.close()
        self.sems = {}

    def sb(self, name, shape, dtype):
        size = int(np.prod(shape[1:])) * (2 if dtype == bf16 else 4)
        at = self.top
        self.top = (at + size + 31) // 32 * 32
        assert self.top <= self.limit, (name, self.top)
        return self.nc.alloc_sbuf_tensor_at(name, shape, dtype, offset=at)

    def scratch(self, name, shape, dtype):
        return self.nc.dram_tensor(name, shape, dtype, kind="Internal").ap()


def across_partitions(ap, n):
    return bass.AP(ap.tensor, ap.offset, [[0, P], [1, n]])


def load_constants(p):
    nc, d = p.nc, p.dram
    c = {}
    c["x"] = p.sb("x_res", [P, NT, D], fp32)
    for l in (0, 1):
        for w in ("q", "k", "v", "o"):
            c[f"w{w}{l}"] = p.sb(f"w{w}{l}", [P, KT, D], fp32)
    for n in ("bq0", "bk0"):
        c[n] = p.sb(n, [P, KT], fp32)
    for n in ("bv0", "bo0", "bo1"):
        c[n] = p.sb(n, [P, D], fp32)
    c["ident"] = p.sb("ident", [P, P], fp32)
    c["identb"] = p.sb("identb", [P, P], bf16)
    c["mask_qk"] = p.sb("mask_qk", [P, TB, S], bf16)
    c["mask_kq"] = p.sb("mask_kq", [P, TB, S], bf16)
    c["minus_half"] = p.sb("minus_half", [P, NT], fp32)
    start = p.top
    raw = p.sb("mask_raw", [P, 2, TB, S], int32)
    p.top = start

    loaded, made = p.sem("constants_loaded"), p.sem("constants_made")
    ident_zero = p.sem("identity_zeroed")
    n_loads = 2 + 8 + 5 + 1
    with nc.Block() as block:
        @block.sync
        def _(sp):
            sp.dma_start(raw[:, 0], d["mask_qk"]).then_inc(loaded, 16)
            sp.dma_start(raw[:, 1], d["mask_kq"]).then_inc(loaded, 16)
            for l in (0, 1):
                for w in ("q", "k", "v", "o"):
                    sp.dma_start(c[f"w{w}{l}"][:], d[f"w{w}{l}"]).then_inc(loaded, 16)
            sp.dma_start(c["bq0"][:], d["bq0"]).then_inc(loaded, 16)
            sp.dma_start(c["bk0"][:], d["bk0"]).then_inc(loaded, 16)
            for n in ("bv0", "bo0", "bo1"):
                sp.dma_start(c[n][:], across_partitions(d[n], D)).then_inc(loaded, 16)
            sp.dma_start(c["x"][:], d["x"].rearrange("(t p) d -> p t d", p=P)).then_inc(loaded, 16)
            sp.wait_ge(loaded, 16 * n_loads)

        @block.gpsimd
        def _(pool):
            nc.gpsimd.memset(c["ident"][:], 0.0).then_inc(ident_zero, 1)
            nc.gpsimd.memset(c["identb"][:], 0.0).then_inc(ident_zero, 1)
            pool.wait_ge(ident_zero, 2)
            for n in ("ident", "identb"):
                nc.gpsimd.affine_select(out=c[n][:], in_=c[n][:], compare_op=ALU.not_equal, fill=1.0, base=0,
                                        pattern=[[-1, P]], channel_multiplier=1).then_inc(made, 1)

        @block.vector
        def _(dve):
            nc.vector.memset(c["minus_half"][:], -0.5).then_inc(made, 1)
            dve.wait_ge(loaded, 16 * n_loads)
            for n, m in enumerate(("mask_qk", "mask_kq")):
                nc.vector.tensor_scalar(c[m][:], raw[:, n], 0, NEG, ALU.is_equal, ALU.mult).then_inc(made, 1)
            nc.vector.tensor_scalar(c["wq0"][:], c["wq0"][:], DH ** -0.5, None, ALU.mult).then_inc(made, 1)
            nc.vector.tensor_scalar(c["bq0"][:], c["bq0"][:], DH ** -0.5, None, ALU.mult).then_inc(made, 1)
            nc.vector.tensor_scalar(c["wq1"][:], c["wq1"][:], D ** -0.5, None, ALU.mult).then_inc(made, 1)
            dve.wait_ge(made, 8)
    return c


def keys_and_values(p, c):
    nc, d = p.nc, p.dram
    start = p.top
    ctx = [p.sb(f"ctx{u}", [P, KT, S], fp32) for u in (0, 1)]
    kk = [[p.sb(f"k_parts{u}{l}", [P, 2, KT, S], fp32r) for l in (0, 1)] for u in (0, 1)]
    vv = [[p.sb(f"v_ones{u}{l}", [P, TB, H, HV], fp32) for l in (0, 1)] for u in (0, 1)]
    p.top = start
    psum = ExitStack()
    ps_k = [psum.enter_context(nc.psum_tensor(f"ps_k{l}", [P, KT, S], fp32)) for l in (0, 1)]
    ps_v = [psum.enter_context(nc.psum_tensor(f"ps_v{l}", [P, TB, D], fp32)) for l in (0, 1)]
    for l in (0, 1):
        c[f"kd{l}"] = p.scratch(f"kd{l}", [2, D, N], fp32)
        c[f"vd{l}"] = p.scratch(f"vd{l}", [N, H * HV], fp32)

    ctx_loaded = [p.sem(f"ctx_loaded{u}") for u in (0, 1)]
    projected, k_high, emptied = p.sem("kv_projected"), p.sem("k_high"), p.sem("kv_emptied")
    stored, ones = [p.sem(f"kv_stored{u}") for u in (0, 1)], p.sem("v_ones_set")
    STORES = 6
    CREDIT = 2 * 4

    with nc.Block() as block:
        @block.sync
        def _(sp):
            def load(b, u):
                sp.wait_ge(projected, b * 4 + 4)
                sp.dma_start(ctx[u][:], d["ctx"][bass.ds(b, 1)].rearrange("o p k t -> p (o k) t")).then_inc(ctx_loaded[u], 16)

            def store(b, u):
                for l in (0, 1):
                    sp.wait_ge(emptied, b * 4 + 2 * l + 2 + 4)
                    for part in (0, 1):
                        sp.dma_start(c[f"kd{l}"][part, :, bass.ds(b * S, S)].rearrange("(m p) t -> p m t", p=P),
                                     kk[u][l][:, part].bitcast(fp32)).then_inc(stored[u], 16)
                    sp.dma_start(c[f"vd{l}"][bass.ds(b * S, S), :].rearrange("(t p) e -> p t e", p=P),
                                 vv[u][l][:].rearrange("p t h e -> p t (h e)")).then_inc(stored[u], 16)

            for u in (0, 1):
                sp.sem_inc(stored[u], 16 * STORES)
            load(0, 0)
            with sp.Fori(0, B // 2 - 1) as i:
                load(i * 2 + 1, 1)
                store(i * 2, 0)
                load(i * 2 + 2, 0)
                store(i * 2 + 1, 1)
            load(B - 1, 1)
            store(B - 2, 0)
            store(B - 1, 1)
            for u in (0, 1):
                sp.wait_ge(stored[u], (B // 2 + 1) * 16 * STORES)

        @block.tensor
        def _(pe):
            pe.sem_inc(projected, CREDIT)
            with pe.Fori(0, B // 2) as i:
                for u in (0, 1):
                    b = i * 2 + u
                    pe.wait_ge(ctx_loaded[u], i * 16 + 16)
                    for l in (0, 1):
                        pe.wait_ge(emptied, b * 4 + 2 * l + 1)
                        for m in range(KT):
                            for k in range(KT):
                                last = nc.tensor.matmul(ps_k[l][:, m], c[f"wk{l}"][:, k, m * P:(m + 1) * P], ctx[u][:, k],
                                                        start=k == 0, stop=k == KT - 1)
                        last.then_inc(projected, 1)
                        pe.wait_ge(emptied, b * 4 + 2 * l + 2)
                        for t in range(TB):
                            for k in range(KT):
                                last = nc.tensor.matmul(ps_v[l][:, t], ctx[u][:, k, t * P:(t + 1) * P], c[f"wv{l}"][:, k],
                                                        start=k == 0, stop=k == KT - 1)
                        last.then_inc(projected, 1)

        @block.scalar
        def _(act):
            with act.Fori(0, B // 2) as i:
                for u in (0, 1):
                    b = i * 2 + u
                    act.wait_ge(stored[u], i * 16 * STORES + 16 * STORES)
                    for l in (0, 1):
                        act.wait_ge(projected, b * 4 + 2 * l + 1 + CREDIT)
                        for m in range(KT):
                            if l == 0:
                                ins = nc.scalar.activation(kk[u][l][:, 0, m], ps_k[l][:, m], ACT.Identity,
                                                           bias=c["bk0"][:, m:m + 1])
                            else:
                                ins = nc.scalar.activation(kk[u][l][:, 0, m], ps_k[l][:, m], ACT.Copy)
                        ins.then_inc(k_high, 1)

        @block.vector
        def _(dve):
            for u in (0, 1):
                for l in (0, 1):
                    nc.vector.memset(vv[u][l][:, :, :, DH:DH + 1], 1.0).then_inc(ones, 1)
                    nc.vector.memset(vv[u][l][:, :, :, DH + 1:HV], 0.0).then_inc(ones, 1)
            dve.wait_ge(ones, 8)
            dve.sem_inc(emptied, 4)
            with dve.Fori(0, B // 2) as i:
                for u in (0, 1):
                    b = i * 2 + u
                    dve.wait_ge(stored[u], i * 16 * STORES + 16 * STORES)
                    for l in (0, 1):
                        dve.wait_ge(k_high, b * 2 + l + 1)
                        for m in range(KT):
                            high = kk[u][l][:, 0, m].bitcast(fp32)
                            if l == 0:
                                ins = nc.vector.scalar_tensor_tensor(kk[u][l][:, 1, m], ps_k[l][:, m], c["bk0"][:, m:m + 1],
                                                                     high, ALU.add, ALU.subtract)
                            else:
                                ins = nc.vector.tensor_tensor(kk[u][l][:, 1, m], ps_k[l][:, m], high, ALU.subtract)
                        ins.then_inc(emptied, 1)
                        dve.wait_ge(projected, b * 4 + 2 * l + 2 + CREDIT)
                        for t in range(TB):
                            heads = ps_v[l][:, t].rearrange("p (h e) -> p h e", h=H)
                            if l == 0:
                                ins = nc.vector.tensor_tensor(vv[u][l][:, t, :, 0:DH], heads,
                                                              c["bv0"][:].rearrange("p (h e) -> p h e", h=H), ALU.add)
                            else:
                                ins = nc.vector.tensor_copy(vv[u][l][:, t, :, 0:DH], heads)
                        ins.then_inc(emptied, 1)
    psum.close()


def queries(p, c, l):
    nc = p.nc
    start = p.top
    stats = p.sb(f"stats{l}", [P, NT, 6], fp32)
    mv = p.sb(f"mean_var{l}", [P, NT, 2], fp32)
    var = p.sb(f"var{l}", [P, NT], fp32)
    rstd = p.sb(f"rstd{l}", [P, NT], fp32)
    xn = [p.sb(f"xn{l}{u}", [P, TB, D], fp32) for u in (0, 1)]
    xnt = [p.sb(f"xnt{l}{u}", [P, KT, S], fp32) for u in (0, 1)]
    qq = [p.sb(f"q_parts{l}{u}", [P, 2, KT, S], fp32r) for u in (0, 1)]
    p.top = start
    psum = ExitStack()
    ps_t = [psum.enter_context(nc.psum_tensor(f"ps_xt{l}{u}", [P, KT, S], fp32)) for u in (0, 1)]
    ps_q = [psum.enter_context(nc.psum_tensor(f"ps_q{l}{u}", [P, KT, S], fp32)) for u in (0, 1)]
    c[f"qd{l}"] = p.scratch(f"qd{l}", [2, D, N], fp32)
    X = c["x"]

    stats_done, var_done, rstd_done = p.sem(f"stats_done{l}"), p.sem(f"var_done{l}"), p.sem(f"rstd_done{l}")
    xn_done, xt_done, xt_copied = p.sem(f"xn_done{l}"), p.sem(f"xt_done{l}"), p.sem(f"xt_copied{l}")
    q_done, q_high, q_low = p.sem(f"q_done{l}"), p.sem(f"q_high{l}"), p.sem(f"q_low{l}")
    stored = [p.sem(f"q_stored{l}{u}") for u in (0, 1)]
    bias_added = p.sem(f"bias_added{l}")

    with nc.Block() as block:
        @block.sync
        def _(sp):
            for u in (0, 1):
                sp.sem_inc(stored[u], 32)
            with sp.Fori(0, B // 2) as i:
                for u in (0, 1):
                    b = i * 2 + u
                    sp.wait_ge(q_low, b + 3)
                    for part in (0, 1):
                        sp.dma_start(c[f"qd{l}"][part, :, bass.ds(b * S, S)].rearrange("(m p) t -> p m t", p=P),
                                     qq[u][:, part].bitcast(fp32)).then_inc(stored[u], 16)
            for u in (0, 1):
                sp.wait_ge(stored[u], (B // 2 + 1) * 32)

        @block.gpsimd
        def _(pool):
            pool.wait_ge(var_done, 1)
            nc.gpsimd.tensor_tensor(rstd[:], var[:], c["minus_half"][:], ALU.pow).then_inc(rstd_done, 1)
            with pool.Fori(0, B) as b:
                pool.wait_ge(xn_done, b + 1)
                for t in range(TB):
                    at = X[:, bass.ds(b * TB + t, 1), :].rearrange("p o d -> p (o d)")
                    nc.gpsimd.tensor_tensor(at, at, c[f"bo{l}"][:], ALU.add).then_inc(bias_added, 1)
            pool.wait_ge(bias_added, NT)

        @block.vector
        def _(dve):
            with dve.Fori(0, NT) as t:
                nc.vector.bn_stats(stats[:, bass.ds(t, 1), :], X[:, bass.ds(t, 1), :]).then_inc(stats_done, 1)
            dve.wait_ge(stats_done, NT)
            for t in range(NT):
                nc.vector.bn_aggr(mv[:, t], stats[:, t]).then_inc(stats_done, 1)
            dve.wait_ge(stats_done, 2 * NT)
            nc.vector.tensor_scalar(var[:], mv[:, :, 1], EPS, None, ALU.add).then_inc(var_done, 1)
            dve.wait_ge(rstd_done, 1)
            dve.sem_inc(q_low, 2)

            def low(b, u):
                dve.wait_ge(q_high, b + 1)
                for m in range(KT):
                    high = qq[u][:, 0, m].bitcast(fp32)
                    if l == 0:
                        ins = nc.vector.scalar_tensor_tensor(qq[u][:, 1, m], ps_q[u][:, m], c["bq0"][:, m:m + 1],
                                                             high, ALU.add, ALU.subtract)
                    else:
                        ins = nc.vector.tensor_tensor(qq[u][:, 1, m], ps_q[u][:, m], high, ALU.subtract)
                ins.then_inc(q_low, 1)

            def norm(b, u):
                dve.wait_ge(xt_done, b + 1)
                for t in range(TB):
                    tile = b * TB + t
                    ins = nc.vector.tensor_scalar(xn[u][:, t], X[:, bass.ds(tile, 1), :].rearrange("p o d -> p (o d)"),
                                                  mv[:, bass.ds(tile, 1), 0], rstd[:, bass.ds(tile, 1)],
                                                  ALU.subtract, ALU.mult)
                ins.then_inc(xn_done, 1)

            with dve.Fori(0, B // 2) as i:
                norm(i * 2, 0)
                norm(i * 2 + 1, 1)
                low(i * 2, 0)
                low(i * 2 + 1, 1)

        @block.tensor
        def _(pe):
            pe.sem_inc(xt_done, 2)

            def transposes(b, u):
                pe.wait_ge(xn_done, b + 1)
                pe.wait_ge(xt_copied, b + 1)
                for t in range(TB):
                    for k in range(KT):
                        last = nc.tensor.transpose(ps_t[u][:, k, t * P:(t + 1) * P], xn[u][:, t, k * P:(k + 1) * P],
                                                   c["ident"][:])
                last.then_inc(xt_done, 1)

            def project(b, u):
                pe.wait_ge(xt_copied, b + 3)
                pe.wait_ge(q_low, b + 1)
                for m in range(KT):
                    for k in range(KT):
                        last = nc.tensor.matmul(ps_q[u][:, m], c[f"wq{l}"][:, k, m * P:(m + 1) * P], xnt[u][:, k],
                                                start=k == 0, stop=k == KT - 1)
                last.then_inc(q_done, 1)

            with pe.Fori(0, B // 2) as i:
                transposes(i * 2, 0)
                transposes(i * 2 + 1, 1)
                project(i * 2, 0)
                project(i * 2 + 1, 1)

        @block.scalar
        def _(act):
            act.sem_inc(xt_copied, 2)

            def copy(b, u):
                act.wait_ge(xt_done, b + 3)
                act.wait_ge(q_done, b + 1)
                nc.scalar.activation(xnt[u][:], ps_t[u][:], ACT.Copy).then_inc(xt_copied, 1)

            def high(i, b, u):
                act.wait_ge(q_done, b + 3)
                act.wait_ge(stored[u], i * 32 + 32)
                for m in range(KT):
                    if l == 0:
                        ins = nc.scalar.activation(qq[u][:, 0, m], ps_q[u][:, m], ACT.Identity, bias=c["bq0"][:, m:m + 1])
                    else:
                        ins = nc.scalar.activation(qq[u][:, 0, m], ps_q[u][:, m], ACT.Copy)
                ins.then_inc(q_high, 1)

            act.sem_inc(q_done, 2)
            with act.Fori(0, B // 2) as i:
                copy(i * 2, 0)
                copy(i * 2 + 1, 1)
                high(i, i * 2, 0)
                high(i, i * 2 + 1, 1)
    psum.close()


def attention(p, c, l):
    nc = p.nc
    masked = l == 0
    start = p.top
    KS = [p.sb(f"k_stack{l}{u}", [STACK, H, S], fp32r) for u in (0, 1)]
    QS = [p.sb(f"q_stack{l}{u}", [STACK, H, S], fp32r) for u in (0, 1)]
    V = [p.sb(f"v{l}{u}", [P, TB, H, HV], fp32) for u in (0, 1)]
    NMAX = [p.sb(f"neg_max{l}{u}", [P, TB, H], fp32) for u in (0, 1)]
    MT = p.sb(f"neg_max_t{l}", [H, 2, S], fp32r)
    NP = 3
    PT = p.sb(f"probs{l}", [P, NP, TB, S], fp32)
    VT = p.sb(f"mixed_t{l}", [P, 2, S], fp32)
    RINV = p.sb(f"rinv{l}", [P, TB, H], fp32)
    O = p.sb(f"attn{l}", [P, TB, D], fp32)
    OT = p.sb(f"attn_t{l}", [P, KT, S], fp32)
    p.top = start
    psum = ExitStack()
    ps_s = [psum.enter_context(nc.psum_tensor(f"ps_s{l}{u}", [P, 2, S], fp32)) for u in (0, 1)]
    ps_p = [psum.enter_context(nc.psum_tensor(f"ps_p{l}{u}", [P, TB, S], fp32)) for u in (0, 1)]
    ps_v = psum.enter_context(nc.psum_tensor(f"ps_vt{l}", [P, 512], fp32))
    ps_o = psum.enter_context(nc.psum_tensor(f"ps_o{l}", [P, TB, 512], fp32))
    ps_m = psum.enter_context(nc.psum_tensor(f"ps_m{l}", [P, 512], fp32))
    ps_y = ps_o[:, 0].rearrange("p (t d) -> p t d", t=TB)
    md = p.scratch(f"md{l}", [B, 2, H, S], fp32)
    X = c["x"]

    stacks_set = p.sem(f"stacks_set{l}")
    loaded = [p.sem(f"kqv_loaded{l}{u}") for u in (0, 1)]
    scored = p.sem(f"scored{l}")
    reduced = p.sem(f"max_reduced{l}")
    max_turned = p.sem(f"max_turned{l}")
    max_split = p.sem(f"max_split{l}")
    max_stored, max_loaded = p.sem(f"max_stored{l}"), p.sem(f"max_loaded{l}")
    shifted = p.sem(f"scores_shifted{l}")
    probs_done = p.sem(f"probs_done{l}")
    mixed = p.sem(f"values_mixed{l}")
    o_scaled, o_turned, ot_copied = p.sem(f"o_scaled{l}"), p.sem(f"o_turned{l}"), p.sem(f"ot_copied{l}")
    vt_copied, vt_turned = p.sem(f"vt_copied{l}"), p.sem(f"vt_turned{l}")
    y_done, x_added = p.sem(f"y_done{l}"), p.sem(f"x_added{l}")
    LOADS = 7 * 16

    def each_batch(engine, f):
        with engine.Fori(0, B // 2 - 1) as i:
            f(i, i * 2, 0, False)
            f(i, i * 2 + 1, 1, False)
        f(B // 2 - 1, B - 2, 0, False)
        f(B // 2 - 1, B - 1, 1, True)

    with nc.Block() as block:
        @block.gpsimd
        def _(pool):
            for u in (0, 1):
                for z in (KS[u], QS[u]):
                    nc.gpsimd.memset(z[32:64].bitcast(fp32), 0.0).then_inc(stacks_set, 1)
                nc.gpsimd.memset(KS[u][ROW_MAX:STACK].bitcast(fp32), 1.0).then_inc(stacks_set, 1)

        @block.sync
        def _(sp):
            def load(b, u):
                sp.wait_ge(mixed, b * H + H)
                for name, buf, parts in (("kd", KS[u], (0, 1, 0)), ("qd", QS[u], (0, 0, 1))):
                    for row, part in enumerate(parts):
                        src = c[f"{name}{l}"][part, :, bass.ds(b * S, S)].rearrange("(h e) t -> e h t", h=H)
                        sp.dma_start(buf[row * DH:(row + 1) * DH].bitcast(fp32), src).then_inc(loaded[u], 16)
                sp.dma_start(V[u][:].rearrange("p t h e -> p t (h e)"),
                             c[f"vd{l}"][bass.ds(b * S, S), :].rearrange("(t p) e -> p t e", p=P)).then_inc(loaded[u], 16)

            def maxima(b, u):
                sp.wait_ge(max_split, b * 2 + 2)
                sp.dma_start(md[bass.ds(b, 1)].rearrange("o a h t -> h (o a) t"), MT[:].bitcast(fp32)).then_inc(max_stored, 16)
                sp.wait_ge(max_stored, b * 16 + 16)
                sp.dma_start(QS[u][ROW_MAX:STACK].rearrange("a h t -> a (h t)").bitcast(fp32),
                             md[bass.ds(b, 1)].rearrange("o a h t -> (o a) (h t)")).then_inc(max_loaded, 16)

            sp.wait_ge(stacks_set, 6)
            load(0, 0)
            maxima(0, 0)

            def batch(i, b, u, last):
                if not last:
                    load(b + 1, 1 - u)
                    maxima(b + 1, 1 - u)
            each_batch(sp, batch)

        @block.tensor
        def _(pe):
            pe.sem_inc(mixed, 2 * H)
            pe.sem_inc(vt_turned, 2)

            def score(b, u, n):
                pe.wait_ge(reduced, b * H + n + 1)
                bank, qt = ps_s[n % 2], n % 2
                for j in (0, 1):
                    h = 2 * (n // 2) + j
                    last = nc.tensor.matmul(bank[:, j], QS[u][0:3 * DH, h, qt * P:(qt + 1) * P], KS[u][0:3 * DH, h],
                                            start=True, stop=not masked)
                    if masked:
                        last = nc.tensor.matmul(bank[:, j], c["identb"][:], c["mask_qk"][:, qt], start=False, stop=True)
                last.then_inc(scored, 1)

            def turn_maxima(b, u):
                pe.wait_ge(reduced, b * H + H + 2)
                for qt in range(TB):
                    last = nc.tensor.transpose(ps_m[0:H, qt * P:(qt + 1) * P], NMAX[u][:, qt], c["ident"][:])
                last.then_inc(max_turned, 1)

            def shift(b, u, h):
                pe.wait_ge(probs_done, b * H + h + 1)
                for kt in range(TB):
                    last = nc.tensor.matmul(ps_p[h % 2][:, kt], KS[u][:, h, kt * P:(kt + 1) * P], QS[u][:, h],
                                            start=True, stop=not masked)
                    if masked:
                        last = nc.tensor.matmul(ps_p[h % 2][:, kt], c["identb"][:], c["mask_kq"][:, kt],
                                                start=False, stop=True)
                last.then_inc(shifted, 1)

            def mix(b, u, h, slot):
                pe.wait_ge(probs_done, b * H + h + 3)
                if h % HQ == 0:
                    pe.wait_ge(vt_copied, b * (H // HQ) + h // HQ + 1)
                rows = ps_v[h % HQ * HV:(h % HQ + 1) * HV, 0:S]
                for kt in range(TB):
                    last = nc.tensor.matmul(rows, V[u][:, kt, h], PT[:, slot, kt], start=kt == 0, stop=kt == TB - 1)
                last.then_inc(mixed, 1)

            def turn_mixed(b, g):
                pe.wait_ge(vt_copied, b * (H // HQ) + g + 2)
                if g == 0:
                    pe.wait_ge(o_scaled, b + 1)
                    pe.wait_ge(x_added, b + 1)
                for qt in range(TB):
                    last = nc.tensor.transpose(ps_o[:, qt, g * P:(g + 1) * P], VT[:, g % 2, qt * P:(qt + 1) * P], c["ident"][:])
                last.then_inc(vt_turned, 1)

            pe.wait_ge(loaded[0], LOADS)
            for n in range(H):
                score(0, 0, n)
            turn_maxima(0, 0)

            def batch(i, b, u, last):
                pe.wait_ge(max_loaded, b * 16 + 16)
                if not last:
                    pe.wait_ge(loaded[1 - u], (i + 1 + u) * LOADS)
                for h in range(H):
                    shift(b, u, h)
                    if not last:
                        score(b + 1, 1 - u, h)
                    if h >= 1:
                        mix(b, u, h - 1, (h - 1) % NP)
                    if h % HQ == 2 and h > HQ:
                        turn_mixed(b, h // HQ - 1)
                mix(b, u, H - 1, (H - 1) % NP)
                if not last:
                    turn_maxima(b + 1, 1 - u)
                    pe.wait_ge(max_split, b * 2 + 4)
                turn_mixed(b, H // HQ - 1)
                pe.wait_ge(o_scaled, b + 2)
                for k in range(KT):
                    for t in range(TB):
                        ins = nc.tensor.transpose(ps_m[:, k * S + t * P:k * S + (t + 1) * P], O[:, t, k * P:(k + 1) * P],
                                                  c["ident"][:])
                ins.then_inc(o_turned, 1)
                pe.wait_ge(ot_copied, b + 1)
                for t in range(TB):
                    for k in range(KT):
                        ins = nc.tensor.matmul(ps_y[:, t], OT[:, k, t * P:(t + 1) * P], c[f"wo{l}"][:, k],
                                               start=k == 0, stop=k == KT - 1)
                ins.then_inc(y_done, 1)
            each_batch(pe, batch)

        @block.vector
        def _(dve):
            dve.sem_inc(reduced, 2)
            dve.sem_inc(o_scaled, 1)
            dve.sem_inc(x_added, 1)

            def reduce(b, u, n):
                dve.wait_ge(scored, b * H + n + 1)
                hp = 2 * (n // 2)
                nc.vector.tensor_reduce(NMAX[u][:, n % 2, hp:hp + 2], ps_s[n % 2][:], AX.X, ALU.max,
                                        negate=True).then_inc(reduced, 1)

            def split_maxima(b):
                dve.wait_ge(max_turned, b + 1)
                if not isinstance(b, int) or b > 0:
                    dve.wait_ge(max_stored, b * 16)
                rows = ps_m[0:H, 0:S]
                nc.vector.tensor_copy(MT[:, 0], rows).then_inc(max_split, 1)
                dve.wait_ge(max_split, b * 2 + 1)
                nc.vector.tensor_tensor(MT[:, 1], rows, MT[:, 0].bitcast(fp32), ALU.subtract).then_inc(max_split, 1)

            for n in range(H):
                reduce(0, 0, n)
            split_maxima(0)

            def batch(i, b, u, last):
                if not last:
                    for n in range(H):
                        reduce(b + 1, 1 - u, n)
                    split_maxima(b + 1)
                dve.wait_ge(vt_turned, (b + 1) * (H // HQ) + 2)
                sums = ps_o[:].rearrange("p t (h e) -> p t h e", h=H)
                nc.vector.reciprocal(RINV[:], sums[:, :, :, DH]).then_inc(rinv_done, 1)
                dve.wait_ge(rinv_done, b + 1)
                for t in range(TB):
                    ins = nc.vector.tensor_tensor(O[:, t].rearrange("p (h e) -> p h e", h=H), sums[:, t, :, 0:DH],
                                                  RINV[:, t].unsqueeze(2).broadcast_to([P, H, DH]), ALU.mult)
                ins.then_inc(o_scaled, 1)
                dve.wait_ge(y_done, b + 1)
                at = X[:, bass.ds(b * TB, TB), :]
                nc.vector.tensor_tensor(at, ps_y[:], at, ALU.add).then_inc(x_added, 1)
            rinv_done = p.sem(f"rinv_done{l}")
            each_batch(dve, batch)
            dve.wait_ge(x_added, B + 1)

        @block.scalar
        def _(act):
            act.sem_inc(probs_done, 2)
            act.sem_inc(vt_copied, 1)

            def copy_mixed(b, g):
                act.wait_ge(mixed, b * H + (g + 1) * HQ + 2 * H)
                act.wait_ge(vt_turned, b * (H // HQ) + g + 1)
                nc.scalar.activation(VT[:, g % 2], ps_v[:, 0:S], ACT.Copy).then_inc(vt_copied, 1)

            def batch(i, b, u, last):
                for h in range(H):
                    act.wait_ge(shifted, b * H + h + 1)
                    act.wait_ge(mixed, b * H + h + 1 + 2 * H - NP)
                    nc.scalar.activation(PT[:, h % NP], ps_p[h % 2][:], ACT.Exp).then_inc(probs_done, 1)
                    if h % HQ == 1 and h > HQ:
                        copy_mixed(b, h // HQ - 1)
                copy_mixed(b, H // HQ - 1)
                act.wait_ge(o_turned, b + 1)
                nc.scalar.activation(OT[:].rearrange("p k t -> p (k t)"), ps_m[:], ACT.Copy).then_inc(ot_copied, 1)
            each_batch(act, batch)
    psum.close()


def in_steps(engine, n, stages):
    most = max(lag for lag, _ in stages)
    first = (most + 1) // 2
    last = n // 2

    def step(s, parity):
        for lag, f in stages:
            if not isinstance(s, int) or 0 <= s - lag < n:
                f(s - lag, (parity - lag) % 2)

    for s in range(2 * first):
        step(s, s % 2)
    with engine.Fori(0, last - first) as i:
        step(i * 2 + 2 * first, 0)
        step(i * 2 + 2 * first + 1, 1)
    for s in range(2 * last, n + most):
        step(s, s % 2)


def routing_constants(p, c):
    nc = p.nc
    c["count_i"] = p.sb("count_i", [P, TILES0], int32)
    c["count"] = p.sb("count", [P, TILES0], fp32)
    c["before"] = p.sb("before", [P, P], bf16)
    c["ones"] = p.sb("ones", [P, P], bf16)
    made = p.sem("routing_constants")
    with nc.Block() as block:
        @block.gpsimd
        def _(pool):
            nc.gpsimd.iota(c["count_i"][:], pattern=[[1, TILES0]], base=0, channel_multiplier=0).then_inc(made, 1)
            nc.gpsimd.memset(c["ones"][:], 1.0).then_inc(made, 1)
            nc.gpsimd.memset(c["before"][:], 1.0).then_inc(made, 1)
            pool.wait_ge(made, 3)
            nc.gpsimd.affine_select(out=c["before"][:], in_=c["before"][:], compare_op=ALU.is_gt, fill=0.0, base=0,
                                    pattern=[[1, P]], channel_multiplier=-1).then_inc(made, 1)

        @block.vector
        def _(dve):
            dve.wait_ge(made, 4)
            nc.vector.tensor_copy(c["count"][:], c["count_i"][:]).then_inc(made, 1)
            dve.wait_ge(made, 5)


def route(p, c, l, E, K):
    nc = p.nc
    XN = c["xn"] = p.sb(f"xn_all{l}", [P, NT, D], fp32)
    SLOT = p.sb(f"slot{l}", [P, K, NT], int32)
    W = p.sb(f"choice_weight{l}", [P, NT, 8], fp32)
    gate = p.sb(f"gate{l}", [P, KT, E], fp32)
    TE = p.sb(f"tile_expert{l}", [P, TILES0], int32)
    c["slot"], c["weight"], c["tile_expert"] = SLOT, W, TE
    if l == 1:
        c["slot_read"] = p.sb("slot_read", [P, K, NT], int32)
        XNT = c["xnt"] = p.sb("xn_turned", [P, KT, N], fp32)
    start = p.top
    stats = p.sb(f"m_stats{l}", [P, NT, 6], fp32)
    mv = p.sb(f"m_mean_var{l}", [P, NT, 2], fp32)
    var = p.sb(f"m_var{l}", [P, NT], fp32)
    rstd = p.sb(f"m_rstd{l}", [P, NT], fp32)
    xn = [p.sb(f"m_xn{l}{u}", [P, TB, D], fp32) for u in (0, 1)]
    xnt = [p.sb(f"m_xnt{l}{u}", [P, KT, S], fp32) for u in (0, 1)]
    top = p.sb(f"top{l}", [P, NT], fp32)
    ex = p.sb(f"gate_exp{l}", [P, NT, E], fp32)
    total = p.sb(f"gate_sum{l}", [P, NT], fp32)
    prob = p.sb(f"gate_prob{l}", [P, NT, E], fp32)
    idx = p.sb(f"choice{l}", [P, NT, 8], mybir.dt.uint32)
    idxf = p.sb(f"choice_f{l}", [P, NT, 8], fp32)
    hot = [p.sb(f"chosen{l}{k}", [P, NT, E], fp32) for k in range(K)]
    M = p.sb(f"chosen{l}", [P, NT, E], bf16)
    where = p.sb(f"where{l}", [P, NT, E], fp32)
    picked = p.sb(f"picked{l}", [P, NT, E], fp32)
    slotf = p.sb(f"slot_f{l}", [P, K, NT], fp32)
    if l == 0:
        cnt_i = p.sb("tiles_i", [P, E], int32)
        tiles = p.sb("tiles_f", [P, E], fp32)
        ends = p.sb("tile_ends", [P, E], fp32)
        base = p.sb("slot_base", [P, E], fp32)
        past = p.sb("tiles_past", [P, TILES0, E], fp32)
        te = p.sb("tile_expert_f", [P, TILES0], fp32)
    else:
        gmax = p.sb("group_max", [P, NT, G1], fp32)
        g8 = p.sb("group_top", [P, NT, 8], fp32)
        gidx = p.sb("group_choice", [P, NT, 8], mybir.dt.uint32)
        gidxf = p.sb("group_choice_f", [P, NT, 8], fp32)
        same = p.sb("group_same", [P, NT, G1, LG1], fp32)
        keep = p.sb("group_kept", [P, NT, G1], fp32)
        drop = p.sb("group_dropped", [P, NT, G1], fp32)
        kept = p.sb("prob_kept", [P, NT, E], fp32)
        pos = p.sb("choice_position", [P, NT], fp32)
        fits = p.sb("choice_fits", [P, NT], fp32)
        over_cap = p.sb("choice_over", [P, NT], fp32)
    p.top = start
    psum = ExitStack()
    ps_t = [psum.enter_context(nc.psum_tensor(f"ps_mt{l}{u}", [P, KT, S], fp32)) for u in (0, 1)]
    ps_l = psum.enter_context(nc.psum_tensor(f"ps_l{l}", [P, NT, E], fp32))
    ps_w = psum.enter_context(nc.psum_tensor(f"ps_w{l}", [P, NT, E], fp32))
    ps_c = psum.enter_context(nc.psum_tensor(f"ps_c{l}", [P, E], fp32))
    X = c["x"]
    gate_loaded = p.sem(f"gate_loaded{l}")
    stats_done, var_done, rstd_done = p.sem(f"m_stats_done{l}"), p.sem(f"m_var_done{l}"), p.sem(f"m_rstd_done{l}")
    xn_done, xt_done, xt_copied = p.sem(f"m_xn_done{l}"), p.sem(f"m_xt_done{l}"), p.sem(f"m_xt_copied{l}")
    xn_kept, xt_kept, logits_done = p.sem(f"m_xn_kept{l}"), p.sem(f"m_xt_kept{l}"), p.sem(f"logits_done{l}")
    shifted, exp_done = p.sem(f"gate_shifted{l}"), p.sem(f"gate_exp_done{l}")
    step, chosen, counted = p.sem(f"route_step{l}"), p.sem(f"chosen_done{l}"), p.sem(f"counted{l}")
    slots_done = p.sem(f"slots_done{l}")
    c["slots_done"] = slots_done

    with nc.Block() as block:
        @block.sync
        def _(sp):
            sp.dma_start(gate[:], p.dram[f"m{l}_gate_w"]).then_inc(gate_loaded, 16)

        @block.gpsimd
        def _(pool):
            pool.wait_ge(var_done, 1)
            nc.gpsimd.tensor_tensor(rstd[:], var[:], c["minus_half"][:], ALU.pow).then_inc(rstd_done, 1)
            pool.sem_inc(xn_kept, 2)
            pool.sem_inc(xt_kept, 2)
            with pool.Fori(0, B // 2) as i:
                for u in (0, 1):
                    pool.wait_ge(xn_done, i * 2 + u + 1)
                    nc.gpsimd.tensor_copy(XN[:, bass.ds((i * 2 + u) * TB, TB), :], xn[u][:]).then_inc(xn_kept, 1)
                    if l == 1:
                        pool.wait_ge(xt_copied, i * 2 + u + 3)
                        nc.gpsimd.tensor_copy(XNT[:, :, bass.ds((i * 2 + u) * S, S)], xnt[u][:]).then_inc(xt_kept, 1)
            pool.wait_ge(xn_kept, B + 2)

        @block.tensor
        def _(pe):
            pe.sem_inc(xt_done, 2)
            pe.wait_ge(gate_loaded, 16)

            def transposes(b, u):
                pe.wait_ge(xn_done, b + 1)
                pe.wait_ge(xt_copied, b + 1)
                for t in range(TB):
                    for k in range(KT):
                        last = nc.tensor.transpose(ps_t[u][:, k, t * P:(t + 1) * P], xn[u][:, t, k * P:(k + 1) * P],
                                                   c["ident"][:])
                last.then_inc(xt_done, 1)

            def logits(b, u):
                pe.wait_ge(xt_copied, b + 3)
                for t in range(TB):
                    at = ps_l[:, bass.ds(b * TB + t, 1), :].rearrange("p o e -> p (o e)")
                    for k in range(KT):
                        last = nc.tensor.matmul(at, xnt[u][:, k, t * P:(t + 1) * P], gate[:, k],
                                                start=k == 0, stop=k == KT - 1)
                last.then_inc(logits_done, 1)

            with pe.Fori(0, B // 2) as i:
                transposes(i * 2, 0)
                transposes(i * 2 + 1, 1)
                logits(i * 2, 0)
                logits(i * 2 + 1, 1)
            pe.wait_ge(chosen, 1)
            nc.tensor.matmul(ps_w[:], c["before"][:], M[:], start=True, stop=False)
            for t in range(NT - 1):
                last = nc.tensor.matmul(ps_w[:, t + 1:], c["ones"][:], M[:, t:t + 1].broadcast_to([P, NT - 1 - t, E]),
                                        start=False, stop=t == NT - 2)
            last.then_inc(counted, 1)
            if l == 0:
                for t in range(NT):
                    last = nc.tensor.matmul(ps_c[:], c["ones"][:], M[:, t], start=t == 0, stop=t == NT - 1)
                last.then_inc(counted, 1)

        @block.scalar
        def _(act):
            act.sem_inc(xt_copied, 2)
            act.sem_inc(logits_done, 2)

            def copy(b, u):
                act.wait_ge(xt_done, b + 3)
                act.wait_ge(logits_done, b + 1)
                if l == 1:
                    act.wait_ge(xt_kept, b + 1)
                nc.scalar.activation(xnt[u][:], ps_t[u][:], ACT.Copy).then_inc(xt_copied, 1)

            with act.Fori(0, B // 2) as i:
                copy(i * 2, 0)
                copy(i * 2 + 1, 1)
            act.wait_ge(shifted, 1)
            nc.scalar.activation(ex[:], ex[:], ACT.Exp).then_inc(exp_done, 1)

        @block.vector
        def _(dve):
            with dve.Fori(0, NT) as t:
                nc.vector.bn_stats(stats[:, bass.ds(t, 1), :], X[:, bass.ds(t, 1), :]).then_inc(stats_done, 1)
            dve.wait_ge(stats_done, NT)
            for t in range(NT):
                nc.vector.bn_aggr(mv[:, t], stats[:, t]).then_inc(stats_done, 1)
            dve.wait_ge(stats_done, 2 * NT)
            nc.vector.tensor_scalar(var[:], mv[:, :, 1], EPS, None, ALU.add).then_inc(var_done, 1)
            dve.wait_ge(rstd_done, 1)
            with dve.Fori(0, B // 2) as i:
                for u in (0, 1):
                    b = i * 2 + u
                    dve.wait_ge(xt_done, b + 1)
                    dve.wait_ge(xn_kept, b + 1)
                    for t in range(TB):
                        tile = b * TB + t
                        ins = nc.vector.tensor_scalar(xn[u][:, t], X[:, bass.ds(tile, 1), :].rearrange("p o d -> p (o d)"),
                                                      mv[:, bass.ds(tile, 1), 0], rstd[:, bass.ds(tile, 1)],
                                                      ALU.subtract, ALU.mult)
                    ins.then_inc(xn_done, 1)

            done = [0]

            def then(ins):
                ins.then_inc(step, 1)
                done[0] += 1
                dve.wait_ge(step, done[0])

            def over(v, n):
                return v.unsqueeze(2).broadcast_to([P, NT, n])

            dve.wait_ge(logits_done, B + 2)
            then(nc.vector.tensor_reduce(top[:], ps_l[:], AX.X, ALU.max))
            nc.vector.tensor_tensor(ex[:], ps_l[:], over(top[:], E), ALU.subtract).then_inc(shifted, 1)
            dve.wait_ge(exp_done, 1)
            then(nc.vector.tensor_reduce(total[:], ex[:], AX.X, ALU.add))
            then(nc.vector.reciprocal(total[:], total[:]))
            then(nc.vector.tensor_tensor(prob[:], ex[:], over(total[:], E), ALU.mult))
            source = prob
            if l == 1:
                then(nc.vector.tensor_reduce(gmax[:], prob[:].rearrange("p t (g e) -> p t g e", g=G1), AX.X, ALU.max))
                for t in range(NT):
                    ins = nc.vector.max(g8[:, t], gmax[:, t])
                then(ins)
                for t in range(NT):
                    ins = nc.vector.max_index(gidx[:, t], g8[:, t], gmax[:, t])
                then(ins)
                then(nc.vector.tensor_copy(gidxf[:], gidx[:]))
                for t in range(NT):
                    ins = nc.vector.tensor_tensor(same[:, t], gidxf[:, t, 0:LG1].unsqueeze(1).broadcast_to([P, G1, LG1]),
                                                  c["count"][:, 0:G1].unsqueeze(2).broadcast_to([P, G1, LG1]), ALU.is_equal)
                then(ins)
                then(nc.vector.tensor_reduce(keep[:], same[:], AX.X, ALU.add))
                then(nc.vector.tensor_scalar(drop[:], keep[:], -1.0, None, ALU.add))
                for t in range(NT):
                    ins = nc.vector.tensor_tensor(kept[:, t].rearrange("p (g e) -> p g e", g=G1),
                                                  prob[:, t].rearrange("p (g e) -> p g e", g=G1),
                                                  keep[:, t].unsqueeze(2).broadcast_to([P, G1, GE1]), ALU.mult)
                then(ins)
                for t in range(NT):
                    ins = nc.vector.tensor_tensor(kept[:, t].rearrange("p (g e) -> p g e", g=G1),
                                                  kept[:, t].rearrange("p (g e) -> p g e", g=G1),
                                                  drop[:, t].unsqueeze(2).broadcast_to([P, G1, GE1]), ALU.add)
                then(ins)
                source = kept
            for t in range(NT):
                ins = nc.vector.max(W[:, t], source[:, t])
            then(ins)
            for t in range(NT):
                ins = nc.vector.max_index(idx[:, t], W[:, t], source[:, t])
            then(ins)
            then(nc.vector.tensor_copy(idxf[:], idx[:]))
            for k in range(K):
                ins = nc.vector.tensor_tensor(hot[k][:], over(idxf[:, :, k], E),
                                              c["count"][:, 0:E].unsqueeze(1).broadcast_to([P, NT, E]), ALU.is_equal)
            then(ins)
            then(nc.vector.tensor_tensor(picked[:], hot[0][:], hot[1][:], ALU.add))
            for k in range(2, K - 1):
                then(nc.vector.tensor_tensor(picked[:], picked[:], hot[k][:], ALU.add))
            if K == 2:
                nc.vector.tensor_copy(M[:], picked[:]).then_inc(chosen, 1)
            else:
                nc.vector.tensor_tensor(M[:], picked[:], hot[K - 1][:], ALU.add).then_inc(chosen, 1)
            then(nc.vector.tensor_reduce(total[:], W[:, :, 0:K], AX.X, ALU.add))
            if l == 1:
                then(nc.vector.tensor_scalar(total[:], total[:], 1e-9, None, ALU.add))
            then(nc.vector.reciprocal(total[:], total[:]))
            then(nc.vector.tensor_tensor(W[:, :, 0:K], W[:, :, 0:K], over(total[:], K), ALU.mult))
            dve.wait_ge(counted, 2 if l == 0 else 1)
            if l == 0:
                then(nc.vector.tensor_scalar(cnt_i[:], ps_c[:], float(P - 1), None, ALU.add))
                then(nc.vector.tensor_scalar(cnt_i[:], cnt_i[:], 7, None, ALU.arith_shift_right))
                then(nc.vector.tensor_copy(tiles[:], cnt_i[:]))
                then(nc.vector.tensor_copy(ends[:, 0:1], tiles[:, 0:1]))
                for e in range(1, E):
                    then(nc.vector.tensor_tensor(ends[:, e:e + 1], ends[:, e - 1:e], tiles[:, e:e + 1], ALU.add))
                then(nc.vector.tensor_tensor(base[:], ends[:], tiles[:], ALU.subtract))
                then(nc.vector.tensor_scalar(base[:], base[:], float(P), None, ALU.mult))
                then(nc.vector.tensor_tensor(where[:], ps_w[:], base[:].unsqueeze(1).broadcast_to([P, NT, E]), ALU.add))
                then(nc.vector.tensor_tensor(past[:], c["count"][:].unsqueeze(2).broadcast_to([P, TILES0, E]),
                                             ends[:].unsqueeze(1).broadcast_to([P, TILES0, E]), ALU.is_ge))
                then(nc.vector.tensor_reduce(te[:], past[:], AX.X, ALU.add))
                then(nc.vector.tensor_scalar(TE[:], te[:], float(E - 1), None, ALU.min))
            else:
                then(nc.vector.tensor_copy(where[:], ps_w[:]))
            for k in range(K):
                then(nc.vector.tensor_tensor(picked[:], where[:], hot[k][:], ALU.mult))
                if l == 0:
                    then(nc.vector.tensor_reduce(slotf[:, k], picked[:], AX.X, ALU.add))
                    nc.vector.tensor_copy(SLOT[:, k], slotf[:, k]).then_inc(slots_done, 1)
                else:
                    then(nc.vector.tensor_reduce(pos[:], picked[:], AX.X, ALU.add))
                    then(nc.vector.tensor_scalar(fits[:], pos[:], float(CAP), None, ALU.is_lt))
                    then(nc.vector.tensor_scalar(over_cap[:], pos[:], float(CAP), float(SLOTS1), ALU.is_ge, ALU.mult))
                    then(nc.vector.scalar_tensor_tensor(slotf[:, k], idxf[:, :, k], float(CAP), pos[:], ALU.mult, ALU.add))
                    then(nc.vector.tensor_tensor(slotf[:, k], slotf[:, k], over_cap[:], ALU.add))
                    then(nc.vector.tensor_tensor(W[:, :, k], W[:, :, k], fits[:], ALU.mult))
                    then(nc.vector.tensor_scalar(c["slot_read"][:, k], slotf[:, k], float(SLOTS1 - 1), None, ALU.min))
                    nc.vector.tensor_copy(SLOT[:, k], slotf[:, k]).then_inc(slots_done, 1)
            dve.wait_ge(slots_done, K)
    psum.close()


def scatter_rows(p, c, l, K, pool, scattered):
    table = c[f"slots_in{l}"]
    for k in range(K):
        for t in range(NT):
            p.nc.gpsimd.indirect_dma_start(table, bass.IndirectOffsetOnAxis(ap=c["slot"][:, k, t:t + 1], axis=0),
                                           c["xn"][:, t, :], None, bounds_check=table.shape[0] - 1,
                                           oob_is_err=False).then_inc(scattered, 16)


def experts_first(p, c):
    nc = p.nc
    W1, W2, TE = c["w1"], c["w2"], c["tile_expert"]
    start = p.top
    B1, G, BB = (p.sb(f"m0_{n}", [P, E0, H0], fp32) for n in ("b1b", "ln1_gb", "ln1_bb"))
    B2 = p.sb("m0_b2b", [P, E0, D], fp32)
    xg = [p.sb(f"xg{u}", [P, D], fp32) for u in (0, 1)]
    xt = [p.sb(f"xgt{u}", [P, KT, P], fp32) for u in (0, 1)]
    hs = [p.sb(f"hs{u}", [P, H0], fp32) for u in (0, 1)]
    gs = [p.sb(f"gs{u}", [P, H0], fp32) for u in (0, 1)]
    ht = [p.sb(f"ht{u}", [P, HT0, P], fp32) for u in (0, 1)]
    ys = [p.sb(f"ys{u}", [P, D], fp32) for u in (0, 1)]
    st = p.sb("h_stats", [P, 2, 6], fp32)
    mv = p.sb("h_mean_var", [P, 2, 2], fp32)
    ve = p.sb("h_var", [P, 2], fp32)
    hold = p.sb("hold", [1, 1], fp32)
    rs = p.sb("h_rstd", [P, 2], fp32)
    p.top = start
    psum = ExitStack()
    ps_x, ps_h, ps_t, ps_y = ([psum.enter_context(nc.psum_tensor(f"ps_m0{n}{u}", [P, 512], fp32)) for u in (0, 1)]
                              for n in ("xg", "h", "ht", "y"))
    table_loaded, scattered = p.sem("tables_loaded"), p.pool_dma_sem("scattered0")
    x_loaded = [p.sem(f"xg_loaded{u}") for u in (0, 1)]
    y_stored = [p.sem(f"yg_stored{u}") for u in (0, 1)]
    x_turned, x_copied = p.sem("xg_turned"), p.sem("xg_copied")
    h_made, h_biased, h_stats = p.sem("h_made"), p.sem("h_biased"), p.sem("h_stats_done")
    h_var, h_rstd, h_normed = p.sem("h_var_done"), p.sem("h_rstd_done"), p.sem("h_normed")
    h_scaled, h_gelu = p.sem("h_scaled"), p.sem("h_gelu")
    h_turned, h_copied = p.sem("h_turned"), p.sem("h_copied")
    y_made, y_biased = p.sem("yg_made"), p.sem("yg_biased")
    LAG_H, LAG_Y = 1, 3

    with nc.Block() as block:
        @block.sync
        def _(sp):
            d = p.dram
            for buf, n, w in ((B1, "b1", H0), (G, "ln1_g", H0), (BB, "ln1_b", H0), (B2, "b2", D)):
                sp.dma_start(buf[:].rearrange("p e h -> p (e h)"), across_partitions(d["m0_" + n], E0 * w))\
                    .then_inc(table_loaded, 16)
            for u in (0, 1):
                sp.sem_inc(y_stored[u], 16)

            sp.wait_ge(scattered, 16 * K0 * NT)

            def load(j, u):
                sp.wait_ge(x_turned, j + 1)
                sp.dma_start(xg[u][:], c["slots_in0"][bass.ds(j * P, P), :]).then_inc(x_loaded[u], 16)

            def store(j, u):
                sp.wait_ge(y_biased, j + 3)
                sp.dma_start(c["slots_out0"][bass.ds(j * P, P), :], ys[u][:]).then_inc(y_stored[u], 16)

            in_steps(sp, TILES0, [(0, load), (LAG_Y + 1, store)])
            for u in (0, 1):
                sp.wait_ge(y_stored[u], 16 * (TILES0 // 2 + 1))

        @block.tensor
        def _(pe):
            pe.sem_inc(x_turned, 2)
            pe.sem_inc(h_turned, 2)
            pe.sem_inc(h_made, 2)
            pe.sem_inc(y_made, 2)
            pe.wait_ge(c["w_loaded"], 32)

            def turn_x(j, u):
                pe.wait_ge(x_loaded[u], half(j, u) * 16 + 16)
                pe.wait_ge(x_copied, j + 1)
                for k in range(KT):
                    last = nc.tensor.transpose(ps_x[u][:, k * P:(k + 1) * P], xg[u][:, k * P:(k + 1) * P], c["ident"][:])
                last.then_inc(x_turned, 1)

            def up(j, u):
                pe.wait_ge(x_copied, j + 3)
                pe.wait_ge(h_biased, j + 1)
                e = pe.value_load(TE[0:1, bass.ds(j, 1)], min_val=0, max_val=E0 - 1)
                for k in range(KT):
                    last = nc.tensor.matmul(ps_h[u][:], xt[u][:, k], W1[:, bass.ds(e, 1), k].rearrange("p o h -> p (o h)"),
                                            start=k == 0, stop=k == KT - 1)
                last.then_inc(h_made, 1)

            def turn_h(j, u):
                pe.wait_ge(h_gelu, j + 3)
                pe.wait_ge(h_copied, j + 1)
                for k in range(HT0):
                    last = nc.tensor.transpose(ps_t[u][:, k * P:(k + 1) * P], gs[u][:, k * P:(k + 1) * P], c["ident"][:])
                last.then_inc(h_turned, 1)

            def down(j, u):
                pe.wait_ge(h_copied, j + 3)
                pe.wait_ge(y_biased, j + 1)
                e = pe.value_load(TE[0:1, bass.ds(j, 1)], min_val=0, max_val=E0 - 1)
                for k in range(HT0):
                    last = nc.tensor.matmul(ps_y[u][:, 0:D], ht[u][:, k], W2[:, bass.ds(e, 1), k].rearrange("p o h -> p (o h)"),
                                            start=k == 0, stop=k == HT0 - 1)
                last.then_inc(y_made, 1)

            in_steps(pe, TILES0, [(0, turn_x), (LAG_Y, turn_h), (LAG_H, up), (LAG_Y, down)])

        @block.scalar
        def _(act):
            act.sem_inc(x_copied, 2)
            act.sem_inc(h_gelu, 2)
            act.sem_inc(h_copied, 2)

            def copy_x(j, u):
                act.wait_ge(x_turned, j + 3)
                act.wait_ge(h_made, j + 1)
                nc.scalar.activation(xt[u][:].rearrange("p k t -> p (k t)"), ps_x[u][:, 0:D], ACT.Copy).then_inc(x_copied, 1)

            def gelu(j, u):
                act.wait_ge(h_scaled, j * 2 + 2)
                act.wait_ge(h_turned, j + 1)
                nc.scalar.activation(gs[u][:], hs[u][:], ACT.Gelu).then_inc(h_gelu, 1)

            def copy_h(j, u):
                act.wait_ge(h_turned, j + 3)
                act.wait_ge(y_made, j + 1)
                nc.scalar.activation(ht[u][:].rearrange("p k t -> p (k t)"), ps_t[u][:], ACT.Copy).then_inc(h_copied, 1)

            in_steps(act, TILES0, [(0, copy_x), (LAG_Y, copy_h), (LAG_H, gelu)])

        @block.vector
        def _(dve):
            dve.wait_ge(table_loaded, 64)
            dve.sem_inc(h_biased, 2)
            dve.sem_inc(y_biased, 2)

            def norm(j, u):
                dve.wait_ge(h_made, j + 3)
                dve.wait_ge(h_gelu, j + 1)
                e = dve.value_load(TE[0:1, bass.ds(j, 1)], min_val=0, max_val=E0 - 1)
                nc.vector.tensor_tensor(hs[u][:], ps_h[u][:], B1[:, bass.ds(e, 1), :].rearrange("p o h -> p (o h)"),
                                        ALU.add).then_inc(h_biased, 1)
                dve.wait_ge(h_biased, j + 3)
                nc.vector.bn_stats(st[:, u], hs[u][:]).then_inc(h_stats, 1)
                dve.wait_ge(h_stats, j * 2 + 1)
                nc.vector.memset(hold[:], 0.0)
                nc.vector.bn_aggr(mv[:, u], st[:, u]).then_inc(h_stats, 1)
                dve.wait_ge(h_stats, j * 2 + 2)
                nc.vector.tensor_scalar(ve[:, u:u + 1], mv[:, u, 1:2], EPS, None, ALU.add).then_inc(h_var, 1)
                dve.wait_ge(h_rstd, j + 1)
                nc.vector.tensor_scalar(hs[u][:], hs[u][:], mv[:, u, 0:1], rs[:, u:u + 1], ALU.subtract, ALU.mult)\
                    .then_inc(h_normed, 1)

            def bias_y(j, u):
                dve.wait_ge(y_made, j + 3)
                dve.wait_ge(y_stored[u], half(j, u) * 16 + 16)
                e = dve.value_load(TE[0:1, bass.ds(j, 1)], min_val=0, max_val=E0 - 1)
                nc.vector.tensor_tensor(ys[u][:], ps_y[u][:, 0:D], B2[:, bass.ds(e, 1), :].rearrange("p o h -> p (o h)"),
                                        ALU.add).then_inc(y_biased, 1)

            in_steps(dve, TILES0, [(LAG_H, norm), (LAG_Y, bias_y)])

        @block.gpsimd
        def _(pool):
            pool.wait_ge(c["zeroed"], 32)
            scatter_rows(p, c, 0, K0, pool, scattered)
            pool.wait_ge(table_loaded, 64)

            def scale(j, u):
                pool.wait_ge(h_var, j + 1)
                nc.gpsimd.tensor_tensor(rs[:, u:u + 1], ve[:, u:u + 1], c["minus_half"][:, 0:1], ALU.pow).then_inc(h_rstd, 1)
                e = pool.value_load(TE[0:1, bass.ds(j, 1)], min_val=0, max_val=E0 - 1)
                pool.wait_ge(h_normed, j + 1)
                nc.gpsimd.tensor_tensor(hs[u][:], hs[u][:], G[:, bass.ds(e, 1), :].rearrange("p o h -> p (o h)"), ALU.mult)\
                    .then_inc(h_scaled, 1)
                pool.wait_ge(h_scaled, j * 2 + 1)
                nc.gpsimd.tensor_tensor(hs[u][:], hs[u][:], BB[:, bass.ds(e, 1), :].rearrange("p o h -> p (o h)"), ALU.add)\
                    .then_inc(h_scaled, 1)

            in_steps(pool, TILES0, [(LAG_H, scale)])
    psum.close()


def half(j, u):
    return (j - u) // 2


def combine_first(p, c):
    nc = p.nc
    X, XN, W, SLOT = c["x"], c["xn"], c["weight"], c["slot"]
    start = p.top
    NB = 4
    yk = [p.sb(f"y_rows{n}", [P, K0, D], fp32) for n in range(NB)]
    f = [p.sb(f"ffn{u}", [P, D], fp32) for u in (0, 1)]
    gb = [p.sb(f"m0_{n}", [P, D], fp32) for n in ("ln_gb", "ln_bb")]
    st = p.sb("f_stats", [P, 2, 6], fp32)
    mv = p.sb("f_mean_var", [P, 2, 2], fp32)
    ve = p.sb("f_var", [P, 2], fp32)
    rs = p.sb("f_rstd", [P, 2], fp32)
    p.top = start
    loaded = p.sem("ln_loaded")
    gathered = [p.pool_dma_sem(f"y_gathered{n}") for n in range(NB)]
    used, step, var_done, rstd_done = p.sem("y_rows_used"), p.sem("combine_step"), p.sem("f_var_done"), p.sem("f_rstd_done")
    with nc.Block() as block:
        @block.sync
        def _(sp):
            for buf, n in zip(gb, ("ln_g", "ln_b")):
                sp.dma_start(buf[:], across_partitions(p.dram["m0_" + n], D)).then_inc(loaded, 16)

        @block.gpsimd
        def _(pool):
            table = c["slots_out0"]
            for t in range(NT + 1):
                if t < NT:
                    if t >= NB:
                        pool.wait_ge(used, t - NB + 1)
                    for k in range(K0):
                        nc.gpsimd.indirect_dma_start(yk[t % NB][:, k], None, table,
                                                     bass.IndirectOffsetOnAxis(ap=SLOT[:, k, t:t + 1], axis=0))\
                            .then_inc(gathered[t % NB], 16)
                if t >= 1:
                    u = (t - 1) % 2
                    pool.wait_ge(var_done, t)
                    nc.gpsimd.tensor_tensor(rs[:, u:u + 1], ve[:, u:u + 1], c["minus_half"][:, 0:1], ALU.pow)\
                        .then_inc(rstd_done, 1)

        @block.vector
        def _(dve):
            dve.wait_ge(loaded, 32)
            done = [0]

            def then(ins):
                ins.then_inc(step, 1)
                done[0] += 1
                dve.wait_ge(step, done[0])

            for t in range(NT):
                u, n = t % 2, t % NB
                dve.wait_ge(gathered[n], 16 * K0 * (t // NB + 1))
                then(nc.vector.scalar_tensor_tensor(f[u][:], yk[n][:, 0], W[:, t, 0:1], XN[:, t], ALU.mult, ALU.add))
                nc.vector.scalar_tensor_tensor(f[u][:], yk[n][:, 1], W[:, t, 1:2], f[u][:], ALU.mult, ALU.add)\
                    .then_inc(used, 1)
                dve.wait_ge(used, t + 1)
                then(nc.vector.bn_stats(st[:, u], f[u][:]))
                then(nc.vector.bn_aggr(mv[:, u], st[:, u]))
                nc.vector.tensor_scalar(ve[:, u:u + 1], mv[:, u, 1:2], EPS, None, ALU.add).then_inc(var_done, 1)
                dve.wait_ge(rstd_done, t + 1)
                then(nc.vector.tensor_scalar(f[u][:], f[u][:], mv[:, u, 0:1], rs[:, u:u + 1], ALU.subtract, ALU.mult))
                then(nc.vector.tensor_tensor(f[u][:], f[u][:], gb[0][:], ALU.mult))
                then(nc.vector.tensor_tensor(f[u][:], f[u][:], gb[1][:], ALU.add))
                then(nc.vector.tensor_tensor(X[:, t], X[:, t], f[u][:], ALU.add))


def experts_second(p, c):
    nc, d = p.nc, p.dram
    X, XNT = c["x"], c["xnt"]
    NS = len(SLOT_TILES)
    FULL = sum(n == P for _, n in SLOT_TILES)
    LAST = SLOT_TILES[-1][1] % P
    start = p.top
    sw = {n: p.sb("m1_" + n, [P, KT, D], fp32) for n in ("sw1", "sw3", "sw2")}
    w1, w3, w2 = ([p.sb(f"m1_{n}{u}", [P, KT, D], fp32) for u in (0, 1)] for n in ("w1", "w3", "w2"))
    xe = [p.sb(f"xe{u}", [P, NS, D], fp32) for u in (0, 1)]
    xt = [p.sb(f"xet{u}", [P, KT, CAP], fp32) for u in (0, 1)]
    sl = [p.sb(f"silu{u}", [P, HT1, CAP], fp32) for u in (0, 1)]
    gt = [p.sb(f"gated{u}", [P, HT1, CAP], fp32) for u in (0, 1)]
    ys = [p.sb(f"ye{u}", [P, NS, D], fp32) for u in (0, 1)]
    p.top = start
    psum = ExitStack()
    ps_x, ps_a, ps_b, ps_y = (psum.enter_context(nc.psum_tensor(f"ps_m1{n}", [P, 2, 512], fp32)) for n in "xaby")
    scattered, shared_loaded = p.pool_dma_sem("scattered1"), p.sem("shared_w_loaded")
    up_loaded = [p.sem(f"w13_loaded{u}") for u in (0, 1)]
    down_loaded = [p.sem(f"w2_loaded{u}") for u in (0, 1)]
    x_loaded = [p.sem(f"xe_loaded{u}") for u in (0, 1)]
    y_stored = [p.sem(f"ye_stored{u}") for u in (0, 1)]
    x_turned, x_copied = p.sem("xe_turned"), p.sem("xe_copied")
    up_made, silu_done, gated, down_made, y_copied = (p.sem("m1_" + n) for n in
                                                      ("up_made", "silu_done", "gated", "down_made", "y_copied"))

    with nc.Block() as block:
        @block.sync
        def _(sp):
            for n in ("sw1", "sw3", "sw2"):
                sp.dma_start(sw[n][:], d["m1_" + n].rearrange("(k p) h -> p k h", p=P)).then_inc(shared_loaded, 16)
            for u in (0, 1):
                sp.sem_inc(y_stored[u], 32)

            def load_weights(e, u):
                sp.wait_ge(up_made, (e + 1) * HT1 + B * HT1)
                for buf, n in ((w1, "w1"), (w3, "w3")):
                    sp.dma_start(buf[u][:], d["m1_" + n][bass.ds(e, 1)].rearrange("o (k p) h -> p (o k) h", p=P))\
                        .then_inc(up_loaded[u], 16)
                sp.wait_ge(down_made, e + 1 + B)
                sp.dma_start(w2[u][:], d["m1_w2"][bass.ds(e, 1)].rearrange("o (k p) h -> p (o k) h", p=P))\
                    .then_inc(down_loaded[u], 16)

            def load_rows(e, u):
                sp.wait_ge(x_turned, e + 1)
                sp.dma_start(xe[u][:, 0:FULL], c["slots_in1"][bass.ds(e * CAP, FULL * P), :].rearrange("(s p) d -> p s d", p=P))\
                    .then_inc(x_loaded[u], 16)
                sp.dma_start(xe[u][0:LAST, FULL], c["slots_in1"][bass.ds(e * CAP + FULL * P, LAST), :])\
                    .then_inc(x_loaded[u], 16)

            def store(e, u):
                sp.wait_ge(y_copied, e + 1 + B + 2)
                sp.dma_start(c["slots_out1"][bass.ds(e * CAP, FULL * P), :].rearrange("(s p) d -> p s d", p=P), ys[u][:, 0:FULL])\
                    .then_inc(y_stored[u], 16)
                sp.dma_start(c["slots_out1"][bass.ds(e * CAP + FULL * P, LAST), :], ys[u][0:LAST, FULL])\
                    .then_inc(y_stored[u], 16)

            sp.wait_ge(scattered, 16 * K1 * NT)
            in_steps(sp, E1, [(0, load_rows), (0, load_weights), (3, store)])
            for u in (0, 1):
                sp.wait_ge(y_stored[u], 32 * (E1 // 2 + 1))

        @block.gpsimd
        def _(pool):
            scatter_rows(p, c, 1, K1, pool, scattered)

        @block.tensor
        def _(pe):
            pe.sem_inc(up_made, 2 * HT1)
            pe.sem_inc(down_made, 2)
            pe.sem_inc(x_turned, 2)

            def up(item, wa, wb, rhs, n):
                for m in range(HT1):
                    pe.wait_ge(gated, (item + 2) * HT1 + m + 1 - HT1)
                    for ps, w in ((ps_a, wa), (ps_b, wb)):
                        for k in range(KT):
                            last = nc.tensor.matmul(ps[:, m, 0:n], w[:, k, m * P:(m + 1) * P], rhs(k),
                                                    start=k == 0, stop=k == KT - 1)
                    last.then_inc(up_made, 1)

            def down(item, u, w, tiles):
                pe.wait_ge(gated, (item + 3) * HT1)
                pe.wait_ge(y_copied, item + 2)
                for s, (at, n) in enumerate(tiles):
                    for k in range(HT1):
                        last = nc.tensor.matmul(ps_y[0:n, s // 2, s % 2 * D:s % 2 * D + D], gt[u][:, k, at:at + n], w[:, k],
                                                start=k == 0, stop=k == HT1 - 1)
                last.then_inc(down_made, 1)

            pe.wait_ge(shared_loaded, 48)
            in_steps(pe, B, [
                (0, lambda b, u: up(b, sw["sw1"], sw["sw3"], lambda k: XNT[:, k, bass.ds(b * S, S)], S)),
                (1, lambda b, u: down(b, u, sw["sw2"], [(0, P), (P, P)]))])

            def turn(e, u):
                pe.wait_ge(x_loaded[u], half(e, u) * 32 + 32)
                pe.wait_ge(x_copied, e + 1)
                for k in range(KT):
                    for s, (at, n) in enumerate(SLOT_TILES):
                        last = nc.tensor.transpose(ps_x[:, k, at:at + n], xe[u][0:n, s, k * P:(k + 1) * P],
                                                   c["ident"][0:n, 0:n])
                last.then_inc(x_turned, 1)

            def up_expert(e, u):
                pe.wait_ge(x_copied, e + 2)
                pe.wait_ge(up_loaded[u], half(e, u) * 32 + 32)
                up(e + B, w1[u], w3[u], lambda k: xt[u][:, k], CAP)

            def down_expert(e, u):
                pe.wait_ge(down_loaded[u], half(e, u) * 16 + 16)
                down(e + B, u, w2[u], SLOT_TILES)

            in_steps(pe, E1, [(0, turn), (1, up_expert), (2, down_expert)])

        @block.scalar
        def _(act):
            act.sem_inc(x_copied, 1)

            def silu(item, u, n):
                for m in range(HT1):
                    act.wait_ge(up_made, (item + 2) * HT1 + m + 1)
                    act.wait_ge(gated, item * HT1 + m + 1)
                    nc.scalar.activation(sl[u][:, m, 0:n], ps_a[:, m, 0:n], ACT.Silu).then_inc(silu_done, 1)

            in_steps(act, B, [(0, lambda b, u: silu(b, u, S))])

            def copy_x(e, u):
                act.wait_ge(x_turned, e + 3)
                act.wait_ge(up_made, (e + B + 1) * HT1)
                nc.scalar.activation(xt[u][:], ps_x[:, :, 0:CAP], ACT.Copy).then_inc(x_copied, 1)

            in_steps(act, E1, [(0, copy_x), (1, lambda e, u: silu(e + B, u, CAP))])

        @block.vector
        def _(dve):
            dve.sem_inc(gated, 2 * HT1)
            dve.sem_inc(y_copied, 2)

            def gate(item, u, n):
                dve.wait_ge(down_made, item + 1)
                for m in range(HT1):
                    dve.wait_ge(silu_done, item * HT1 + m + 1)
                    nc.vector.tensor_tensor(gt[u][:, m, 0:n], ps_b[:, m, 0:n], sl[u][:, m, 0:n], ALU.mult)\
                        .then_inc(gated, 1)

            def add_shared(b, u):
                dve.wait_ge(down_made, b + 3)
                at = X[:, bass.ds(b * TB, TB), :]
                nc.vector.tensor_tensor(at, ps_y[:, 0].rearrange("p (t d) -> p t d", t=TB), at, ALU.add).then_inc(y_copied, 1)

            in_steps(dve, B, [(0, lambda b, u: gate(b, u, S)), (1, add_shared)])

            def copy_y(e, u):
                dve.wait_ge(down_made, e + B + 3)
                dve.wait_ge(y_stored[u], half(e, u) * 32 + 32)
                nc.vector.tensor_copy(ys[u][:, 0:FULL], ps_y[:, 0].rearrange("p (t d) -> p t d", t=FULL)).then_inc(y_half, 1)
                nc.vector.tensor_copy(ys[u][0:LAST, FULL], ps_y[0:LAST, 1, 0:D]).then_inc(y_copied, 1)

            y_half = p.sem("ye_first_copied")
            in_steps(dve, E1, [(1, lambda e, u: gate(e + B, u, CAP)), (2, copy_y)])
    psum.close()


def combine_second(p, c):
    nc = p.nc
    X, W, SLOT = c["x"], c["weight"], c["slot_read"]
    start = p.top
    NB = 4
    yk = [p.sb(f"z_rows{n}", [P, K1, D], fp32) for n in range(NB)]
    p.top = start
    gathered = [p.pool_dma_sem(f"z_gathered{n}") for n in range(NB)]
    added, done = p.sem("z_added"), p.sem("out_stored")
    out = p.dram["out"].rearrange("(t p) d -> t p d", p=P)
    with nc.Block() as block:
        @block.sync
        def _(sp):
            for t in range(NT):
                sp.wait_ge(added, K1 * (t + 1))
                sp.dma_start(out[t], X[:, t]).then_inc(done, 16)
            sp.wait_ge(done, 16 * NT)

        @block.gpsimd
        def _(pool):
            for t in range(NT):
                if t >= NB:
                    pool.wait_ge(added, K1 * (t - NB + 1))
                for k in range(K1):
                    nc.gpsimd.indirect_dma_start(yk[t % NB][:, k], None, c["slots_out1"],
                                                 bass.IndirectOffsetOnAxis(ap=SLOT[:, k, t:t + 1], axis=0))\
                        .then_inc(gathered[t % NB], 16)

        @block.vector
        def _(dve):
            for t in range(NT):
                n = t % NB
                dve.wait_ge(gathered[n], 16 * K1 * (t // NB + 1))
                for k in range(K1):
                    nc.vector.scalar_tensor_tensor(X[:, t], yk[n][:, k], W[:, t, k:k + 1], X[:, t], ALU.mult, ALU.add)\
                        .then_inc(added, 1)
                    dve.wait_ge(added, K1 * t + k + 1)


def prepare_mixtures(p, c):
    nc = p.nc
    c["w1"] = p.sb("m0_w1", [P, E0, KT, H0], fp32)
    c["w2"] = p.sb("m0_w2", [P, E0, HT0, D], fp32)
    zero = p.sb("zero_row", [P, D], fp32)
    for l, n in ((0, TILES0 * P), (1, SLOTS1)):
        c[f"slots_in{l}"] = p.scratch(f"slots_in{l}", [n, D], fp32)
        c[f"slots_out{l}"] = p.scratch(f"slots_out{l}", [n, D], fp32)
    c["w_loaded"], zeroed, zero_set = p.sem("m0_w_loaded"), p.sem("slots_zeroed"), p.sem("zero_set")
    c["zeroed"] = zeroed
    with nc.Block() as block:
        @block.gpsimd
        def _(pool):
            nc.gpsimd.memset(zero[:], 0.0).then_inc(zero_set, 1)

        @block.sync
        def _(sp):
            sp.dma_start(c["w1"][:], p.dram["m0_w1"].rearrange("e (k p) h -> p e k h", p=P)).then_inc(c["w_loaded"], 16)
            sp.dma_start(c["w2"][:], p.dram["m0_w2"].rearrange("e (k p) h -> p e k h", p=P)).then_inc(c["w_loaded"], 16)
            sp.wait_ge(zero_set, 1)
            for l in (0, 1):
                n = c[f"slots_in{l}"].shape[0] // P
                sp.dma_start(c[f"slots_in{l}"].rearrange("(n p) d -> p n d", p=P),
                             zero[:].unsqueeze(1).broadcast_to([P, n, D])).then_inc(zeroed, 16)


def program(nc, dram):
    p = Program(nc, dram)
    with p.lasting:
        c = load_constants(p)
        routing_constants(p, c)
        prepare_mixtures(p, c)
        keys_and_values(p, c)
        queries(p, c, 0)
        attention(p, c, 0)
        kept = p.top
        route(p, c, 0, E0, K0)
        experts_first(p, c)
        combine_first(p, c)
        p.top = kept
        p.renew_semaphores()
        queries(p, c, 1)
        attention(p, c, 1)
        route(p, c, 1, E1, K1)
        experts_second(p, c)
        combine_second(p, c)
        p.stack.close()


def laid_out(inputs):
    def w_t(w):
        return w.T.reshape(KT, P, -1).transpose(1, 0, 2)

    a = {}
    a["x"] = inputs["x"].reshape(N, D)
    a["ctx"] = inputs["ctx_1024"].transpose(0, 2, 1).reshape(B, KT, P, S).transpose(0, 2, 1, 3)
    mask = inputs["mask_1x1xSxS2_ik0"].reshape(S, S)
    a["mask_qk"] = mask.reshape(TB, P, S).transpose(1, 0, 2)
    a["mask_kq"] = mask.T.reshape(TB, P, S).transpose(1, 0, 2)
    for l, names in ((0, ("Wq", "Wk", "Wv", "Wo")), (1, ("Wq", "Wk", "Wv", "Wu"))):
        for n, w in zip("qkvo", names):
            a[f"w{n}{l}"] = w_t(inputs[f"L{l}_xattn_{w}"])
    for n in ("bq", "bk"):
        a[n + "0"] = inputs[f"L0_xattn_{n}"].reshape(KT, P).T
    a["bv0"], a["bo0"], a["bo1"] = inputs["L0_xattn_bv"], inputs["L0_xattn_bo"], inputs["L1_xattn_bu"]
    for n in ("gate_w", "w1", "b1", "ln1_g", "ln1_b", "w2", "b2", "ln_g", "ln_b"):
        a["m0_" + n] = inputs["L0_ffn_" + n]
    for n in ("w1", "w2", "w3", "sw1", "sw2", "sw3"):
        a["m1_" + n] = inputs["L1_ffn_" + n]
    a["m0_gate_w"] = a["m0_gate_w"].reshape(KT, P, E0).transpose(1, 0, 2)
    a["m1_gate_w"] = w_t(inputs["L1_ffn_wg"])
    return {n: np.ascontiguousarray(v) for n, v in a.items()}


def kernel(**inputs):
    import concourse.bacc as bacc
    from concourse.bass_utils import run_bass_kernel_spmd

    arrays = laid_out({n: np.asarray(v) for n, v in inputs.items()})
    nc = bacc.Bacc("TRN2", target_bir_lowering=False, num_devices=1)
    dram = {n: nc.dram_tensor(f"in_{n}", v.shape, mybir.dt.from_np(v.dtype), kind="ExternalInput").ap()
            for n, v in arrays.items()}
    dram["out"] = nc.dram_tensor("out_x", [N, D], fp32, kind="ExternalOutput").ap()
    program(nc, dram)
    result = run_bass_kernel_spmd(nc, [{f"in_{n}": v for n, v in arrays.items()}], core_ids=[0])
    return result.results[0]["out_x"].reshape(B, S, D)
```

```python
import numpy as np
import concourse.bass as bass
from concourse import mybir
from contextlib import ExitStack

fp32 = mybir.dt.float32
fp32r = mybir.dt.float32r
bf16 = mybir.dt.bfloat16
int32 = mybir.dt.int32
ALU = mybir.AluOpType
ACT = mybir.ActivationFunctionType
AX = mybir.AxisListType

P = 128
B, S, D = 8, 256, 256
N = B * S
NT = N // P
TB = S // P
KT = D // P
H, DH = 16, 16
HV = 32
HQ = P // HV
NEG = -float(2 ** 100)
EPS = 1e-5
ROW_MAX = 64
STACK = ROW_MAX + 2

E0, K0, H0 = 8, 2, 512
HT0 = H0 // P
TILES0 = N * K0 // P + E0 - 1 + 1
E1, K1, H1 = 32, 4, 256
G1, LG1 = 8, 4
GE1 = E1 // G1
HT1 = H1 // P
CAP = int(1.25 * N * K1 / E1)
SLOTS1 = E1 * CAP
SLOT_TILES = [(s, min(P, CAP - s)) for s in range(0, CAP, P)]


class Program:

    def __init__(self, nc, dram):
        self.nc = nc
        self.dram = dram
        self.sems = {}
        self.stack = ExitStack()
        self.lasting = ExitStack()
        self.top = 16640
        self.limit = 229344

    def sem(self, name):
        if name not in self.sems:
            self.sems[name] = self.stack.enter_context(self.nc.semaphore(name))
        return self.sems[name]

    def pool_dma_sem(self, name):
        return self.lasting.enter_context(self.nc.semaphore(name))

    def renew_semaphores(self):
        with self.nc.Block() as block:
            @block.gpsimd
            def _(pool):
                for sem in self.sems.values():
                    pool.sem_clear(sem)
        self.stack.close()
        self.sems = {}

    def sb(self, name, shape, dtype):
        size = int(np.prod(shape[1:])) * (2 if dtype == bf16 else 4)
        at = self.top
        self.top = (at + size + 31) // 32 * 32
        assert self.top <= self.limit, (name, self.top)
        return self.nc.alloc_sbuf_tensor_at(name, shape, dtype, offset=at)

    def scratch(self, name, shape, dtype):
        return self.nc.dram_tensor(name, shape, dtype, kind="Internal").ap()


def across_partitions(ap, n):
    return bass.AP(ap.tensor, ap.offset, [[0, P], [1, n]])


def load_constants(p):
    nc, d = p.nc, p.dram
    c = {}
    c["x"] = p.sb("x_res", [P, NT, D], fp32)
    for l in (0, 1):
        for w in ("q", "k", "v", "o"):
            c[f"w{w}{l}"] = p.sb(f"w{w}{l}", [P, KT, D], fp32)
    for n in ("bq0", "bk0"):
        c[n] = p.sb(n, [P, KT], fp32)
    for n in ("bv0", "bo0", "bo1"):
        c[n] = p.sb(n, [P, D], fp32)
    c["ident"] = p.sb("ident", [P, P], fp32)
    c["identb"] = p.sb("identb", [P, P], bf16)
    c["mask_qk"] = p.sb("mask_qk", [P, TB, S], bf16)
    c["mask_kq"] = p.sb("mask_kq", [P, TB, S], bf16)
    c["minus_half"] = p.sb("minus_half", [P, NT], fp32)
    c["zero_row"] = p.sb("zero_row", [P, D], fp32)
    c["stats"] = p.sb("x_stats", [P, NT, 6], fp32)
    start = p.top
    raw = p.sb("mask_raw", [P, 2, TB, S], int32)
    p.top = start

    loaded, made = p.sem("constants_loaded"), p.sem("constants_made")
    ident_zero = p.sem("identity_zeroed")
    n_loads = 2 + 8 + 5 + 1
    with nc.Block() as block:
        @block.sync
        def _(sp):
            sp.dma_start(raw[:, 0], d["mask_qk"]).then_inc(loaded, 16)
            sp.dma_start(raw[:, 1], d["mask_kq"]).then_inc(loaded, 16)
            for l in (0, 1):
                for w in ("q", "k", "v", "o"):
                    sp.dma_start(c[f"w{w}{l}"][:], d[f"w{w}{l}"]).then_inc(loaded, 16)
            sp.dma_start(c["bq0"][:], d["bq0"]).then_inc(loaded, 16)
            sp.dma_start(c["bk0"][:], d["bk0"]).then_inc(loaded, 16)
            for n in ("bv0", "bo0", "bo1"):
                sp.dma_start(c[n][:], across_partitions(d[n], D)).then_inc(loaded, 16)
            sp.dma_start(c["x"][:], d["x"].rearrange("(t p) d -> p t d", p=P)).then_inc(loaded, 16)
            sp.wait_ge(loaded, 16 * n_loads)

        @block.gpsimd
        def _(pool):
            nc.gpsimd.memset(c["ident"][:], 0.0).then_inc(ident_zero, 1)
            nc.gpsimd.memset(c["identb"][:], 0.0).then_inc(ident_zero, 1)
            nc.gpsimd.memset(c["zero_row"][:], 0.0).then_inc(made, 1)
            pool.wait_ge(ident_zero, 2)
            for n in ("ident", "identb"):
                nc.gpsimd.affine_select(out=c[n][:], in_=c[n][:], compare_op=ALU.not_equal, fill=1.0, base=0,
                                        pattern=[[-1, P]], channel_multiplier=1).then_inc(made, 1)

        @block.vector
        def _(dve):
            nc.vector.memset(c["minus_half"][:], -0.5).then_inc(made, 1)
            dve.wait_ge(loaded, 16 * n_loads)
            for n, m in enumerate(("mask_qk", "mask_kq")):
                nc.vector.tensor_scalar(c[m][:], raw[:, n], 0, NEG, ALU.is_equal, ALU.mult).then_inc(made, 1)
            nc.vector.tensor_scalar(c["wq0"][:], c["wq0"][:], DH ** -0.5, None, ALU.mult).then_inc(made, 1)
            nc.vector.tensor_scalar(c["bq0"][:], c["bq0"][:], DH ** -0.5, None, ALU.mult).then_inc(made, 1)
            nc.vector.tensor_scalar(c["wq1"][:], c["wq1"][:], D ** -0.5, None, ALU.mult).then_inc(made, 1)
            dve.wait_ge(made, 9)
    return c


def keys_and_values(p, c):
    nc, d = p.nc, p.dram
    start = p.top
    ctx = [p.sb(f"ctx{u}", [P, KT, S], fp32) for u in (0, 1)]
    kk = [[p.sb(f"k_parts{u}{l}", [P, 2, KT, S], fp32r) for l in (0, 1)] for u in (0, 1)]
    vv = [[p.sb(f"v_ones{u}{l}", [P, TB, H, HV], fp32) for l in (0, 1)] for u in (0, 1)]
    p.top = start
    psum = ExitStack()
    ps_k = [psum.enter_context(nc.psum_tensor(f"ps_k{l}", [P, KT, S], fp32)) for l in (0, 1)]
    ps_v = [psum.enter_context(nc.psum_tensor(f"ps_v{l}", [P, TB, D], fp32)) for l in (0, 1)]
    for l in (0, 1):
        c[f"kd{l}"] = p.scratch(f"kd{l}", [2, D, N], fp32)
        c[f"vd{l}"] = p.scratch(f"vd{l}", [N, H * HV], fp32)

    ctx_loaded = [p.sem(f"ctx_loaded{u}") for u in (0, 1)]
    projected, k_high, emptied = p.sem("kv_projected"), p.sem("k_high"), p.sem("kv_emptied")
    stored, ones = [p.sem(f"kv_stored{u}") for u in (0, 1)], p.sem("v_ones_set")
    STORES = 6
    CREDIT = 2 * 4

    with nc.Block() as block:
        @block.sync
        def _(sp):
            def load(b, u):
                sp.wait_ge(projected, b * 4 + 4)
                sp.dma_start(ctx[u][:], d["ctx"][bass.ds(b, 1)].rearrange("o p k t -> p (o k) t")).then_inc(ctx_loaded[u], 16)

            def store(b, u):
                for l in (0, 1):
                    sp.wait_ge(emptied, b * 4 + 2 * l + 2 + 4)
                    for part in (0, 1):
                        sp.dma_start(c[f"kd{l}"][part, :, bass.ds(b * S, S)].rearrange("(m p) t -> p m t", p=P),
                                     kk[u][l][:, part].bitcast(fp32)).then_inc(stored[u], 16)
                    sp.dma_start(c[f"vd{l}"][bass.ds(b * S, S), :].rearrange("(t p) e -> p t e", p=P),
                                 vv[u][l][:].rearrange("p t h e -> p t (h e)")).then_inc(stored[u], 16)

            for u in (0, 1):
                sp.sem_inc(stored[u], 16 * STORES)
            load(0, 0)
            with sp.Fori(0, B // 2 - 1) as i:
                load(i * 2 + 1, 1)
                store(i * 2, 0)
                load(i * 2 + 2, 0)
                store(i * 2 + 1, 1)
            load(B - 1, 1)
            store(B - 2, 0)
            store(B - 1, 1)
            for u in (0, 1):
                sp.wait_ge(stored[u], (B // 2 + 1) * 16 * STORES)

        @block.tensor
        def _(pe):
            pe.sem_inc(projected, CREDIT)
            with pe.Fori(0, B // 2) as i:
                for u in (0, 1):
                    b = i * 2 + u
                    pe.wait_ge(ctx_loaded[u], i * 16 + 16)
                    for l in (0, 1):
                        pe.wait_ge(emptied, b * 4 + 2 * l + 1)
                        for m in range(KT):
                            for k in range(KT):
                                last = nc.tensor.matmul(ps_k[l][:, m], c[f"wk{l}"][:, k, m * P:(m + 1) * P], ctx[u][:, k],
                                                        start=k == 0, stop=k == KT - 1)
                        last.then_inc(projected, 1)
                        pe.wait_ge(emptied, b * 4 + 2 * l + 2)
                        for t in range(TB):
                            for k in range(KT):
                                last = nc.tensor.matmul(ps_v[l][:, t], ctx[u][:, k, t * P:(t + 1) * P], c[f"wv{l}"][:, k],
                                                        start=k == 0, stop=k == KT - 1)
                        last.then_inc(projected, 1)

        @block.scalar
        def _(act):
            with act.Fori(0, B // 2) as i:
                for u in (0, 1):
                    b = i * 2 + u
                    act.wait_ge(stored[u], i * 16 * STORES + 16 * STORES)
                    for l in (0, 1):
                        act.wait_ge(projected, b * 4 + 2 * l + 1 + CREDIT)
                        for m in range(KT):
                            if l == 0:
                                ins = nc.scalar.activation(kk[u][l][:, 0, m], ps_k[l][:, m], ACT.Identity,
                                                           bias=c["bk0"][:, m:m + 1])
                            else:
                                ins = nc.scalar.activation(kk[u][l][:, 0, m], ps_k[l][:, m], ACT.Copy)
                        ins.then_inc(k_high, 1)

        @block.vector
        def _(dve):
            for u in (0, 1):
                for l in (0, 1):
                    nc.vector.memset(vv[u][l][:, :, :, DH:DH + 1], 1.0).then_inc(ones, 1)
                    nc.vector.memset(vv[u][l][:, :, :, DH + 1:HV], 0.0).then_inc(ones, 1)
            for t in range(NT):
                nc.vector.bn_stats(c["stats"][:, t], c["x"][:, t]).then_inc(ones, 1)
            dve.wait_ge(ones, 8 + NT)
            dve.sem_inc(emptied, 4)
            with dve.Fori(0, B // 2) as i:
                for u in (0, 1):
                    b = i * 2 + u
                    dve.wait_ge(stored[u], i * 16 * STORES + 16 * STORES)
                    for l in (0, 1):
                        dve.wait_ge(k_high, b * 2 + l + 1)
                        for m in range(KT):
                            high = kk[u][l][:, 0, m].bitcast(fp32)
                            if l == 0:
                                ins = nc.vector.scalar_tensor_tensor(kk[u][l][:, 1, m], ps_k[l][:, m], c["bk0"][:, m:m + 1],
                                                                     high, ALU.add, ALU.subtract)
                            else:
                                ins = nc.vector.tensor_tensor(kk[u][l][:, 1, m], ps_k[l][:, m], high, ALU.subtract)
                        ins.then_inc(emptied, 1)
                        dve.wait_ge(projected, b * 4 + 2 * l + 2 + CREDIT)
                        for t in range(TB):
                            heads = ps_v[l][:, t].rearrange("p (h e) -> p h e", h=H)
                            if l == 0:
                                ins = nc.vector.tensor_tensor(vv[u][l][:, t, :, 0:DH], heads,
                                                              c["bv0"][:].rearrange("p (h e) -> p h e", h=H), ALU.add)
                            else:
                                ins = nc.vector.tensor_copy(vv[u][l][:, t, :, 0:DH], heads)
                        ins.then_inc(emptied, 1)
    psum.close()


def queries(p, c, l):
    nc = p.nc
    start = p.top
    mv = p.sb(f"mean_var{l}", [P, NT, 2], fp32)
    var = p.sb(f"var{l}", [P, NT], fp32)
    rstd = p.sb(f"rstd{l}", [P, NT], fp32)
    xn = [p.sb(f"xn{l}{u}", [P, TB, D], fp32) for u in (0, 1)]
    xnt = [p.sb(f"xnt{l}{u}", [P, KT, S], fp32) for u in (0, 1)]
    qq = [p.sb(f"q_parts{l}{u}", [P, 2, KT, S], fp32r) for u in (0, 1)]
    p.top = start
    psum = ExitStack()
    ps_t = [psum.enter_context(nc.psum_tensor(f"ps_xt{l}{u}", [P, KT, S], fp32)) for u in (0, 1)]
    ps_q = [psum.enter_context(nc.psum_tensor(f"ps_q{l}{u}", [P, KT, S], fp32)) for u in (0, 1)]
    c[f"qd{l}"] = p.scratch(f"qd{l}", [2, D, N], fp32)
    X = c["x"]

    stats_done, var_done, rstd_done = p.sem(f"stats_done{l}"), p.sem(f"var_done{l}"), p.sem(f"rstd_done{l}")
    xn_done, xt_done, xt_copied = p.sem(f"xn_done{l}"), p.sem(f"xt_done{l}"), p.sem(f"xt_copied{l}")
    q_done, q_high, q_low = p.sem(f"q_done{l}"), p.sem(f"q_high{l}"), p.sem(f"q_low{l}")
    stored = [p.sem(f"q_stored{l}{u}") for u in (0, 1)]
    bias_added = p.sem(f"bias_added{l}")

    with nc.Block() as block:
        @block.sync
        def _(sp):
            for u in (0, 1):
                sp.sem_inc(stored[u], 32)
            with sp.Fori(0, B // 2) as i:
                for u in (0, 1):
                    b = i * 2 + u
                    sp.wait_ge(q_low, b + 3)
                    for part in (0, 1):
                        sp.dma_start(c[f"qd{l}"][part, :, bass.ds(b * S, S)].rearrange("(m p) t -> p m t", p=P),
                                     qq[u][:, part].bitcast(fp32)).then_inc(stored[u], 16)
            for u in (0, 1):
                sp.wait_ge(stored[u], (B // 2 + 1) * 32)

        @block.gpsimd
        def _(pool):
            pool.wait_ge(var_done, 1)
            nc.gpsimd.tensor_tensor(rstd[:], var[:], c["minus_half"][:], ALU.pow).then_inc(rstd_done, 1)
            with pool.Fori(0, B) as b:
                pool.wait_ge(xn_done, b + 1)
                for t in range(TB):
                    at = X[:, bass.ds(b * TB + t, 1), :].rearrange("p o d -> p (o d)")
                    nc.gpsimd.tensor_tensor(at, at, c[f"bo{l}"][:], ALU.add).then_inc(bias_added, 1)
            pool.wait_ge(bias_added, NT)

        @block.vector
        def _(dve):
            for t in range(NT):
                nc.vector.bn_aggr(mv[:, t], c["stats"][:, t]).then_inc(stats_done, 1)
            dve.wait_ge(stats_done, NT)
            nc.vector.tensor_scalar(var[:], mv[:, :, 1], EPS, None, ALU.add).then_inc(var_done, 1)
            dve.wait_ge(rstd_done, 1)
            dve.sem_inc(q_low, 2)

            def low(b, u):
                dve.wait_ge(q_high, b + 1)
                for m in range(KT):
                    high = qq[u][:, 0, m].bitcast(fp32)
                    if l == 0:
                        ins = nc.vector.scalar_tensor_tensor(qq[u][:, 1, m], ps_q[u][:, m], c["bq0"][:, m:m + 1],
                                                             high, ALU.add, ALU.subtract)
                    else:
                        ins = nc.vector.tensor_tensor(qq[u][:, 1, m], ps_q[u][:, m], high, ALU.subtract)
                ins.then_inc(q_low, 1)

            def norm(b, u):
                dve.wait_ge(xt_done, b + 1)
                for t in range(TB):
                    tile = b * TB + t
                    ins = nc.vector.tensor_scalar(xn[u][:, t], X[:, bass.ds(tile, 1), :].rearrange("p o d -> p (o d)"),
                                                  mv[:, bass.ds(tile, 1), 0], rstd[:, bass.ds(tile, 1)],
                                                  ALU.subtract, ALU.mult)
                ins.then_inc(xn_done, 1)

            in_steps(dve, B, [(0, norm), (2, low)])

        @block.tensor
        def _(pe):
            pe.sem_inc(xt_done, 2)

            def transposes(b, u):
                pe.wait_ge(xn_done, b + 1)
                pe.wait_ge(xt_copied, b + 1)
                for t in range(TB):
                    for k in range(KT):
                        last = nc.tensor.transpose(ps_t[u][:, k, t * P:(t + 1) * P], xn[u][:, t, k * P:(k + 1) * P],
                                                   c["ident"][:])
                last.then_inc(xt_done, 1)

            def project(b, u):
                pe.wait_ge(xt_copied, b + 3)
                pe.wait_ge(q_low, b + 1)
                for m in range(KT):
                    for k in range(KT):
                        last = nc.tensor.matmul(ps_q[u][:, m], c[f"wq{l}"][:, k, m * P:(m + 1) * P], xnt[u][:, k],
                                                start=k == 0, stop=k == KT - 1)
                last.then_inc(q_done, 1)

            in_steps(pe, B, [(0, transposes), (1, project)])

        @block.scalar
        def _(act):
            act.sem_inc(xt_copied, 2)

            def copy(b, u):
                act.wait_ge(xt_done, b + 3)
                act.wait_ge(q_done, b + 1)
                nc.scalar.activation(xnt[u][:], ps_t[u][:], ACT.Copy).then_inc(xt_copied, 1)

            def high(b, u):
                act.wait_ge(q_done, b + 3)
                act.wait_ge(stored[u], use_of(b, u) * 32 + 32)
                for m in range(KT):
                    if l == 0:
                        ins = nc.scalar.activation(qq[u][:, 0, m], ps_q[u][:, m], ACT.Identity, bias=c["bq0"][:, m:m + 1])
                    else:
                        ins = nc.scalar.activation(qq[u][:, 0, m], ps_q[u][:, m], ACT.Copy)
                ins.then_inc(q_high, 1)

            act.sem_inc(q_done, 2)
            in_steps(act, B, [(0, copy), (1, high)])
    psum.close()


def attention(p, c, l, background):
    nc = p.nc
    masked = l == 0
    start = p.top
    KS = [p.sb(f"k_stack{l}{u}", [STACK, H, S], fp32r) for u in (0, 1)]
    QS = [p.sb(f"q_stack{l}{u}", [STACK, H, S], fp32r) for u in (0, 1)]
    V = [p.sb(f"v{l}{u}", [P, TB, H, HV], fp32) for u in (0, 1)]
    NMAX = [p.sb(f"neg_max{l}{u}", [P, TB, H], fp32) for u in (0, 1)]
    MT = p.sb(f"neg_max_t{l}", [H, 2, S], fp32r)
    NP = 4
    PT = p.sb(f"probs{l}", [P, NP, TB, S], fp32)
    VT = p.sb(f"mixed_t{l}", [P, 2, S], fp32)
    RINV = p.sb(f"rinv{l}", [P, TB, H], fp32)
    O = p.sb(f"attn{l}", [P, TB, D], fp32)
    OT = p.sb(f"attn_t{l}", [P, KT, S], fp32)
    p.top = start
    psum = ExitStack()
    ps_s = [psum.enter_context(nc.psum_tensor(f"ps_s{l}{u}", [P, 2, S], fp32)) for u in (0, 1)]
    ps_p = [psum.enter_context(nc.psum_tensor(f"ps_p{l}{u}", [P, TB, S], fp32)) for u in (0, 1)]
    ps_v = psum.enter_context(nc.psum_tensor(f"ps_vt{l}", [P, 512], fp32))
    ps_o = psum.enter_context(nc.psum_tensor(f"ps_o{l}", [P, TB, 512], fp32))
    ps_m = psum.enter_context(nc.psum_tensor(f"ps_m{l}", [P, 512], fp32))
    ps_y = ps_o[:, 0].rearrange("p (t d) -> p t d", t=TB)
    md = p.scratch(f"md{l}", [B, 2, H, S], fp32)
    X = c["x"]

    stacks_set = p.sem(f"stacks_set{l}")
    loaded = [[p.sem(f"kqv_loaded{l}{u}{part}") for part in (0, 1)] for u in (0, 1)]
    scored = p.sem(f"scored{l}")
    reduced = p.sem(f"max_reduced{l}")
    max_turned = p.sem(f"max_turned{l}")
    max_split = p.sem(f"max_split{l}")
    max_stored, max_loaded = p.sem(f"max_stored{l}"), p.sem(f"max_loaded{l}")
    shifted = p.sem(f"scores_shifted{l}")
    probs_done = p.sem(f"probs_done{l}")
    mixed = p.sem(f"values_mixed{l}")
    o_scaled, o_turned, ot_copied = p.sem(f"o_scaled{l}"), p.sem(f"o_turned{l}"), p.sem(f"ot_copied{l}")
    vt_copied, vt_turned = p.sem(f"vt_copied{l}"), p.sem(f"vt_turned{l}")
    y_done, x_added = p.sem(f"y_done{l}"), p.sem(f"x_added{l}")
    LOADS = 7 * 16
    HH = H // 2
    G = H // HQ
    UNITS = (1, 1, 2, 1, 2, 1, 2, 2, 2, 2, 0, 0, 0, 0, 0, 0)
    assert sum(UNITS) == H and sum(UNITS[:6]) == HH
    TURN_MAXIMA = 10
    TURN_MIXED = {10: 0, 12: 1, 14: 2}
    TURN_LAST, NORMALISE, TURN_O, COPY_O, PROJECT, ADD = 1, 2, 5, 6, 7, 8


    def units(h):
        return range(sum(UNITS[:h]), sum(UNITS[:h + 1]))

    def exists(b, ahead):
        return not isinstance(b, int) or 0 <= b + ahead < B

    def each_batch(engine, f):
        f(0, 0)
        f(1, 1)
        with engine.Fori(0, B // 2 - 2) as i:
            f(i * 2 + 2, 0)
            f(i * 2 + 3, 1)
        f(B - 2, 0)
        f(B - 1, 1)

    with nc.Block() as block:
        @block.gpsimd
        def _(pool):
            for u in (0, 1):
                for z in (KS[u], QS[u]):
                    nc.gpsimd.memset(z[32:64].bitcast(fp32), 0.0).then_inc(stacks_set, 1)
                nc.gpsimd.memset(KS[u][ROW_MAX:STACK].bitcast(fp32), 1.0).then_inc(stacks_set, 1)
            background(pool)

        @block.sync
        def _(sp):
            def load(b, u, part):
                sp.wait_ge(mixed, b * H + (part + 1) * HH)
                heads = slice(part * HH, (part + 1) * HH)
                for name, buf, parts in (("kd", KS[u], (0, 1, 0)), ("qd", QS[u], (0, 0, 1))):
                    for row, hl in enumerate(parts):
                        src = c[f"{name}{l}"][hl, :, bass.ds(b * S, S)].rearrange("(h e) t -> e h t", h=H)
                        sp.dma_start(buf[row * DH:(row + 1) * DH, heads].bitcast(fp32), src[:, heads])\
                            .then_inc(loaded[u][part], 16)
                sp.dma_start(V[u][:, :, heads],
                             c[f"vd{l}"][bass.ds(b * S, S), :].rearrange("(t p) (h e) -> p t h e", p=P, h=H)[:, :, heads])\
                    .then_inc(loaded[u][part], 16)

            def maxima(b, u):
                sp.wait_ge(max_split, b * 2 + 2)
                sp.dma_start(md[bass.ds(b, 1)].rearrange("o a h t -> h (o a) t"), MT[:].bitcast(fp32)).then_inc(max_stored, 16)
                sp.wait_ge(max_stored, b * 16 + 16)
                sp.dma_start(QS[u][ROW_MAX:STACK].rearrange("a h t -> a (h t)").bitcast(fp32),
                             md[bass.ds(b, 1)].rearrange("o a h t -> (o a) (h t)")).then_inc(max_loaded, 16)

            sp.wait_ge(stacks_set, 6)
            load(0, 0, 0)
            load(0, 0, 1)
            load(1, 1, 0)
            maxima(0, 0)

            def batch(b, u):
                if exists(b, 1):
                    load(b + 1, 1 - u, 1)
                if exists(b, 2):
                    load(b + 2, u, 0)
                if exists(b, 1):
                    maxima(b + 1, 1 - u)
            each_batch(sp, batch)

        @block.tensor
        def _(pe):
            pe.sem_inc(mixed, 2 * H)
            pe.sem_inc(vt_turned, 2)

            def score(b, u, n):
                if n % HH == 0:
                    pe.wait_ge(loaded[u][n // HH], (use_of(b, u) + 1) * LOADS)
                pe.wait_ge(reduced, b * H + n + 1)
                bank, qt = ps_s[n % 2], n % 2
                for j in (0, 1):
                    h = 2 * (n // 2) + j
                    last = nc.tensor.matmul(bank[:, j], QS[u][0:3 * DH, h, qt * P:(qt + 1) * P], KS[u][0:3 * DH, h],
                                            start=True, stop=not masked)
                    if masked:
                        last = nc.tensor.matmul(bank[:, j], c["identb"][:], c["mask_qk"][:, qt], start=False, stop=True)
                last.then_inc(scored, 1)

            def turn_maxima(b, u):
                pe.wait_ge(reduced, b * H + H + 2)
                for qt in range(TB):
                    last = nc.tensor.transpose(ps_m[0:H, qt * P:(qt + 1) * P], NMAX[u][:, qt], c["ident"][:])
                last.then_inc(max_turned, 1)

            def shift(b, u, h):
                pe.wait_ge(probs_done, b * H + h + 1)
                for kt in range(TB):
                    last = nc.tensor.matmul(ps_p[h % 2][:, kt], KS[u][:, h, kt * P:(kt + 1) * P], QS[u][:, h],
                                            start=True, stop=not masked)
                    if masked:
                        last = nc.tensor.matmul(ps_p[h % 2][:, kt], c["identb"][:], c["mask_kq"][:, kt],
                                                start=False, stop=True)
                last.then_inc(shifted, 1)

            def mix(b, u, h):
                pe.wait_ge(probs_done, b * H + h + 3)
                if h % HQ == 0:
                    pe.wait_ge(vt_copied, b * G + h // HQ + 1)
                rows = ps_v[h % HQ * HV:(h % HQ + 1) * HV, 0:S]
                for kt in range(TB):
                    last = nc.tensor.matmul(rows, V[u][:, kt, h], PT[:, h % NP, kt], start=kt == 0, stop=kt == TB - 1)
                last.then_inc(mixed, 1)

            def turn_mixed(b, g):
                pe.wait_ge(vt_copied, b * G + g + 2)
                if g == 0:
                    pe.wait_ge(o_scaled, b + 1)
                    pe.wait_ge(x_added, b + 1)
                for qt in range(TB):
                    last = nc.tensor.transpose(ps_o[:, qt, g * P:(g + 1) * P], VT[:, g % 2, qt * P:(qt + 1) * P], c["ident"][:])
                last.then_inc(vt_turned, 1)

            def turn_o(b):
                pe.wait_ge(o_scaled, b + 2)
                if exists(b, 1):
                    pe.wait_ge(max_split, b * 2 + 4)
                for k in range(KT):
                    for t in range(TB):
                        last = nc.tensor.transpose(ps_m[:, k * S + t * P:k * S + (t + 1) * P], O[:, t, k * P:(k + 1) * P],
                                                   c["ident"][:])
                last.then_inc(o_turned, 1)

            def project(b):
                pe.wait_ge(ot_copied, b + 1)
                for t in range(TB):
                    for k in range(KT):
                        last = nc.tensor.matmul(ps_y[:, t], OT[:, k, t * P:(t + 1) * P], c[f"wo{l}"][:, k],
                                                start=k == 0, stop=k == KT - 1)
                last.then_inc(y_done, 1)

            for n in range(H):
                score(0, 0, n)
            turn_maxima(0, 0)

            def batch(b, u):
                pe.wait_ge(max_loaded, b * 16 + 16)
                for h in range(H):
                    shift(b, u, h)
                    if exists(b, 1):
                        for n in units(h):
                            score(b + 1, 1 - u, n)
                    if h >= 1:
                        mix(b, u, h - 1)
                    elif exists(b, -1):
                        mix(b - 1, 1 - u, H - 1)
                    if exists(b, 1) and h == TURN_MAXIMA:
                        turn_maxima(b + 1, 1 - u)
                    if exists(b, -1):
                        if h == TURN_LAST:
                            turn_mixed(b - 1, G - 1)
                        if h == TURN_O:
                            turn_o(b - 1)
                        if h == PROJECT:
                            project(b - 1)
                    if h in TURN_MIXED:
                        turn_mixed(b, TURN_MIXED[h])
            each_batch(pe, batch)
            mix(B - 1, (B - 1) % 2, H - 1)
            turn_mixed(B - 1, G - 1)
            turn_o(B - 1)
            project(B - 1)

        @block.vector
        def _(dve):
            dve.sem_inc(reduced, 2)
            dve.sem_inc(o_scaled, 1)
            dve.sem_inc(x_added, 1)

            def reduce(b, u, n):
                dve.wait_ge(scored, b * H + n + 1)
                hp = 2 * (n // 2)
                nc.vector.tensor_reduce(NMAX[u][:, n % 2, hp:hp + 2], ps_s[n % 2][:], AX.X, ALU.max,
                                        negate=True).then_inc(reduced, 1)

            def split_maxima(b):
                dve.wait_ge(max_turned, b + 1)
                if exists(b, -1):
                    dve.wait_ge(max_stored, b * 16)
                rows = ps_m[0:H, 0:S]
                nc.vector.tensor_copy(MT[:, 0], rows).then_inc(max_split, 1)
                dve.wait_ge(max_split, b * 2 + 1)
                nc.vector.tensor_tensor(MT[:, 1], rows, MT[:, 0].bitcast(fp32), ALU.subtract).then_inc(max_split, 1)

            sums = ps_o[:].rearrange("p t (h e) -> p t h e", h=H)

            def invert(b):
                dve.wait_ge(vt_turned, (b + 1) * G + 2)
                nc.vector.reciprocal(RINV[:], sums[:, :, :, DH]).then_inc(rinv_done, 1)

            def normalise(b, t):
                dve.wait_ge(rinv_done, b + 1)
                ins = nc.vector.tensor_tensor(O[:, t].rearrange("p (h e) -> p h e", h=H), sums[:, t, :, 0:DH],
                                              RINV[:, t].unsqueeze(2).broadcast_to([P, H, DH]), ALU.mult)
                if t == TB - 1:
                    ins.then_inc(o_scaled, 1)

            def add(b):
                dve.wait_ge(y_done, b + 1)
                at = X[:, bass.ds(b * TB, TB), :]
                nc.vector.tensor_tensor(at, ps_y[:], at, ALU.add).then_inc(x_added, 1)

            def stats(b, t):
                dve.wait_ge(x_added, b + 2)
                nc.vector.bn_stats(c["stats"][:, bass.ds(b * TB + t, 1), :], X[:, bass.ds(b * TB + t, 1), :])\
                    .then_inc(stats_done, 1)

            rinv_done, stats_done = p.sem(f"rinv_done{l}"), p.sem(f"x_stats_done{l}")
            for n in range(H):
                reduce(0, 0, n)
            split_maxima(0)

            def batch(b, u):
                for h in range(H):
                    if exists(b, 1):
                        if h == TURN_MAXIMA:
                            split_maxima(b + 1)
                        for n in units(h):
                            reduce(b + 1, 1 - u, n)
                    if exists(b, -1):
                        if h == NORMALISE:
                            invert(b - 1)
                        if h > NORMALISE and h - NORMALISE <= TB:
                            normalise(b - 1, h - NORMALISE - 1)
                        if h == ADD:
                            add(b - 1)
                        if h > ADD and h - ADD <= TB:
                            stats(b - 1, h - ADD - 1)
            each_batch(dve, batch)
            invert(B - 1)
            for t in range(TB):
                normalise(B - 1, t)
            add(B - 1)
            for t in range(TB):
                stats(B - 1, t)
            dve.wait_ge(stats_done, NT)

        @block.scalar
        def _(act):
            act.sem_inc(probs_done, 2)
            act.sem_inc(vt_copied, 1)

            def copy_mixed(b, g):
                act.wait_ge(mixed, b * H + (g + 1) * HQ + 2 * H)
                act.wait_ge(vt_turned, b * G + g + 1)
                nc.scalar.activation(VT[:, g % 2], ps_v[:, 0:S], ACT.Copy).then_inc(vt_copied, 1)

            def copy_o(b):
                act.wait_ge(o_turned, b + 1)
                nc.scalar.activation(OT[:].rearrange("p k t -> p (k t)"), ps_m[:], ACT.Copy).then_inc(ot_copied, 1)

            def batch(b, u):
                for h in range(H):
                    act.wait_ge(shifted, b * H + h + 1)
                    act.wait_ge(mixed, b * H + h + 1 + 2 * H - NP)
                    nc.scalar.activation(PT[:, h % NP], ps_p[h % 2][:], ACT.Exp).then_inc(probs_done, 1)
                    if h % HQ == 0:
                        if h > 0:
                            copy_mixed(b, h // HQ - 1)
                        elif exists(b, -1):
                            copy_mixed(b - 1, G - 1)
                    if h == COPY_O and exists(b, -1):
                        copy_o(b - 1)
            each_batch(act, batch)
            copy_mixed(B - 1, G - 1)
            copy_o(B - 1)
    psum.close()


def in_steps(engine, n, stages, unroll=2):
    most = max(lag for lag, _ in stages)
    first = (most + unroll - 1) // unroll
    last = n // unroll

    def step(s, place):
        for lag, f in stages:
            if not isinstance(s, int) or 0 <= s - lag < n:
                f(s - lag, (place - lag) % unroll)

    for s in range(unroll * first):
        step(s, s % unroll)
    with engine.Fori(0, last - first) as i:
        for place in range(unroll):
            step(i * unroll + unroll * first + place, place)
    for s in range(unroll * last, n + most):
        step(s, s % unroll)


def routing_constants(p, c):
    nc = p.nc
    c["count_i"] = p.sb("count_i", [P, TILES0], int32)
    c["count"] = p.sb("count", [P, TILES0], fp32)
    c["before"] = p.sb("before", [P, P], bf16)
    c["ones"] = p.sb("ones", [P, P], bf16)
    made = p.sem("routing_constants")
    with nc.Block() as block:
        @block.gpsimd
        def _(pool):
            nc.gpsimd.iota(c["count_i"][:], pattern=[[1, TILES0]], base=0, channel_multiplier=0).then_inc(made, 1)
            nc.gpsimd.memset(c["ones"][:], 1.0).then_inc(made, 1)
            nc.gpsimd.memset(c["before"][:], 1.0).then_inc(made, 1)
            pool.wait_ge(made, 3)
            nc.gpsimd.affine_select(out=c["before"][:], in_=c["before"][:], compare_op=ALU.is_gt, fill=0.0, base=0,
                                    pattern=[[1, P]], channel_multiplier=-1).then_inc(made, 1)

        @block.vector
        def _(dve):
            dve.wait_ge(made, 4)
            nc.vector.tensor_copy(c["count"][:], c["count_i"][:]).then_inc(made, 1)
            dve.wait_ge(made, 5)


def route(p, c, l, E, K):
    nc = p.nc
    XN = c["xn"] = p.sb(f"xn_all{l}", [P, NT, D], fp32)
    SLOT = p.sb(f"slot{l}", [P, K, NT], int32)
    W = p.sb(f"choice_weight{l}", [P, NT, 8], fp32)
    gate = p.sb(f"gate{l}", [P, KT, E], fp32)
    TE = p.sb(f"tile_expert{l}", [P, TILES0], int32)
    c["slot"], c["weight"], c["tile_expert"] = SLOT, W, TE
    if l == 1:
        c["slot_read"] = p.sb("slot_read", [P, K, NT], int32)
        XNT = c["xnt"] = p.sb("xn_turned", [P, KT, N], fp32)
    start = p.top
    mv = p.sb(f"m_mean_var{l}", [P, NT, 2], fp32)
    var = p.sb(f"m_var{l}", [P, NT], fp32)
    rstd = p.sb(f"m_rstd{l}", [P, NT], fp32)
    xn = [p.sb(f"m_xn{l}{u}", [P, TB, D], fp32) for u in (0, 1)]
    xnt = [p.sb(f"m_xnt{l}{u}", [P, KT, S], fp32) for u in (0, 1)]
    top = p.sb(f"top{l}", [P, NT], fp32)
    ex = p.sb(f"gate_exp{l}", [P, NT, E], fp32)
    total = p.sb(f"gate_sum{l}", [P, NT], fp32)
    prob = p.sb(f"gate_prob{l}", [P, NT, E], fp32)
    idx = p.sb(f"choice{l}", [P, NT, 8], mybir.dt.uint32)
    idxf = p.sb(f"choice_f{l}", [P, NT, 8], fp32)
    hot = [p.sb(f"chosen{l}{k}", [P, NT, E], fp32) for k in range(K)]
    M = p.sb(f"chosen{l}", [P, NT, E], bf16)
    where = p.sb(f"where{l}", [P, NT, E], fp32)
    picked = p.sb(f"picked{l}", [P, NT, E], fp32)
    slotf = p.sb(f"slot_f{l}", [P, K, NT], fp32)
    if l == 0:
        cnt_i = p.sb("tiles_i", [P, E], int32)
        tiles = p.sb("tiles_f", [P, E], fp32)
        ends = p.sb("tile_ends", [P, E], fp32)
        base = p.sb("slot_base", [P, E], fp32)
        past = p.sb("tiles_past", [P, TILES0, E], fp32)
        te = p.sb("tile_expert_f", [P, TILES0], fp32)
    else:
        gmax = p.sb("group_max", [P, NT, G1], fp32)
        g8 = p.sb("group_top", [P, NT, 8], fp32)
        gidx = p.sb("group_choice", [P, NT, 8], mybir.dt.uint32)
        gidxf = p.sb("group_choice_f", [P, NT, 8], fp32)
        same = p.sb("group_same", [P, NT, G1, LG1], fp32)
        keep = p.sb("group_kept", [P, NT, G1], fp32)
        drop = p.sb("group_dropped", [P, NT, G1], fp32)
        kept = p.sb("prob_kept", [P, NT, E], fp32)
        pos = p.sb("choice_position", [P, NT], fp32)
        fits = p.sb("choice_fits", [P, NT], fp32)
        over_cap = p.sb("choice_over", [P, NT], fp32)
    p.top = start
    psum = ExitStack()
    ps_t = [psum.enter_context(nc.psum_tensor(f"ps_mt{l}{u}", [P, KT, S], fp32)) for u in (0, 1)]
    ps_l = psum.enter_context(nc.psum_tensor(f"ps_l{l}", [P, NT, E], fp32))
    ps_w = psum.enter_context(nc.psum_tensor(f"ps_w{l}", [P, NT, E], fp32))
    ps_c = psum.enter_context(nc.psum_tensor(f"ps_c{l}", [P, E], fp32))
    X = c["x"]
    gate_loaded = p.sem(f"gate_loaded{l}")
    stats_done, var_done, rstd_done = p.sem(f"m_stats_done{l}"), p.sem(f"m_var_done{l}"), p.sem(f"m_rstd_done{l}")
    xn_done, xt_done, xt_copied = p.sem(f"m_xn_done{l}"), p.sem(f"m_xt_done{l}"), p.sem(f"m_xt_copied{l}")
    xn_kept, xt_kept, logits_done = p.sem(f"m_xn_kept{l}"), p.sem(f"m_xt_kept{l}"), p.sem(f"logits_done{l}")
    shifted, exp_done = p.sem(f"gate_shifted{l}"), p.sem(f"gate_exp_done{l}")
    step, chosen, counted = p.sem(f"route_step{l}"), p.sem(f"chosen_done{l}"), p.sem(f"counted{l}")
    slots_done = p.sem(f"slots_done{l}")
    c["slots_done"] = slots_done

    with nc.Block() as block:
        @block.sync
        def _(sp):
            sp.dma_start(gate[:], p.dram[f"m{l}_gate_w"]).then_inc(gate_loaded, 16)

        @block.gpsimd
        def _(pool):
            pool.wait_ge(var_done, 1)
            nc.gpsimd.tensor_tensor(rstd[:], var[:], c["minus_half"][:], ALU.pow).then_inc(rstd_done, 1)
            pool.sem_inc(xn_kept, 2)
            pool.sem_inc(xt_kept, 2)
            with pool.Fori(0, B // 2) as i:
                for u in (0, 1):
                    pool.wait_ge(xn_done, i * 2 + u + 1)
                    nc.gpsimd.tensor_copy(XN[:, bass.ds((i * 2 + u) * TB, TB), :], xn[u][:]).then_inc(xn_kept, 1)
                    if l == 1:
                        pool.wait_ge(xt_copied, i * 2 + u + 3)
                        nc.gpsimd.tensor_copy(XNT[:, :, bass.ds((i * 2 + u) * S, S)], xnt[u][:]).then_inc(xt_kept, 1)
            pool.wait_ge(xn_kept, B + 2)

        @block.tensor
        def _(pe):
            pe.sem_inc(xt_done, 2)
            pe.wait_ge(gate_loaded, 16)

            def transposes(b, u):
                pe.wait_ge(xn_done, b + 1)
                pe.wait_ge(xt_copied, b + 1)
                for t in range(TB):
                    for k in range(KT):
                        last = nc.tensor.transpose(ps_t[u][:, k, t * P:(t + 1) * P], xn[u][:, t, k * P:(k + 1) * P],
                                                   c["ident"][:])
                last.then_inc(xt_done, 1)

            def logits(b, u):
                pe.wait_ge(xt_copied, b + 3)
                for t in range(TB):
                    at = ps_l[:, bass.ds(b * TB + t, 1), :].rearrange("p o e -> p (o e)")
                    for k in range(KT):
                        last = nc.tensor.matmul(at, xnt[u][:, k, t * P:(t + 1) * P], gate[:, k],
                                                start=k == 0, stop=k == KT - 1)
                last.then_inc(logits_done, 1)

            with pe.Fori(0, B // 2) as i:
                transposes(i * 2, 0)
                transposes(i * 2 + 1, 1)
                logits(i * 2, 0)
                logits(i * 2 + 1, 1)
            pe.wait_ge(chosen, 1)
            nc.tensor.matmul(ps_w[:], c["before"][:], M[:], start=True, stop=False)
            for t in range(NT - 1):
                last = nc.tensor.matmul(ps_w[:, t + 1:], c["ones"][:], M[:, t:t + 1].broadcast_to([P, NT - 1 - t, E]),
                                        start=False, stop=t == NT - 2)
            last.then_inc(counted, 1)
            if l == 0:
                for t in range(NT):
                    last = nc.tensor.matmul(ps_c[:], c["ones"][:], M[:, t], start=t == 0, stop=t == NT - 1)
                last.then_inc(counted, 1)

        @block.scalar
        def _(act):
            act.sem_inc(xt_copied, 2)
            act.sem_inc(logits_done, 2)

            def copy(b, u):
                act.wait_ge(xt_done, b + 3)
                act.wait_ge(logits_done, b + 1)
                if l == 1:
                    act.wait_ge(xt_kept, b + 1)
                nc.scalar.activation(xnt[u][:], ps_t[u][:], ACT.Copy).then_inc(xt_copied, 1)

            with act.Fori(0, B // 2) as i:
                copy(i * 2, 0)
                copy(i * 2 + 1, 1)
            act.wait_ge(shifted, 1)
            nc.scalar.activation(ex[:], ex[:], ACT.Exp).then_inc(exp_done, 1)

        @block.vector
        def _(dve):
            for t in range(NT):
                nc.vector.bn_aggr(mv[:, t], c["stats"][:, t]).then_inc(stats_done, 1)
            dve.wait_ge(stats_done, NT)
            nc.vector.tensor_scalar(var[:], mv[:, :, 1], EPS, None, ALU.add).then_inc(var_done, 1)
            dve.wait_ge(rstd_done, 1)
            with dve.Fori(0, B // 2) as i:
                for u in (0, 1):
                    b = i * 2 + u
                    dve.wait_ge(xt_done, b + 1)
                    dve.wait_ge(xn_kept, b + 1)
                    for t in range(TB):
                        tile = b * TB + t
                        ins = nc.vector.tensor_scalar(xn[u][:, t], X[:, bass.ds(tile, 1), :].rearrange("p o d -> p (o d)"),
                                                      mv[:, bass.ds(tile, 1), 0], rstd[:, bass.ds(tile, 1)],
                                                      ALU.subtract, ALU.mult)
                    ins.then_inc(xn_done, 1)

            done = [0]

            def then(ins):
                ins.then_inc(step, 1)
                done[0] += 1
                dve.wait_ge(step, done[0])

            def over(v, n):
                return v.unsqueeze(2).broadcast_to([P, NT, n])

            dve.wait_ge(logits_done, B + 2)
            then(nc.vector.tensor_reduce(top[:], ps_l[:], AX.X, ALU.max))
            nc.vector.tensor_tensor(ex[:], ps_l[:], over(top[:], E), ALU.subtract).then_inc(shifted, 1)
            dve.wait_ge(exp_done, 1)
            then(nc.vector.tensor_reduce(total[:], ex[:], AX.X, ALU.add))
            then(nc.vector.reciprocal(total[:], total[:]))
            then(nc.vector.tensor_tensor(prob[:], ex[:], over(total[:], E), ALU.mult))
            source = prob
            if l == 1:
                then(nc.vector.tensor_reduce(gmax[:], prob[:].rearrange("p t (g e) -> p t g e", g=G1), AX.X, ALU.max))
                for t in range(NT):
                    ins = nc.vector.max(g8[:, t], gmax[:, t])
                then(ins)
                for t in range(NT):
                    ins = nc.vector.max_index(gidx[:, t], g8[:, t], gmax[:, t])
                then(ins)
                then(nc.vector.tensor_copy(gidxf[:], gidx[:]))
                for t in range(NT):
                    ins = nc.vector.tensor_tensor(same[:, t], gidxf[:, t, 0:LG1].unsqueeze(1).broadcast_to([P, G1, LG1]),
                                                  c["count"][:, 0:G1].unsqueeze(2).broadcast_to([P, G1, LG1]), ALU.is_equal)
                then(ins)
                then(nc.vector.tensor_reduce(keep[:], same[:], AX.X, ALU.add))
                then(nc.vector.tensor_scalar(drop[:], keep[:], -1.0, None, ALU.add))
                for t in range(NT):
                    ins = nc.vector.tensor_tensor(kept[:, t].rearrange("p (g e) -> p g e", g=G1),
                                                  prob[:, t].rearrange("p (g e) -> p g e", g=G1),
                                                  keep[:, t].unsqueeze(2).broadcast_to([P, G1, GE1]), ALU.mult)
                then(ins)
                for t in range(NT):
                    ins = nc.vector.tensor_tensor(kept[:, t].rearrange("p (g e) -> p g e", g=G1),
                                                  kept[:, t].rearrange("p (g e) -> p g e", g=G1),
                                                  drop[:, t].unsqueeze(2).broadcast_to([P, G1, GE1]), ALU.add)
                then(ins)
                source = kept
            for t in range(NT):
                ins = nc.vector.max(W[:, t], source[:, t])
            then(ins)
            for t in range(NT):
                ins = nc.vector.max_index(idx[:, t], W[:, t], source[:, t])
            then(ins)
            then(nc.vector.tensor_copy(idxf[:], idx[:]))
            for k in range(K):
                ins = nc.vector.tensor_tensor(hot[k][:], over(idxf[:, :, k], E),
                                              c["count"][:, 0:E].unsqueeze(1).broadcast_to([P, NT, E]), ALU.is_equal)
            then(ins)
            then(nc.vector.tensor_tensor(picked[:], hot[0][:], hot[1][:], ALU.add))
            for k in range(2, K - 1):
                then(nc.vector.tensor_tensor(picked[:], picked[:], hot[k][:], ALU.add))
            if K == 2:
                nc.vector.tensor_copy(M[:], picked[:]).then_inc(chosen, 1)
            else:
                nc.vector.tensor_tensor(M[:], picked[:], hot[K - 1][:], ALU.add).then_inc(chosen, 1)
            then(nc.vector.tensor_reduce(total[:], W[:, :, 0:K], AX.X, ALU.add))
            if l == 1:
                then(nc.vector.tensor_scalar(total[:], total[:], 1e-9, None, ALU.add))
            then(nc.vector.reciprocal(total[:], total[:]))
            then(nc.vector.tensor_tensor(W[:, :, 0:K], W[:, :, 0:K], over(total[:], K), ALU.mult))
            dve.wait_ge(counted, 2 if l == 0 else 1)
            if l == 0:
                then(nc.vector.tensor_scalar(cnt_i[:], ps_c[:], float(P - 1), None, ALU.add))
                then(nc.vector.tensor_scalar(cnt_i[:], cnt_i[:], 7, None, ALU.arith_shift_right))
                then(nc.vector.tensor_copy(tiles[:], cnt_i[:]))
                then(nc.vector.tensor_copy(ends[:, 0:1], tiles[:, 0:1]))
                for e in range(1, E):
                    then(nc.vector.tensor_tensor(ends[:, e:e + 1], ends[:, e - 1:e], tiles[:, e:e + 1], ALU.add))
                then(nc.vector.tensor_tensor(base[:], ends[:], tiles[:], ALU.subtract))
                then(nc.vector.tensor_scalar(base[:], base[:], float(P), None, ALU.mult))
                then(nc.vector.tensor_tensor(where[:], ps_w[:], base[:].unsqueeze(1).broadcast_to([P, NT, E]), ALU.add))
                then(nc.vector.tensor_tensor(past[:], c["count"][:].unsqueeze(2).broadcast_to([P, TILES0, E]),
                                             ends[:].unsqueeze(1).broadcast_to([P, TILES0, E]), ALU.is_ge))
                then(nc.vector.tensor_reduce(te[:], past[:], AX.X, ALU.add))
                then(nc.vector.tensor_scalar(TE[:], te[:], float(E - 1), None, ALU.min))
            else:
                then(nc.vector.tensor_copy(where[:], ps_w[:]))
            for k in range(K):
                then(nc.vector.tensor_tensor(picked[:], where[:], hot[k][:], ALU.mult))
                if l == 0:
                    then(nc.vector.tensor_reduce(slotf[:, k], picked[:], AX.X, ALU.add))
                    nc.vector.tensor_copy(SLOT[:, k], slotf[:, k]).then_inc(slots_done, 1)
                else:
                    then(nc.vector.tensor_reduce(pos[:], picked[:], AX.X, ALU.add))
                    then(nc.vector.tensor_scalar(fits[:], pos[:], float(CAP), None, ALU.is_lt))
                    then(nc.vector.tensor_scalar(over_cap[:], pos[:], float(CAP), float(SLOTS1), ALU.is_ge, ALU.mult))
                    then(nc.vector.scalar_tensor_tensor(slotf[:, k], idxf[:, :, k], float(CAP), pos[:], ALU.mult, ALU.add))
                    then(nc.vector.tensor_tensor(slotf[:, k], slotf[:, k], over_cap[:], ALU.add))
                    then(nc.vector.tensor_tensor(W[:, :, k], W[:, :, k], fits[:], ALU.mult))
                    then(nc.vector.tensor_scalar(c["slot_read"][:, k], slotf[:, k], float(SLOTS1 - 1), None, ALU.min))
                    nc.vector.tensor_copy(SLOT[:, k], slotf[:, k]).then_inc(slots_done, 1)
            dve.wait_ge(slots_done, K)
    psum.close()


def scatter_rows(p, c, l, K, pool, scattered):
    table = c[f"slots_in{l}"]
    for k in range(K):
        for t in range(NT):
            p.nc.gpsimd.indirect_dma_start(table, bass.IndirectOffsetOnAxis(ap=c["slot"][:, k, t:t + 1], axis=0),
                                           c["xn"][:, t, :], None, bounds_check=table.shape[0] - 1,
                                           oob_is_err=False).then_inc(scattered, 16)


def experts_first(p, c):
    nc = p.nc
    W1, W2, TE = c["w1"], c["w2"], c["tile_expert"]
    start = p.top
    B1, G, BB = (p.sb(f"m0_{n}", [P, E0, H0], fp32) for n in ("b1b", "ln1_gb", "ln1_bb"))
    B2 = p.sb("m0_b2b", [P, E0, D], fp32)
    NB = 4
    xg = [p.sb(f"xg{u}", [P, D], fp32) for u in range(NB)]
    xt = [p.sb(f"xgt{u}", [P, KT, P], fp32) for u in (0, 1)]
    hs = [p.sb(f"hs{u}", [P, H0], fp32) for u in range(NB)]
    gs = [p.sb(f"gs{u}", [P, H0], fp32) for u in (0, 1)]
    ht = [p.sb(f"ht{u}", [P, HT0, P], fp32) for u in (0, 1)]
    ys = [p.sb(f"ys{u}", [P, D], fp32) for u in range(NB)]
    st = p.sb("h_stats", [P, NB, 6], fp32)
    mv = p.sb("h_mean_var", [P, NB, 2], fp32)
    ve = p.sb("h_var", [P, NB], fp32)
    hold = p.sb("hold", [1, 1], fp32)
    rs = p.sb("h_rstd", [P, NB], fp32)
    p.top = start
    psum = ExitStack()
    ps_x, ps_h, ps_t, ps_y = ([psum.enter_context(nc.psum_tensor(f"ps_m0{n}{u}", [P, 512], fp32)) for u in (0, 1)]
                              for n in ("xg", "h", "ht", "y"))
    table_loaded, scattered = p.sem("tables_loaded"), p.pool_dma_sem("scattered0")
    x_loaded = [p.sem(f"xg_loaded{u}") for u in range(NB)]
    y_stored = [p.sem(f"yg_stored{u}") for u in range(NB)]
    x_turned, x_copied = p.sem("xg_turned"), p.sem("xg_copied")
    h_made, h_biased, h_stats = p.sem("h_made"), p.sem("h_biased"), p.sem("h_stats_done")
    h_var, h_rstd, h_normed = p.sem("h_var_done"), p.sem("h_rstd_done"), p.sem("h_normed")
    h_scaled, h_gelu = p.sem("h_scaled"), p.sem("h_gelu")
    h_turned, h_copied = p.sem("h_turned"), p.sem("h_copied")
    y_made, y_biased = p.sem("yg_made"), p.sem("yg_biased")
    LAG_UP, LAG_NORM, LAG_GELU, LAG_DOWN, LAG_STORE = 1, 2, 3, 4, 5

    with nc.Block() as block:
        @block.sync
        def _(sp):
            d = p.dram
            for buf, n, w in ((B1, "b1", H0), (G, "ln1_g", H0), (BB, "ln1_b", H0), (B2, "b2", D)):
                sp.dma_start(buf[:].rearrange("p e h -> p (e h)"), across_partitions(d["m0_" + n], E0 * w))\
                    .then_inc(table_loaded, 16)
            sp.wait_ge(scattered, 16 * K0 * NT)

            def load(j, u):
                sp.wait_ge(x_turned, j + 1)
                sp.dma_start(xg[u][:], c["slots_in0"][bass.ds(j * P, P), :]).then_inc(x_loaded[u], 16)

            in_steps(sp, TILES0, [(0, load)], NB)
            for u in range(NB):
                sp.wait_ge(y_stored[u], 16 * (TILES0 // NB + 1))

        @block.tensor
        def _(pe):
            pe.sem_inc(x_turned, NB)
            pe.sem_inc(h_turned, 2)
            pe.sem_inc(h_made, 2)
            pe.sem_inc(y_made, 2)

            def turn_x(j, u):
                pe.wait_ge(x_loaded[u], use_of(j, u, NB) * 16 + 16)
                pe.wait_ge(x_copied, j + 1)
                for k in range(KT):
                    last = nc.tensor.transpose(ps_x[u % 2][:, k * P:(k + 1) * P], xg[u][:, k * P:(k + 1) * P], c["ident"][:])
                last.then_inc(x_turned, 1)

            def up(j, u):
                e = pe.value_load(TE[0:1, bass.ds(j, 1)], min_val=0, max_val=E0 - 1)
                pe.wait_ge(x_copied, j + 3)
                pe.wait_ge(h_biased, j + 1)
                for k in range(KT):
                    last = nc.tensor.matmul(ps_h[u % 2][:], xt[u % 2][:, k], W1[:, bass.ds(e, 1), k].rearrange("p o h -> p (o h)"),
                                            start=k == 0, stop=k == KT - 1)
                last.then_inc(h_made, 1)

            def turn_h(j, u):
                pe.wait_ge(h_gelu, j + 1 + NB)
                pe.wait_ge(h_copied, j + 1)
                for k in range(HT0):
                    last = nc.tensor.transpose(ps_t[u % 2][:, k * P:(k + 1) * P], gs[u % 2][:, k * P:(k + 1) * P], c["ident"][:])
                last.then_inc(h_turned, 1)

            def down(j, u):
                e = pe.value_load(TE[0:1, bass.ds(j, 1)], min_val=0, max_val=E0 - 1)
                pe.wait_ge(h_copied, j + 3)
                pe.wait_ge(y_biased, j + 1)
                for k in range(HT0):
                    last = nc.tensor.matmul(ps_y[u % 2][:, 0:D], ht[u % 2][:, k], W2[:, bass.ds(e, 1), k].rearrange("p o h -> p (o h)"),
                                            start=k == 0, stop=k == HT0 - 1)
                last.then_inc(y_made, 1)

            in_steps(pe, TILES0, [(0, turn_x), (LAG_DOWN, turn_h), (LAG_UP, up), (LAG_DOWN, down)], NB)

        @block.scalar
        def _(act):
            act.sem_inc(x_copied, 2)
            act.sem_inc(h_gelu, NB)
            act.sem_inc(h_copied, 2)

            def copy_x(j, u):
                act.wait_ge(x_turned, j + 1 + NB)
                act.wait_ge(h_made, j + 1)
                nc.scalar.activation(xt[u % 2][:].rearrange("p k t -> p (k t)"), ps_x[u % 2][:, 0:D], ACT.Copy).then_inc(x_copied, 1)

            def gelu(j, u):
                act.wait_ge(h_scaled, j * 2 + 2)
                act.wait_ge(h_turned, j + 1)
                nc.scalar.activation(gs[u % 2][:], hs[u][:], ACT.Gelu).then_inc(h_gelu, 1)

            def copy_h(j, u):
                act.wait_ge(h_turned, j + 3)
                act.wait_ge(y_made, j + 1)
                nc.scalar.activation(ht[u % 2][:].rearrange("p k t -> p (k t)"), ps_t[u % 2][:], ACT.Copy).then_inc(h_copied, 1)

            def store(j, u):
                act.wait_ge(y_biased, j + 3)
                act.dma_start(c["slots_out0"][bass.ds(j * P, P), :], ys[u][:]).then_inc(y_stored[u], 16)

            for u in range(NB):
                act.sem_inc(y_stored[u], 16)
            in_steps(act, TILES0, [(0, copy_x), (LAG_DOWN, copy_h), (LAG_GELU, gelu), (LAG_STORE, store)], NB)

        @block.vector
        def _(dve):
            dve.wait_ge(table_loaded, 64)
            dve.sem_inc(h_biased, 2)
            dve.sem_inc(y_biased, 2)

            def stats(j, u):
                e = dve.value_load(TE[0:1, bass.ds(j, 1)], min_val=0, max_val=E0 - 1)
                dve.wait_ge(h_made, j + 3)
                dve.wait_ge(h_gelu, j + 1)
                nc.vector.tensor_tensor(hs[u][:], ps_h[u % 2][:], B1[:, bass.ds(e, 1), :].rearrange("p o h -> p (o h)"),
                                        ALU.add).then_inc(h_biased, 1)
                dve.wait_ge(h_biased, j + 3)
                nc.vector.bn_stats(st[:, u], hs[u][:]).then_inc(h_stats, 1)
                dve.wait_ge(h_stats, j * 2 + 1)
                nc.vector.memset(hold[:], 0.0)
                nc.vector.bn_aggr(mv[:, u], st[:, u]).then_inc(h_stats, 1)
                dve.wait_ge(h_stats, j * 2 + 2)
                nc.vector.tensor_scalar(ve[:, u:u + 1], mv[:, u, 1:2], EPS, None, ALU.add).then_inc(h_var, 1)

            def norm(j, u):
                dve.wait_ge(h_rstd, j + 1)
                nc.vector.tensor_scalar(hs[u][:], hs[u][:], mv[:, u, 0:1], rs[:, u:u + 1], ALU.subtract, ALU.mult)\
                    .then_inc(h_normed, 1)

            def bias_y(j, u):
                e = dve.value_load(TE[0:1, bass.ds(j, 1)], min_val=0, max_val=E0 - 1)
                dve.wait_ge(y_made, j + 3)
                dve.wait_ge(y_stored[u], use_of(j, u, NB) * 16 + 16)
                nc.vector.tensor_tensor(ys[u][:], ps_y[u % 2][:, 0:D], B2[:, bass.ds(e, 1), :].rearrange("p o h -> p (o h)"),
                                        ALU.add).then_inc(y_biased, 1)

            in_steps(dve, TILES0, [(LAG_NORM, norm), (LAG_UP, stats), (LAG_DOWN, bias_y)], NB)

        @block.gpsimd
        def _(pool):
            scatter_rows(p, c, 0, K0, pool, scattered)
            pool.wait_ge(table_loaded, 64)

            def inverse(j, u):
                pool.wait_ge(h_var, j + 1)
                nc.gpsimd.tensor_tensor(rs[:, u:u + 1], ve[:, u:u + 1], c["minus_half"][:, 0:1], ALU.pow).then_inc(h_rstd, 1)

            def scale(j, u):
                e = pool.value_load(TE[0:1, bass.ds(j, 1)], min_val=0, max_val=E0 - 1)
                pool.wait_ge(h_normed, j + 1)
                nc.gpsimd.tensor_tensor(hs[u][:], hs[u][:], G[:, bass.ds(e, 1), :].rearrange("p o h -> p (o h)"), ALU.mult)\
                    .then_inc(h_scaled, 1)
                pool.wait_ge(h_scaled, j * 2 + 1)
                nc.gpsimd.tensor_tensor(hs[u][:], hs[u][:], BB[:, bass.ds(e, 1), :].rearrange("p o h -> p (o h)"), ALU.add)\
                    .then_inc(h_scaled, 1)

            in_steps(pool, TILES0, [(LAG_NORM, scale), (LAG_UP, inverse)], NB)
    psum.close()


def use_of(j, u, buffers=2):
    return (j - u) // buffers


def combine_first(p, c):
    nc = p.nc
    X, XN, W, SLOT = c["x"], c["xn"], c["weight"], c["slot"]
    start = p.top
    NB = 4
    NF = 8
    LAG_POW, LAG_NORM = 3, 5
    yk = [p.sb(f"y_rows{n}", [P, K0, D], fp32) for n in range(NB)]
    f = [p.sb(f"ffn{n}", [P, D], fp32) for n in range(NF)]
    gb = [p.sb(f"m0_{n}", [P, D], fp32) for n in ("ln_gb", "ln_bb")]
    st = p.sb("f_stats", [P, NF, 6], fp32)
    mv = p.sb("f_mean_var", [P, NF, 2], fp32)
    ve = p.sb("f_var", [P, NF], fp32)
    rs = p.sb("f_rstd", [P, NF], fp32)
    p.top = start
    loaded = p.sem("ln_loaded")
    gathered = [p.pool_dma_sem(f"y_gathered{n}") for n in range(NB)]
    first, used = p.sem("y_first_used"), p.sem("y_rows_used")
    stats_done, aggregated, var_done, rstd_done = (p.sem("f_" + n) for n in ("stats_done", "aggregated", "var_done", "rstd_done"))
    normed, scaled, added = p.sem("f_normed"), p.sem("f_scaled"), p.sem("f_added")
    done, done_stats = p.sem("x_mixture_added"), p.sem("x_new_stats")
    with nc.Block() as block:
        @block.sync
        def _(sp):
            for buf, n in zip(gb, ("ln_g", "ln_b")):
                sp.dma_start(buf[:], across_partitions(p.dram["m0_" + n], D)).then_inc(loaded, 16)

        @block.gpsimd
        def _(pool):
            table = c["slots_out0"]
            for t in range(NT + LAG_POW):
                if t < NT:
                    if t >= NB:
                        pool.wait_ge(used, t - NB + 1)
                    for k in range(K0):
                        nc.gpsimd.indirect_dma_start(yk[t % NB][:, k], None, table,
                                                     bass.IndirectOffsetOnAxis(ap=SLOT[:, k, t:t + 1], axis=0))\
                            .then_inc(gathered[t % NB], 16)
                if t >= LAG_POW:
                    u = (t - LAG_POW) % NF
                    pool.wait_ge(var_done, t - LAG_POW + 1)
                    nc.gpsimd.tensor_tensor(rs[:, u:u + 1], ve[:, u:u + 1], c["minus_half"][:, 0:1], ALU.pow)\
                        .then_inc(rstd_done, 1)

        @block.vector
        def _(dve):
            dve.wait_ge(loaded, 32)
            def weigh(t):
                dve.wait_ge(gathered[t % NB], 16 * K0 * (t // NB + 1))
                nc.vector.scalar_tensor_tensor(f[t % NF][:], yk[t % NB][:, 0], W[:, t, 0:1], XN[:, t], ALU.mult, ALU.add)\
                    .then_inc(first, 1)

            def weigh_second(t):
                dve.wait_ge(first, t + 1)
                nc.vector.scalar_tensor_tensor(f[t % NF][:], yk[t % NB][:, 1], W[:, t, 1:2], f[t % NF][:], ALU.mult, ALU.add)\
                    .then_inc(used, 1)

            def stats(t):
                dve.wait_ge(used, t + 1)
                nc.vector.bn_stats(st[:, t % NF], f[t % NF][:]).then_inc(stats_done, 1)

            def aggregate(t):
                dve.wait_ge(stats_done, t + 1)
                nc.vector.bn_aggr(mv[:, t % NF], st[:, t % NF]).then_inc(aggregated, 1)

            def variance(t):
                dve.wait_ge(aggregated, t + 1)
                nc.vector.tensor_scalar(ve[:, t % NF:t % NF + 1], mv[:, t % NF, 1:2], EPS, None, ALU.add).then_inc(var_done, 1)

            def norm(t):
                dve.wait_ge(rstd_done, t + 1)
                nc.vector.tensor_scalar(f[t % NF][:], f[t % NF][:], mv[:, t % NF, 0:1], rs[:, t % NF:t % NF + 1],
                                        ALU.subtract, ALU.mult).then_inc(normed, 1)

            def scale(t):
                dve.wait_ge(normed, t + 1)
                nc.vector.tensor_tensor(f[t % NF][:], f[t % NF][:], gb[0][:], ALU.mult).then_inc(scaled, 1)

            def add(t):
                dve.wait_ge(scaled, t + 1)
                nc.vector.tensor_tensor(f[t % NF][:], f[t % NF][:], X[:, t], ALU.add).then_inc(added, 1)

            def shift(t):
                dve.wait_ge(added, t + 1)
                nc.vector.tensor_tensor(X[:, t], f[t % NF][:], gb[1][:], ALU.add).then_inc(done, 1)

            def new_stats(t):
                dve.wait_ge(done, t + 1)
                nc.vector.bn_stats(c["stats"][:, t], X[:, t]).then_inc(done_stats, 1)

            stages = [(0, weigh), (LAG_NORM, norm), (0, weigh_second), (LAG_NORM, scale), (1, stats), (LAG_NORM, add), (1, aggregate),
                      (LAG_NORM, shift), (1, variance), (LAG_NORM, new_stats)]
            for s in range(NT + LAG_NORM):
                for lag, f_ in stages:
                    if 0 <= s - lag < NT:
                        f_(s - lag)
            dve.wait_ge(done_stats, NT)


def experts_second(p, c):
    nc, d = p.nc, p.dram
    X, XNT = c["x"], c["xnt"]
    NS = len(SLOT_TILES)
    FULL = sum(n == P for _, n in SLOT_TILES)
    LAST = SLOT_TILES[-1][1] % P
    start = p.top
    sw = {n: p.sb("m1_" + n, [P, KT, D], fp32) for n in ("sw1", "sw3", "sw2")}
    NB = 4
    w1, w3, w2 = ([p.sb(f"m1_{n}{u}", [P, KT, D], fp32) for u in range(NB)] for n in ("w1", "w3", "w2"))
    xe = [p.sb(f"xe{u}", [P, NS, D], fp32) for u in range(NB)]
    xt = [p.sb(f"xet{u}", [P, KT, CAP], fp32) for u in (0, 1)]
    sl = [p.sb(f"silu{u}", [P, HT1, CAP], fp32) for u in (0, 1)]
    gt = [p.sb(f"gated{u}", [P, HT1, CAP], fp32) for u in (0, 1)]
    ys = [p.sb(f"ye{u}", [P, NS, D], fp32) for u in range(NB)]
    p.top = start
    psum = ExitStack()
    ps_x, ps_a, ps_b, ps_y = (psum.enter_context(nc.psum_tensor(f"ps_m1{n}", [P, 2, 512], fp32)) for n in "xaby")
    scattered, shared_loaded = p.pool_dma_sem("scattered1"), p.sem("shared_w_loaded")
    up_loaded = [p.sem(f"w13_loaded{u}") for u in range(NB)]
    down_loaded = [p.sem(f"w2_loaded{u}") for u in range(NB)]
    x_loaded = [p.sem(f"xe_loaded{u}") for u in range(NB)]
    y_stored = [p.sem(f"ye_stored{u}") for u in range(NB)]
    x_turned, x_copied = p.sem("xe_turned"), p.sem("xe_copied")
    up_made, silu_done, gated, down_made, y_copied = (p.sem("m1_" + n) for n in
                                                      ("up_made", "silu_done", "gated", "down_made", "y_copied"))

    with nc.Block() as block:
        @block.sync
        def _(sp):
            for n in ("sw1", "sw3", "sw2"):
                sp.dma_start(sw[n][:], d["m1_" + n].rearrange("(k p) h -> p k h", p=P)).then_inc(shared_loaded, 16)
            def load_weights(e, u):
                sp.wait_ge(up_made, (e + B + 3 - NB) * HT1)
                for buf, n in ((w1, "w1"), (w3, "w3")):
                    sp.dma_start(buf[u][:], d["m1_" + n][bass.ds(e, 1)].rearrange("o (k p) h -> p (o k) h", p=P))\
                        .then_inc(up_loaded[u], 16)
                sp.wait_ge(down_made, e + B + 3 - NB)
                sp.dma_start(w2[u][:], d["m1_w2"][bass.ds(e, 1)].rearrange("o (k p) h -> p (o k) h", p=P))\
                    .then_inc(down_loaded[u], 16)

            def load_rows(e, u):
                if isinstance(e, int) and e == 0:
                    sp.wait_ge(scattered, 16 * K1 * NT)
                sp.wait_ge(x_turned, e + 1)
                sp.dma_start(xe[u][:, 0:FULL], c["slots_in1"][bass.ds(e * CAP, FULL * P), :].rearrange("(s p) d -> p s d", p=P))\
                    .then_inc(x_loaded[u], 16)
                sp.dma_start(xe[u][0:LAST, FULL], c["slots_in1"][bass.ds(e * CAP + FULL * P, LAST), :])\
                    .then_inc(x_loaded[u], 16)

            in_steps(sp, E1, [(1, load_rows), (0, load_weights)], NB)
            for u in range(NB):
                sp.wait_ge(y_stored[u], 32 * (E1 // NB + 1))

        @block.gpsimd
        def _(pool):
            scatter_rows(p, c, 1, K1, pool, scattered)

        @block.tensor
        def _(pe):
            pe.sem_inc(up_made, 2 * HT1)
            pe.sem_inc(down_made, 2)
            pe.sem_inc(x_turned, NB)

            def up(item, wa, wb, rhs, n):
                for m in range(HT1):
                    pe.wait_ge(gated, (item + 2) * HT1 + m + 1 - HT1)
                    for ps, w in ((ps_a, wa), (ps_b, wb)):
                        for k in range(KT):
                            last = nc.tensor.matmul(ps[:, m, 0:n], w[:, k, m * P:(m + 1) * P], rhs(k),
                                                    start=k == 0, stop=k == KT - 1)
                    last.then_inc(up_made, 1)

            def down(item, u, w, tiles):
                pe.wait_ge(gated, (item + 3) * HT1)
                pe.wait_ge(y_copied, item + 2)
                for s, (at, n) in enumerate(tiles):
                    for k in range(HT1):
                        last = nc.tensor.matmul(ps_y[0:n, s // 2, s % 2 * D:s % 2 * D + D], gt[u][:, k, at:at + n], w[:, k],
                                                start=k == 0, stop=k == HT1 - 1)
                last.then_inc(down_made, 1)

            pe.wait_ge(shared_loaded, 48)
            in_steps(pe, B, [
                (0, lambda b, u: up(b, sw["sw1"], sw["sw3"], lambda k: XNT[:, k, bass.ds(b * S, S)], S)),
                (1, lambda b, u: down(b, u, sw["sw2"], [(0, P), (P, P)]))])

            def turn(e, u):
                pe.wait_ge(x_loaded[u], use_of(e, u, NB) * 32 + 32)
                pe.wait_ge(x_copied, e + 1)
                for k in range(KT):
                    for s, (at, n) in enumerate(SLOT_TILES):
                        last = nc.tensor.transpose(ps_x[:, k, at:at + n], xe[u][0:n, s, k * P:(k + 1) * P],
                                                   c["ident"][0:n, 0:n])
                last.then_inc(x_turned, 1)

            def up_expert(e, u):
                pe.wait_ge(x_copied, e + 2)
                pe.wait_ge(up_loaded[u], use_of(e, u, NB) * 32 + 32)
                up(e + B, w1[u], w3[u], lambda k: xt[u % 2][:, k], CAP)

            def down_expert(e, u):
                pe.wait_ge(down_loaded[u], use_of(e, u, NB) * 16 + 16)
                down(e + B, u % 2, w2[u], SLOT_TILES)

            in_steps(pe, E1, [(0, turn), (1, up_expert), (2, down_expert)], NB)

        @block.scalar
        def _(act):
            act.sem_inc(x_copied, 1)

            def silu(item, u, n):
                for m in range(HT1):
                    act.wait_ge(up_made, (item + 2) * HT1 + m + 1)
                    act.wait_ge(gated, item * HT1 + m + 1)
                    nc.scalar.activation(sl[u][:, m, 0:n], ps_a[:, m, 0:n], ACT.Silu).then_inc(silu_done, 1)

            in_steps(act, B, [(0, lambda b, u: silu(b, u, S))])

            def copy_x(e, u):
                act.wait_ge(x_turned, e + 1 + NB)
                act.wait_ge(up_made, (e + B + 1) * HT1)
                nc.scalar.activation(xt[u % 2][:], ps_x[:, :, 0:CAP], ACT.Copy).then_inc(x_copied, 1)

            def store(e, u):
                act.wait_ge(y_copied, e + 1 + B + 2)
                act.dma_start(c["slots_out1"][bass.ds(e * CAP, FULL * P), :].rearrange("(s p) d -> p s d", p=P), ys[u][:, 0:FULL])\
                    .then_inc(y_stored[u], 16)
                act.dma_start(c["slots_out1"][bass.ds(e * CAP + FULL * P, LAST), :], ys[u][0:LAST, FULL])\
                    .then_inc(y_stored[u], 16)

            for u in range(NB):
                act.sem_inc(y_stored[u], 32)
            in_steps(act, E1, [(0, copy_x), (1, lambda e, u: silu(e + B, u % 2, CAP)), (3, store)], NB)

        @block.vector
        def _(dve):
            dve.sem_inc(gated, 2 * HT1)
            dve.sem_inc(y_copied, 2)

            def gate(item, u, n):
                dve.wait_ge(down_made, item + 1)
                for m in range(HT1):
                    dve.wait_ge(silu_done, item * HT1 + m + 1)
                    nc.vector.tensor_tensor(gt[u][:, m, 0:n], ps_b[:, m, 0:n], sl[u][:, m, 0:n], ALU.mult)\
                        .then_inc(gated, 1)

            def add_shared(b, u):
                dve.wait_ge(down_made, b + 3)
                at = X[:, bass.ds(b * TB, TB), :]
                nc.vector.tensor_tensor(at, ps_y[:, 0].rearrange("p (t d) -> p t d", t=TB), at, ALU.add).then_inc(y_copied, 1)

            in_steps(dve, B, [(0, lambda b, u: gate(b, u, S)), (1, add_shared)])

            def copy_y(e, u):
                dve.wait_ge(down_made, e + B + 3)
                dve.wait_ge(y_stored[u], use_of(e, u, NB) * 32 + 32)
                nc.vector.tensor_copy(ys[u][:, 0:FULL], ps_y[:, 0].rearrange("p (t d) -> p t d", t=FULL)).then_inc(y_half, 1)
                nc.vector.tensor_copy(ys[u][0:LAST, FULL], ps_y[0:LAST, 1, 0:D]).then_inc(y_copied, 1)

            y_half = p.sem("ye_first_copied")
            in_steps(dve, E1, [(1, lambda e, u: gate(e + B, u % 2, CAP)), (2, copy_y)], NB)
    psum.close()


def combine_second(p, c):
    nc = p.nc
    X, W, SLOT = c["x"], c["weight"], c["slot_read"]
    start = p.top
    NB = 4
    yk = [p.sb(f"z_rows{n}", [P, K1, D], fp32) for n in range(NB)]
    p.top = start
    gathered = [p.pool_dma_sem(f"z_gathered{n}") for n in range(NB)]
    added, done = p.sem("z_added"), p.sem("out_stored")
    out = p.dram["out"].rearrange("(t p) d -> t p d", p=P)
    with nc.Block() as block:
        @block.sync
        def _(sp):
            for t in range(NT):
                sp.wait_ge(added, K1 * (t + 1))
                sp.dma_start(out[t], X[:, t]).then_inc(done, 16)
            sp.wait_ge(done, 16 * NT)

        @block.gpsimd
        def _(pool):
            for t in range(NT):
                if t >= NB:
                    pool.wait_ge(added, K1 * (t - NB + 1))
                for k in range(K1):
                    nc.gpsimd.indirect_dma_start(yk[t % NB][:, k], None, c["slots_out1"],
                                                 bass.IndirectOffsetOnAxis(ap=SLOT[:, k, t:t + 1], axis=0))\
                        .then_inc(gathered[t % NB], 16)

        @block.vector
        def _(dve):
            for t in range(NT):
                n = t % NB
                dve.wait_ge(gathered[n], 16 * K1 * (t // NB + 1))
                for k in range(K1):
                    nc.vector.scalar_tensor_tensor(X[:, t], yk[n][:, k], W[:, t, k:k + 1], X[:, t], ALU.mult, ALU.add)\
                        .then_inc(added, 1)
                    dve.wait_ge(added, K1 * t + k + 1)


def prepare_mixtures(p, c):
    nc = p.nc
    c["w1"] = p.sb("m0_w1", [P, E0, KT, H0], fp32)
    c["w2"] = p.sb("m0_w2", [P, E0, HT0, D], fp32)
    for l, n in ((0, TILES0 * P), (1, SLOTS1)):
        c[f"slots_in{l}"] = p.scratch(f"slots_in{l}", [n, D], fp32)
        c[f"slots_out{l}"] = p.scratch(f"slots_out{l}", [n, D], fp32)
        c[f"filled{l}"] = p.pool_dma_sem(f"mixture_filled{l}")
    ROWS = 8

    def background(l):
        def run(pool):
            done = 0
            pieces = []
            if l == 0:
                for e in range(E0):
                    pieces.append((c["w1"][:, e], p.dram["m0_w1"][e].rearrange("(k p) h -> p k h", p=P)))
                    pieces.append((c["w2"][:, e], p.dram["m0_w2"][e].rearrange("(k p) h -> p k h", p=P)))
            rows = c[f"slots_in{l}"].rearrange("(p n) d -> p n d", p=P)
            for at in range(0, rows.shape[1], ROWS):
                pieces.append((rows[:, at:at + ROWS], c["zero_row"][:].unsqueeze(1).broadcast_to([P, ROWS, D])))
            for to, what in pieces:
                pool.dma_start(to, what).then_inc(c[f"filled{l}"], 16)
                done += 16
                pool.wait_ge(c[f"filled{l}"], done)
        return run
    return background


def program(nc, dram):
    p = Program(nc, dram)
    with p.lasting:
        c = load_constants(p)
        routing_constants(p, c)
        background = prepare_mixtures(p, c)
        keys_and_values(p, c)
        queries(p, c, 0)
        attention(p, c, 0, background(0))
        kept = p.top
        route(p, c, 0, E0, K0)
        experts_first(p, c)
        combine_first(p, c)
        p.top = kept
        p.renew_semaphores()
        queries(p, c, 1)
        attention(p, c, 1, background(1))
        route(p, c, 1, E1, K1)
        experts_second(p, c)
        combine_second(p, c)
        p.stack.close()


def laid_out(inputs):
    def w_t(w):
        return w.T.reshape(KT, P, -1).transpose(1, 0, 2)

    a = {}
    a["x"] = inputs["x"].reshape(N, D)
    a["ctx"] = inputs["ctx_1024"].transpose(0, 2, 1).reshape(B, KT, P, S).transpose(0, 2, 1, 3)
    mask = inputs["mask_1x1xSxS2_ik0"].reshape(S, S)
    a["mask_qk"] = mask.reshape(TB, P, S).transpose(1, 0, 2)
    a["mask_kq"] = mask.T.reshape(TB, P, S).transpose(1, 0, 2)
    for l, names in ((0, ("Wq", "Wk", "Wv", "Wo")), (1, ("Wq", "Wk", "Wv", "Wu"))):
        for n, w in zip("qkvo", names):
            a[f"w{n}{l}"] = w_t(inputs[f"L{l}_xattn_{w}"])
    for n in ("bq", "bk"):
        a[n + "0"] = inputs[f"L0_xattn_{n}"].reshape(KT, P).T
    a["bv0"], a["bo0"], a["bo1"] = inputs["L0_xattn_bv"], inputs["L0_xattn_bo"], inputs["L1_xattn_bu"]
    for n in ("gate_w", "w1", "b1", "ln1_g", "ln1_b", "w2", "b2", "ln_g", "ln_b"):
        a["m0_" + n] = inputs["L0_ffn_" + n]
    for n in ("w1", "w2", "w3", "sw1", "sw2", "sw3"):
        a["m1_" + n] = inputs["L1_ffn_" + n]
    a["m0_gate_w"] = a["m0_gate_w"].reshape(KT, P, E0).transpose(1, 0, 2)
    a["m1_gate_w"] = w_t(inputs["L1_ffn_wg"])
    return {n: np.ascontiguousarray(v) for n, v in a.items()}


def kernel(**inputs):
    import concourse.bacc as bacc
    from concourse.bass_utils import run_bass_kernel_spmd

    arrays = laid_out({n: np.asarray(v) for n, v in inputs.items()})
    nc = bacc.Bacc("TRN2", target_bir_lowering=False, num_devices=1)
    dram = {n: nc.dram_tensor(f"in_{n}", v.shape, mybir.dt.from_np(v.dtype), kind="ExternalInput").ap()
            for n, v in arrays.items()}
    dram["out"] = nc.dram_tensor("out_x", [N, D], fp32, kind="ExternalOutput").ap()
    program(nc, dram)
    result = run_bass_kernel_spmd(nc, [{f"in_{n}": v for n, v in arrays.items()}], core_ids=[0])
    return result.results[0]["out_x"].reshape(B, S, D)
```

```python
import numpy as np
import concourse.bass as bass
from concourse import mybir
from contextlib import ExitStack

fp32 = mybir.dt.float32
fp32r = mybir.dt.float32r
bf16 = mybir.dt.bfloat16
int32 = mybir.dt.int32
ALU = mybir.AluOpType
ACT = mybir.ActivationFunctionType
AX = mybir.AxisListType

P = 128
B, S, D = 8, 256, 256
N = B * S
NT = N // P
TB = S // P
KT = D // P
H, DH = 16, 16
HV = 32
HQ = P // HV
NEG = -float(2 ** 100)
EPS = 1e-5
ROW_MAX = 64
STACK = ROW_MAX + 2

E0, K0, H0 = 8, 2, 512
HT0 = H0 // P
CHOOSE = 10
TILES0 = N * K0 // P + E0 - 1 + 1
E1, K1, H1 = 32, 4, 256
G1, LG1 = 8, 4
GE1 = E1 // G1
HT1 = H1 // P
CAP = int(1.25 * N * K1 / E1)
SLOTS1 = E1 * CAP
SLOT_TILES = [(s, min(P, CAP - s)) for s in range(0, CAP, P)]


class Program:

    def __init__(self, nc, dram):
        self.nc = nc
        self.dram = dram
        self.sems = {}
        self.stack = ExitStack()
        self.lasting = ExitStack()
        self.top = 16640
        self.limit = 229344

    def sem(self, name):
        if name not in self.sems:
            self.sems[name] = self.stack.enter_context(self.nc.semaphore(name))
        return self.sems[name]

    def pool_dma_sem(self, name):
        return self.lasting.enter_context(self.nc.semaphore(name))

    def renew_semaphores(self):
        sems = list(self.sems.values())

        def clear(engine, n):
            for sem in sems[n::5]:
                engine.sem_clear(sem)

        with self.nc.Block() as block:
            @block.sync
            def _(sp):
                clear(sp, 0)

            @block.tensor
            def _(pe):
                clear(pe, 1)

            @block.scalar
            def _(act):
                clear(act, 2)

            @block.vector
            def _(dve):
                clear(dve, 3)

            @block.gpsimd
            def _(pool):
                clear(pool, 4)

        self.stack.close()
        self.sems = {}

    def sb(self, name, shape, dtype):
        size = int(np.prod(shape[1:])) * (2 if dtype == bf16 else 4)
        at = self.top
        self.top = (at + size + 31) // 32 * 32
        assert self.top <= self.limit, (name, self.top)
        return self.nc.alloc_sbuf_tensor_at(name, shape, dtype, offset=at)

    def scratch(self, name, shape, dtype):
        return self.nc.dram_tensor(name, shape, dtype, kind="Internal").ap()


def across_partitions(ap, n):
    return bass.AP(ap.tensor, ap.offset, [[0, P], [1, n]])


def load_constants(p):
    nc, d = p.nc, p.dram
    c = {}
    c["x"] = p.sb("x_res", [P, NT, D], fp32)
    for l in (0, 1):
        for w in ("q", "k", "v", "o"):
            c[f"w{w}{l}"] = p.sb(f"w{w}{l}", [P, KT, D], fp32)
    for n in ("bq0", "bk0"):
        c[n] = p.sb(n, [P, KT], fp32)
    for n in ("bv0", "bo0", "bo1"):
        c[n] = p.sb(n, [P, D], fp32)
    c["ident"] = p.sb("ident", [P, P], fp32)
    c["identb"] = p.sb("identb", [P, P], bf16)
    c["mask_qk"] = p.sb("mask_qk", [P, TB, S], bf16)
    c["mask_kq"] = p.sb("mask_kq", [P, TB, S], bf16)
    c["minus_half"] = p.sb("minus_half", [P, NT], fp32)
    c["zero_row"] = p.sb("zero_row", [P, D], fp32)
    c["stats"] = p.sb("x_stats", [P, NT, 6], fp32)
    c["kv_loaded"], c["x_loaded"], made = p.sem("kv_weights_loaded"), p.sem("x_loaded"), p.sem("constants_made")
    ident_zero = p.sem("identity_zeroed")
    with nc.Block() as block:
        @block.sync
        def _(sp):
            for w in ("k", "v"):
                sp.dma_start(c[f"w{w}0"][:], d[f"w{w}0"]).then_inc(c["kv_loaded"], 16)
            sp.dma_start(c["bk0"][:], d["bk0"]).then_inc(c["kv_loaded"], 16)
            sp.dma_start(c["bv0"][:], across_partitions(d["bv0"], D)).then_inc(c["kv_loaded"], 16)
            sp.dma_start(c["x"][:], d["x"].rearrange("(t p) d -> p t d", p=P)).then_inc(c["x_loaded"], 16)

        @block.gpsimd
        def _(pool):
            nc.gpsimd.memset(c["ident"][:], 0.0).then_inc(ident_zero, 1)
            nc.gpsimd.memset(c["identb"][:], 0.0).then_inc(ident_zero, 1)
            nc.gpsimd.memset(c["zero_row"][:], 0.0).then_inc(made, 1)
            pool.wait_ge(ident_zero, 2)
            for n in ("ident", "identb"):
                nc.gpsimd.affine_select(out=c[n][:], in_=c[n][:], compare_op=ALU.not_equal, fill=1.0, base=0,
                                        pattern=[[-1, P]], channel_multiplier=1).then_inc(made, 1)

        @block.vector
        def _(dve):
            nc.vector.memset(c["minus_half"][:], -0.5).then_inc(made, 1)
            dve.wait_ge(made, 4)
    return c


class KeysAndValues:
    STORES = 3 * 16

    def __init__(self, p, c, l):
        nc = self.nc = p.nc
        self.c, self.l, self.d = c, l, p.dram
        self.ctx = [p.sb(f"ctx{l}{u}", [P, KT, S], fp32) for u in (0, 1)]
        self.kk = [p.sb(f"k_parts{l}{u}", [P, 2, KT, S], fp32r) for u in (0, 1)]
        self.vv = [p.sb(f"v_ones{l}{u}", [P, TB, H, HV], fp32) for u in (0, 1)]
        self.psum = ExitStack()
        self.ps_k = [self.psum.enter_context(nc.psum_tensor(f"ps_k{l}{u}", [P, KT, S], fp32)) for u in (0, 1)]
        self.ps_v = [self.psum.enter_context(nc.psum_tensor(f"ps_v{l}{u}", [P, TB, D], fp32)) for u in (0, 1)]
        self.kd = c[f"kd{l}"] = p.scratch(f"kd{l}", [2, D, N], fp32)
        self.vd = c[f"vd{l}"] = p.scratch(f"vd{l}", [N, H * HV], fp32)
        self.ctx_loaded = [p.sem(f"ctx_loaded{l}{u}") for u in (0, 1)]
        self.projected = p.sem(f"kv_projected{l}")
        self.high_done = p.sem(f"k_high{l}")
        self.emptied = p.sem(f"kv_emptied{l}")
        self.stored = [p.sem(f"kv_stored{l}{u}") for u in (0, 1)]
        self.ones = p.sem(f"v_ones_set{l}")

    def begin_pe(self, pe):
        pe.sem_inc(self.projected, 4)

    def begin_act(self, act):
        for u in (0, 1):
            act.sem_inc(self.stored[u], self.STORES)

    def begin_dve(self, dve):
        for u in (0, 1):
            self.nc.vector.memset(self.vv[u][:, :, :, DH:DH + 1], 1.0).then_inc(self.ones, 1)
            self.nc.vector.memset(self.vv[u][:, :, :, DH + 1:HV], 0.0).then_inc(self.ones, 1)
        dve.wait_ge(self.ones, 4)
        dve.sem_inc(self.emptied, 4)

    def load(self, sp, b, u):
        sp.wait_ge(self.projected, b * 2 + 2)
        sp.dma_start(self.ctx[u][:], self.d["ctx"][bass.ds(b, 1)].rearrange("o p k t -> p (o k) t")).then_inc(self.ctx_loaded[u], 16)

    def store(self, sp, b, u):
        sp.wait_ge(self.emptied, b * 2 + 2 + 4)
        for part in (0, 1):
            sp.dma_start(self.kd[part, :, bass.ds(b * S, S)].rearrange("(m p) t -> p m t", p=P),
                         self.kk[u][:, part].bitcast(fp32)).then_inc(self.stored[u], 16)
        sp.dma_start(self.vd[bass.ds(b * S, S), :].rearrange("(t p) e -> p t e", p=P),
                     self.vv[u][:].rearrange("p t h e -> p t (h e)")).then_inc(self.stored[u], 16)

    def end(self, sp):
        for u in (0, 1):
            sp.wait_ge(self.stored[u], (B // 2 + 1) * self.STORES)

    def project(self, pe, b, u):
        nc, c, l, ctx = self.nc, self.c, self.l, self.ctx[u]
        pe.wait_ge(self.ctx_loaded[u], use_of(b, u) * 16 + 16)
        pe.wait_ge(self.emptied, b * 2 + 1)
        for m in range(KT):
            for k in range(KT):
                last = nc.tensor.matmul(self.ps_k[u][:, m], c[f"wk{l}"][:, k, m * P:(m + 1) * P], ctx[:, k],
                                        start=k == 0, stop=k == KT - 1)
        last.then_inc(self.projected, 1)
        pe.wait_ge(self.emptied, b * 2 + 2)
        for t in range(TB):
            for k in range(KT):
                last = nc.tensor.matmul(self.ps_v[u][:, t], ctx[:, k, t * P:(t + 1) * P], c[f"wv{l}"][:, k],
                                        start=k == 0, stop=k == KT - 1)
        last.then_inc(self.projected, 1)

    def high(self, act, b, u):
        nc, c = self.nc, self.c
        act.wait_ge(self.stored[u], (use_of(b, u) + 1) * self.STORES)
        act.wait_ge(self.projected, b * 2 + 1 + 4)
        for m in range(KT):
            if self.l == 0:
                ins = nc.scalar.activation(self.kk[u][:, 0, m], self.ps_k[u][:, m], ACT.Identity, bias=c["bk0"][:, m:m + 1])
            else:
                ins = nc.scalar.activation(self.kk[u][:, 0, m], self.ps_k[u][:, m], ACT.Copy)
        ins.then_inc(self.high_done, 1)

    def low(self, dve, b, u):
        nc, c = self.nc, self.c
        dve.wait_ge(self.stored[u], (use_of(b, u) + 1) * self.STORES)
        dve.wait_ge(self.high_done, b + 1)
        for m in range(KT):
            high = self.kk[u][:, 0, m].bitcast(fp32)
            if self.l == 0:
                ins = nc.vector.scalar_tensor_tensor(self.kk[u][:, 1, m], self.ps_k[u][:, m], c["bk0"][:, m:m + 1],
                                                     high, ALU.add, ALU.subtract)
            else:
                ins = nc.vector.tensor_tensor(self.kk[u][:, 1, m], self.ps_k[u][:, m], high, ALU.subtract)
        ins.then_inc(self.emptied, 1)
        dve.wait_ge(self.projected, b * 2 + 2 + 4)
        for t in range(TB):
            heads = self.ps_v[u][:, t].rearrange("p (h e) -> p h e", h=H)
            if self.l == 0:
                ins = nc.vector.tensor_tensor(self.vv[u][:, t, :, 0:DH], heads,
                                              c["bv0"][:].rearrange("p (h e) -> p h e", h=H), ALU.add)
            else:
                ins = nc.vector.tensor_copy(self.vv[u][:, t, :, 0:DH], heads)
        ins.then_inc(self.emptied, 1)


class Queries:

    def __init__(self, p, c, l):
        nc = self.nc = p.nc
        self.c, self.l, self.X = c, l, c["x"]
        self.mv = p.sb(f"mean_var{l}", [P, NT, 2], fp32)
        self.var = p.sb(f"var{l}", [P, NT], fp32)
        self.rstd = p.sb(f"rstd{l}", [P, NT], fp32)
        self.xn = [p.sb(f"xn{l}{u}", [P, TB, D], fp32) for u in (0, 1)]
        self.xnt = [p.sb(f"xnt{l}{u}", [P, KT, S], fp32) for u in (0, 1)]
        self.qq = [p.sb(f"q_parts{l}{u}", [P, 2, KT, S], fp32r) for u in (0, 1)]
        self.psum = ExitStack()
        self.ps_t = [self.psum.enter_context(nc.psum_tensor(f"ps_xt{l}{u}", [P, KT, S], fp32)) for u in (0, 1)]
        self.ps_q = [self.psum.enter_context(nc.psum_tensor(f"ps_q{l}{u}", [P, KT, S], fp32)) for u in (0, 1)]
        self.qd = c[f"qd{l}"] = p.scratch(f"qd{l}", [2, D, N], fp32)
        self.aggregated, self.tiles = p.sem(f"x_aggregated{l}"), 0
        self.var_done, self.rstd_done = p.sem(f"var_done{l}"), p.sem(f"rstd_done{l}")
        self.xn_done, self.xt_done, self.xt_copied = p.sem(f"xn_done{l}"), p.sem(f"xt_done{l}"), p.sem(f"xt_copied{l}")
        self.q_done, self.q_high, self.q_low = p.sem(f"q_done{l}"), p.sem(f"q_high{l}"), p.sem(f"q_low{l}")
        self.stored = [p.sem(f"q_stored{l}{u}") for u in (0, 1)]

    def aggregate(self, dve, tiles):
        for t in tiles:
            self.nc.vector.bn_aggr(self.mv[:, t], self.c["stats"][:, t]).then_inc(self.aggregated, 1)
            self.tiles += 1
        dve.wait_ge(self.aggregated, self.tiles)
        at = slice(tiles[0], tiles[-1] + 1)
        self.nc.vector.tensor_scalar(self.var[:, at], self.mv[:, at, 1], EPS, None, ALU.add).then_inc(self.var_done, 1)

    def invert(self, pool, n, tiles):
        pool.wait_ge(self.var_done, n)
        at = slice(tiles[0], tiles[-1] + 1)
        self.nc.gpsimd.tensor_tensor(self.rstd[:, at], self.var[:, at], self.c["minus_half"][:, at], ALU.pow)\
            .then_inc(self.rstd_done, 1)

    def norm(self, dve, b, u):
        dve.wait_ge(self.xt_done, b + 1)
        for t in range(TB):
            tile = b * TB + t
            ins = self.nc.vector.tensor_scalar(self.xn[u][:, t], self.X[:, bass.ds(tile, 1), :].rearrange("p o d -> p (o d)"),
                                               self.mv[:, bass.ds(tile, 1), 0], self.rstd[:, bass.ds(tile, 1)],
                                               ALU.subtract, ALU.mult)
        ins.then_inc(self.xn_done, 1)

    def low(self, dve, b, u):
        nc = self.nc
        dve.wait_ge(self.q_high, b + 1)
        for m in range(KT):
            high = self.qq[u][:, 0, m].bitcast(fp32)
            if self.l == 0:
                ins = nc.vector.scalar_tensor_tensor(self.qq[u][:, 1, m], self.ps_q[u][:, m], self.c["bq0"][:, m:m + 1],
                                                     high, ALU.add, ALU.subtract)
            else:
                ins = nc.vector.tensor_tensor(self.qq[u][:, 1, m], self.ps_q[u][:, m], high, ALU.subtract)
        ins.then_inc(self.q_low, 1)

    def begin_dve(self, dve):
        dve.sem_inc(self.q_low, 2)

    def begin_pe(self, pe):
        pe.sem_inc(self.xt_done, 2)
        pe.sem_inc(self.q_done, 2)

    def begin_act(self, act):
        act.sem_inc(self.xt_copied, 2)
        for u in (0, 1):
            act.sem_inc(self.stored[u], 32)

    def transposes(self, pe, b, u):
        pe.wait_ge(self.xn_done, b + 1)
        pe.wait_ge(self.xt_copied, b + 1)
        for t in range(TB):
            for k in range(KT):
                last = self.nc.tensor.transpose(self.ps_t[u][:, k, t * P:(t + 1) * P], self.xn[u][:, t, k * P:(k + 1) * P],
                                                self.c["ident"][:])
        last.then_inc(self.xt_done, 1)

    def project(self, pe, b, u):
        pe.wait_ge(self.xt_copied, b + 3)
        pe.wait_ge(self.q_low, b + 1)
        for m in range(KT):
            for k in range(KT):
                last = self.nc.tensor.matmul(self.ps_q[u][:, m], self.c[f"wq{self.l}"][:, k, m * P:(m + 1) * P],
                                             self.xnt[u][:, k], start=k == 0, stop=k == KT - 1)
        last.then_inc(self.q_done, 1)

    def copy(self, act, b, u):
        act.wait_ge(self.xt_done, b + 3)
        act.wait_ge(self.q_done, b + 1)
        self.nc.scalar.activation(self.xnt[u][:], self.ps_t[u][:], ACT.Copy).then_inc(self.xt_copied, 1)

    def high(self, act, b, u):
        nc = self.nc
        act.wait_ge(self.q_done, b + 3)
        act.wait_ge(self.stored[u], use_of(b, u) * 32 + 32)
        for m in range(KT):
            if self.l == 0:
                ins = nc.scalar.activation(self.qq[u][:, 0, m], self.ps_q[u][:, m], ACT.Identity, bias=self.c["bq0"][:, m:m + 1])
            else:
                ins = nc.scalar.activation(self.qq[u][:, 0, m], self.ps_q[u][:, m], ACT.Copy)
        ins.then_inc(self.q_high, 1)

    def store(self, sp, b, u):
        sp.wait_ge(self.q_low, b + 3)
        for part in (0, 1):
            sp.dma_start(self.qd[part, :, bass.ds(b * S, S)].rearrange("(m p) t -> p m t", p=P),
                         self.qq[u][:, part].bitcast(fp32)).then_inc(self.stored[u], 16)

    def end(self, sp):
        for u in (0, 1):
            sp.wait_ge(self.stored[u], (B // 2 + 1) * 32)


def on(engine, step):
    return lambda b, u: step(engine, b, u)


def first_projections(p, c):
    nc, d = p.nc, p.dram
    start = p.top
    raw = p.sb("mask_raw", [P, 2, TB, S], int32)
    q_loaded, rest_loaded, scaled = p.sem("q_weights_loaded"), p.sem("constants_loaded"), p.sem("constants_scaled")
    kv, q = KeysAndValues(p, c, 0), Queries(p, c, 0)
    p.top = start
    x_stats = p.sem("x_stats_done")
    with nc.Block() as block:
        @block.sync
        def _(sp):
            in_steps(sp, B, [(0, on(sp, kv.load)), (2, on(sp, kv.store)), (3, on(sp, q.store))])
            kv.end(sp)
            q.end(sp)

        @block.gpsimd
        def _(pool):
            q.invert(pool, 1, range(NT))

        @block.tensor
        def _(pe):
            kv.begin_pe(pe)
            q.begin_pe(pe)
            pe.wait_ge(c["kv_loaded"], 64)
            in_steps(pe, B, [(0, on(pe, kv.project)), (0, on(pe, q.transposes)), (1, on(pe, q.project))])

        @block.scalar
        def _(act):
            kv.begin_act(act)
            q.begin_act(act)
            act.dma_start(c["wq0"][:], d["wq0"]).then_inc(q_loaded, 16)
            act.dma_start(c["bq0"][:], d["bq0"]).then_inc(q_loaded, 16)
            act.dma_start(raw[:, 0], d["mask_qk"]).then_inc(rest_loaded, 16)
            act.dma_start(raw[:, 1], d["mask_kq"]).then_inc(rest_loaded, 16)
            for w in ("wo0", "wk1", "wv1", "wq1", "wo1"):
                act.dma_start(c[w][:], d[w]).then_inc(rest_loaded, 16)
            for n in ("bo0", "bo1"):
                act.dma_start(c[n][:], across_partitions(d[n], D)).then_inc(rest_loaded, 16)
            act.wait_ge(c["kv_loaded"], 64)
            in_steps(act, B, [(0, on(act, kv.high)), (0, on(act, q.copy)), (1, on(act, q.high))])

        @block.vector
        def _(dve):
            kv.begin_dve(dve)
            q.begin_dve(dve)
            dve.wait_ge(c["x_loaded"], 16)
            for t in range(NT):
                nc.vector.bn_stats(c["stats"][:, t], c["x"][:, t]).then_inc(x_stats, 1)
            dve.wait_ge(x_stats, NT)
            q.aggregate(dve, range(NT))
            dve.wait_ge(q_loaded, 32)
            nc.vector.tensor_scalar(c["wq0"][:], c["wq0"][:], DH ** -0.5, None, ALU.mult).then_inc(scaled, 1)
            nc.vector.tensor_scalar(c["bq0"][:], c["bq0"][:], DH ** -0.5, None, ALU.mult).then_inc(scaled, 1)
            dve.wait_ge(scaled, 2)
            dve.wait_ge(q.rstd_done, 1)
            in_steps(dve, B, [(0, on(dve, q.norm)), (0, on(dve, kv.low)), (2, on(dve, q.low))])
            dve.wait_ge(rest_loaded, 16 * 9)
            for n, m in enumerate(("mask_qk", "mask_kq")):
                nc.vector.tensor_scalar(c[m][:], raw[:, n], 0, NEG, ALU.is_equal, ALU.mult).then_inc(scaled, 1)
            nc.vector.tensor_scalar(c["wq1"][:], c["wq1"][:], D ** -0.5, None, ALU.mult).then_inc(scaled, 1)
            dve.wait_ge(scaled, 5)
    q.psum.close()
    kv.psum.close()


def attention(p, c, l, R, fill):
    nc = p.nc
    masked = l == 0
    start = p.top
    KS = [p.sb(f"k_stack{l}{u}", [STACK, H, S], fp32r) for u in (0, 1)]
    QS = [p.sb(f"q_stack{l}{u}", [STACK, H, S], fp32r) for u in (0, 1)]
    V = [p.sb(f"v{l}{u}", [P, TB, H, HV], fp32) for u in (0, 1)]
    NMAX = [p.sb(f"neg_max{l}{u}", [P, TB, H], fp32) for u in (0, 1)]
    MT = p.sb(f"neg_max_t{l}", [H, 2, S], fp32r)
    NP = 4
    PT = p.sb(f"probs{l}", [P, NP, TB, S], fp32)
    VT = p.sb(f"mixed_t{l}", [P, 2, S], fp32)
    RINV = p.sb(f"rinv{l}", [P, TB, H], fp32)
    O = p.sb(f"attn{l}", [P, TB, D], fp32)
    OT = p.sb(f"attn_t{l}", [P, KT, S], fp32)
    p.top = start
    psum = ExitStack()
    ps_s = [psum.enter_context(nc.psum_tensor(f"ps_s{l}{u}", [P, 2, S], fp32)) for u in (0, 1)]
    ps_p = [psum.enter_context(nc.psum_tensor(f"ps_p{l}{u}", [P, TB, S], fp32)) for u in (0, 1)]
    ps_v = psum.enter_context(nc.psum_tensor(f"ps_vt{l}", [P, 512], fp32))
    ps_o = psum.enter_context(nc.psum_tensor(f"ps_o{l}", [P, TB, 512], fp32))
    ps_m = psum.enter_context(nc.psum_tensor(f"ps_m{l}", [P, 512], fp32))
    ps_y = ps_o[:, 0].rearrange("p (t d) -> p t d", t=TB)
    md = p.scratch(f"md{l}", [B, 2, H, S], fp32)
    X = c["x"]

    first_set, stacks_set = p.sem(f"first_stacks_set{l}"), p.sem(f"stacks_set{l}")
    loaded = [[p.sem(f"kqv_loaded{l}{u}{part}") for part in (0, 1)] for u in (0, 1)]
    scored = p.sem(f"scored{l}")
    reduced = p.sem(f"max_reduced{l}")
    max_turned = p.sem(f"max_turned{l}")
    max_split = p.sem(f"max_split{l}")
    max_stored, max_loaded = p.sem(f"max_stored{l}"), p.sem(f"max_loaded{l}")
    shifted = p.sem(f"scores_shifted{l}")
    probs_done = p.sem(f"probs_done{l}")
    mixed = p.sem(f"values_mixed{l}")
    o_scaled, o_turned, ot_copied = p.sem(f"o_scaled{l}"), p.sem(f"o_turned{l}"), p.sem(f"ot_copied{l}")
    vt_copied, vt_turned = p.sem(f"vt_copied{l}"), p.sem(f"vt_turned{l}")
    y_done, x_added, bias_added = p.sem(f"y_done{l}"), p.sem(f"x_added{l}"), p.sem(f"bias_added{l}")
    LOADS = 7 * 16
    HH = H // 2
    G = H // HQ
    UNITS = (1, 1, 2, 1, 2, 1, 2, 2, 2, 2, 0, 0, 0, 0, 0, 0)
    assert sum(UNITS) == H and sum(UNITS[:6]) == HH
    TURN_MAXIMA = 10
    TURN_MIXED = {10: 0, 12: 1, 14: 2}
    TURN_LAST, NORMALISE, TURN_O, COPY_O, PROJECT, ADD = 1, 2, 5, 6, 7, 8


    R_TURN, R_COPY, R_LOGITS, R_EXP, R_NORM, R_COUNT, R_PLACE = 0, 1, 2, 4, 12, 14, 14
    R_CHOOSE = {6: (0,), 7: (1, 2), 8: (3, 4), 9: (5, 6), 10: (7, 8), 11: (9,)}

    def units(h):
        return range(sum(UNITS[:h]), sum(UNITS[:h + 1]))

    def exists(b, ahead):
        return not isinstance(b, int) or 0 <= b + ahead < B


    def each_batch(engine, f):
        f(0, 0)
        f(1, 1)
        with engine.Fori(0, B // 2 - 2) as i:
            f(i * 2 + 2, 0)
            f(i * 2 + 3, 1)
        f(B - 2, 0)
        f(B - 1, 1)

    with nc.Block() as block:
        @block.gpsimd
        def _(pool):
            nc.gpsimd.memset(QS[0][32:64].bitcast(fp32), 0.0).then_inc(first_set, 1)
            nc.gpsimd.memset(KS[0][ROW_MAX:STACK].bitcast(fp32), 1.0).then_inc(stacks_set, 1)
            nc.gpsimd.memset(QS[1][32:64].bitcast(fp32), 0.0).then_inc(stacks_set, 1)
            nc.gpsimd.memset(KS[1][32:64].bitcast(fp32), 0.0).then_inc(stacks_set, 1)
            nc.gpsimd.memset(KS[1][ROW_MAX:STACK].bitcast(fp32), 1.0).then_inc(stacks_set, 1)
            pool.wait_ge(first_set, 2)
            pool.wait_ge(stacks_set, 4)
            R.begin_pool(pool)

            def batch(b, u):
                if exists(b, -2) and l == 1:
                    R.keep_turned(pool, b - 2)
                if exists(b, 0):
                    for t in range(TB):
                        at = X[:, bass.ds(b * TB + t, 1), :].rearrange("p o d -> p (o d)")
                        nc.gpsimd.tensor_tensor(at, at, c[f"bo{l}"][:], ALU.add).then_inc(bias_added, 1)
                if exists(b, -1):
                    R.invert(pool, b - 1)
                    if l == 0:
                        R.keep_xn(pool, b - 1, 1 - u)
                if exists(b, -2) and l == 1:
                    R.scatter(pool, b - 2, u)
            each_batch(pool, batch)
            batch(B, 0)
            if l == 1:
                R.keep_turned(pool, B - 1)
                pool.wait_ge(R.xt_kept, B + 1)
            else:
                pool.wait_ge(R.xn_kept, B + 2)

        @block.sync
        def _(sp):
            def load(b, u, part):
                sp.wait_ge(mixed, b * H + (part + 1) * HH)
                heads = slice(part * HH, (part + 1) * HH)
                for name, buf, parts in (("kd", KS[u], (0, 1, 0)), ("qd", QS[u], (0, 0, 1))):
                    for row, hl in enumerate(parts):
                        src = c[f"{name}{l}"][hl, :, bass.ds(b * S, S)].rearrange("(h e) t -> e h t", h=H)
                        sp.dma_start(buf[row * DH:(row + 1) * DH, heads].bitcast(fp32), src[:, heads])\
                            .then_inc(loaded[u][part], 16)
                sp.dma_start(V[u][:, :, heads],
                             c[f"vd{l}"][bass.ds(b * S, S), :].rearrange("(t p) (h e) -> p t h e", p=P, h=H)[:, :, heads])\
                    .then_inc(loaded[u][part], 16)

            def maxima(b, u):
                sp.wait_ge(max_split, b * 2 + 2)
                sp.dma_start(md[bass.ds(b, 1)].rearrange("o a h t -> h (o a) t"), MT[:].bitcast(fp32)).then_inc(max_stored, 16)
                sp.wait_ge(max_stored, b * 16 + 16)
                sp.dma_start(QS[u][ROW_MAX:STACK].rearrange("a h t -> a (h t)").bitcast(fp32),
                             md[bass.ds(b, 1)].rearrange("o a h t -> (o a) (h t)")).then_inc(max_loaded, 16)

            sp.dma_start(R.gate[:], p.dram[f"m{l}_gate_w"]).then_inc(R.gate_loaded, 16)
            sp.wait_ge(first_set, 2)
            load(0, 0, 0)
            load(0, 0, 1)
            sp.wait_ge(stacks_set, 4)
            load(1, 1, 0)
            maxima(0, 0)

            def batch(b, u):
                if exists(b, 1):
                    load(b + 1, 1 - u, 1)
                if exists(b, 2):
                    load(b + 2, u, 0)
                if exists(b, 1):
                    maxima(b + 1, 1 - u)
                if fill:
                    fill(sp, b)
            each_batch(sp, batch)
            if fill:
                sp.wait_ge(c["filled"], B * c["FILLS"] * 16)

        @block.tensor
        def _(pe):
            pe.sem_inc(mixed, 2 * H)
            pe.sem_inc(vt_turned, 2)

            def score(b, u, n):
                if n % HH == 0:
                    pe.wait_ge(loaded[u][n // HH], (use_of(b, u) + 1) * LOADS)
                pe.wait_ge(reduced, b * H + n + 1)
                bank, qt = ps_s[n % 2], n % 2
                for j in (0, 1):
                    h = 2 * (n // 2) + j
                    last = nc.tensor.matmul(bank[:, j], QS[u][0:3 * DH, h, qt * P:(qt + 1) * P], KS[u][0:3 * DH, h],
                                            start=True, stop=not masked)
                    if masked:
                        last = nc.tensor.matmul(bank[:, j], c["identb"][:], c["mask_qk"][:, qt], start=False, stop=True)
                last.then_inc(scored, 1)

            def turn_maxima(b, u):
                pe.wait_ge(reduced, b * H + H + 2)
                for qt in range(TB):
                    last = nc.tensor.transpose(ps_m[0:H, qt * P:(qt + 1) * P], NMAX[u][:, qt], c["ident"][:])
                last.then_inc(max_turned, 1)

            def shift(b, u, h):
                pe.wait_ge(probs_done, b * H + h + 1)
                for kt in range(TB):
                    last = nc.tensor.matmul(ps_p[h % 2][:, kt], KS[u][:, h, kt * P:(kt + 1) * P], QS[u][:, h],
                                            start=True, stop=not masked)
                    if masked:
                        last = nc.tensor.matmul(ps_p[h % 2][:, kt], c["identb"][:], c["mask_kq"][:, kt],
                                                start=False, stop=True)
                last.then_inc(shifted, 1)

            def mix(b, u, h):
                pe.wait_ge(probs_done, b * H + h + 3)
                if h % HQ == 0:
                    pe.wait_ge(vt_copied, b * G + h // HQ + 1)
                rows = ps_v[h % HQ * HV:(h % HQ + 1) * HV, 0:S]
                for kt in range(TB):
                    last = nc.tensor.matmul(rows, V[u][:, kt, h], PT[:, h % NP, kt], start=kt == 0, stop=kt == TB - 1)
                last.then_inc(mixed, 1)

            def turn_mixed(b, g):
                pe.wait_ge(vt_copied, b * G + g + 2)
                if g == 0:
                    pe.wait_ge(o_scaled, b + 1)
                    pe.wait_ge(x_added, b + 1)
                for qt in range(TB):
                    last = nc.tensor.transpose(ps_o[:, qt, g * P:(g + 1) * P], VT[:, g % 2, qt * P:(qt + 1) * P], c["ident"][:])
                last.then_inc(vt_turned, 1)

            def turn_o(b):
                pe.wait_ge(o_scaled, b + 2)
                if isinstance(b, int) and b == 0:
                    pe.wait_ge(max_split, b * 2 + 4)
                for k in range(KT):
                    for t in range(TB):
                        last = nc.tensor.transpose(ps_m[:, k * S + t * P:k * S + (t + 1) * P], O[:, t, k * P:(k + 1) * P],
                                                   c["ident"][:])
                last.then_inc(o_turned, 1)

            def project(b):
                pe.wait_ge(ot_copied, b + 1)
                for t in range(TB):
                    for k in range(KT):
                        last = nc.tensor.matmul(ps_y[:, t], OT[:, k, t * P:(t + 1) * P], c[f"wo{l}"][:, k],
                                                start=k == 0, stop=k == KT - 1)
                last.then_inc(y_done, 1)

            R.begin_pe(pe)
            for n in range(H):
                score(0, 0, n)
            turn_maxima(0, 0)
            pe.wait_ge(stacks_set, 4)

            def batch(b, u):
                pe.wait_ge(max_loaded, b * 16 + 16)
                for h in range(H):
                    shift(b, u, h)
                    if exists(b, 1):
                        for n in units(h):
                            score(b + 1, 1 - u, n)
                    if h >= 1:
                        mix(b, u, h - 1)
                    elif exists(b, -1):
                        mix(b - 1, 1 - u, H - 1)
                    if exists(b, 1) and h == TURN_MAXIMA:
                        turn_maxima(b + 1, 1 - u)
                    if exists(b, -2):
                        if h == R_TURN:
                            R.turn(pe, b - 2, u, ps_m)
                        if h == R_LOGITS:
                            R.logits(pe, b - 2, ps_m)
                        if h == R_COUNT:
                            if exists(b, 1):
                                pe.wait_ge(max_split, b * 2 + 4)
                            R.count(pe, b - 2, ps_m)
                    if exists(b, -1):
                        if h == TURN_LAST:
                            turn_mixed(b - 1, G - 1)
                        if h == TURN_O:
                            if exists(b, -2):
                                pe.wait_ge(R.exp_done, b * TB)
                            turn_o(b - 1)
                        if h == PROJECT:
                            project(b - 1)
                    if h in TURN_MIXED:
                        turn_mixed(b, TURN_MIXED[h])
            each_batch(pe, batch)
            mix(B - 1, (B - 1) % 2, H - 1)
            turn_mixed(B - 1, G - 1)
            R.turn(pe, B - 2, 0, ps_m)
            R.logits(pe, B - 2, ps_m)
            pe.wait_ge(R.exp_done, B * TB)
            turn_o(B - 1)
            project(B - 1)
            R.count(pe, B - 2, ps_m)
            R.turn(pe, B - 1, 1, ps_m)
            R.logits(pe, B - 1, ps_m)
            pe.wait_ge(R.exp_done, (B + 1) * TB)
            R.count(pe, B - 1, ps_m)

        @block.vector
        def _(dve):
            dve.sem_inc(reduced, 2)
            dve.sem_inc(o_scaled, 1)
            dve.sem_inc(x_added, 1)

            def reduce(b, u, n):
                dve.wait_ge(scored, b * H + n + 1)
                hp = 2 * (n // 2)
                nc.vector.tensor_reduce(NMAX[u][:, n % 2, hp:hp + 2], ps_s[n % 2][:], AX.X, ALU.max,
                                        negate=True).then_inc(reduced, 1)

            def split_maxima(b):
                dve.wait_ge(max_turned, b + 1)
                if exists(b, -1):
                    dve.wait_ge(max_stored, b * 16)
                rows = ps_m[0:H, 0:S]
                nc.vector.tensor_copy(MT[:, 0], rows).then_inc(max_split, 1)
                dve.wait_ge(max_split, b * 2 + 1)
                nc.vector.tensor_tensor(MT[:, 1], rows, MT[:, 0].bitcast(fp32), ALU.subtract).then_inc(max_split, 1)

            sums = ps_o[:].rearrange("p t (h e) -> p t h e", h=H)

            def invert(b):
                dve.wait_ge(vt_turned, (b + 1) * G + 2)
                nc.vector.reciprocal(RINV[:], sums[:, :, :, DH]).then_inc(rinv_done, 1)

            def normalise(b, t):
                dve.wait_ge(rinv_done, b + 1)
                ins = nc.vector.tensor_tensor(O[:, t].rearrange("p (h e) -> p h e", h=H), sums[:, t, :, 0:DH],
                                              RINV[:, t].unsqueeze(2).broadcast_to([P, H, DH]), ALU.mult)
                if t == TB - 1:
                    ins.then_inc(o_scaled, 1)

            def add(b):
                dve.wait_ge(bias_added, b * TB + TB)
                dve.wait_ge(y_done, b + 1)
                at = X[:, bass.ds(b * TB, TB), :]
                nc.vector.tensor_tensor(at, ps_y[:], at, ALU.add).then_inc(x_added, 1)

            def stats(b, t):
                dve.wait_ge(x_added, b + 2)
                R.stats(dve, b, t)

            rinv_done = p.sem(f"rinv_done{l}")
            R.begin_dve(dve)
            nc.vector.memset(KS[0][32:64].bitcast(fp32), 0.0).then_inc(first_set, 1)
            for n in range(H):
                reduce(0, 0, n)
            split_maxima(0)

            def batch(b, u):
                for h in range(H):
                    parts = R_CHOOSE.get(h, ()) if exists(b, -2) else ()
                    made = len(units(h)) if exists(b, 1) else 0
                    if exists(b, 1):
                        if h == TURN_MAXIMA:
                            split_maxima(b + 1)
                        for i, n in enumerate(units(h)):
                            reduce(b + 1, 1 - u, n)
                            if i < len(parts):
                                R.choose(dve, b - 2, parts[i])
                    for part in parts[made:]:
                        R.choose(dve, b - 2, part)
                    if exists(b, -1):
                        if h == NORMALISE:
                            invert(b - 1)
                        if h > NORMALISE and h - NORMALISE <= TB:
                            normalise(b - 1, h - NORMALISE - 1)
                        if h == ADD:
                            add(b - 1)
                        if h > ADD and h - ADD <= TB:
                            stats(b - 1, h - ADD - 1)
                        if h == R_NORM - 1:
                            R.aggregate(dve, b - 1)
                    if exists(b, -2):
                        if h == R_EXP - 1:
                            R.top(dve, b - 2, ps_m)
                    if exists(b, -1) and h == R_NORM:
                        R.norm(dve, b - 1, 1 - u)
                    if exists(b, -2) and h == R_PLACE:
                        R.place(dve, b - 2, u, ps_m)
            each_batch(dve, batch)
            invert(B - 1)
            for t in range(TB):
                normalise(B - 1, t)
            R.top(dve, B - 2, ps_m)
            add(B - 1)
            for t in range(TB):
                stats(B - 1, t)
            R.aggregate(dve, B - 1)
            for part in range(CHOOSE):
                R.choose(dve, B - 2, part)
            R.norm(dve, B - 1, 1)
            R.place(dve, B - 2, 0, ps_m)
            R.top(dve, B - 1, ps_m)
            for part in range(CHOOSE):
                R.choose(dve, B - 1, part)
            R.place(dve, B - 1, 1, ps_m)

        @block.scalar
        def _(act):
            act.sem_inc(probs_done, 2)
            act.sem_inc(vt_copied, 1)
            R.begin_act(act)

            def copy_mixed(b, g):
                act.wait_ge(mixed, b * H + (g + 1) * HQ + 2 * H)
                act.wait_ge(vt_turned, b * G + g + 1)
                nc.scalar.activation(VT[:, g % 2], ps_v[:, 0:S], ACT.Copy).then_inc(vt_copied, 1)

            def copy_o(b):
                act.wait_ge(o_turned, b + 1)
                nc.scalar.activation(OT[:].rearrange("p k t -> p (k t)"), ps_m[:], ACT.Copy).then_inc(ot_copied, 1)

            def batch(b, u):
                for h in range(H):
                    act.wait_ge(shifted, b * H + h + 1)
                    act.wait_ge(mixed, b * H + h + 1 + 2 * H - NP)
                    nc.scalar.activation(PT[:, h % NP], ps_p[h % 2][:], ACT.Exp).then_inc(probs_done, 1)
                    if h % HQ == 0:
                        if h > 0:
                            copy_mixed(b, h // HQ - 1)
                        elif exists(b, -1):
                            copy_mixed(b - 1, G - 1)
                    if exists(b, -2):
                        if h == R_COPY:
                            R.copy_turned(act, b - 2, ps_m)
                        if h == R_EXP:
                            R.exp(act, b - 2, ps_m)
                    if h == COPY_O and exists(b, -1):
                        copy_o(b - 1)
            each_batch(act, batch)
            copy_mixed(B - 1, G - 1)
            R.copy_turned(act, B - 2, ps_m)
            R.exp(act, B - 2, ps_m)
            copy_o(B - 1)
            R.copy_turned(act, B - 1, ps_m)
            R.exp(act, B - 1, ps_m)
    psum.close()


def in_steps(engine, n, stages, unroll=2):
    most = max(lag for lag, _ in stages)
    first = (most + unroll - 1) // unroll
    last = n // unroll

    def step(s, place):
        for lag, f in stages:
            if not isinstance(s, int) or 0 <= s - lag < n:
                f(s - lag, (place - lag) % unroll)

    for s in range(unroll * first):
        step(s, s % unroll)
    with engine.Fori(0, last - first) as i:
        for place in range(unroll):
            step(i * unroll + unroll * first + place, place)
    for s in range(unroll * last, n + most):
        step(s, s % unroll)


def routing_constants(p, c):
    nc = p.nc
    c["count_i"] = p.sb("count_i", [P, TILES0], int32)
    c["count"] = p.sb("count", [P, TILES0], fp32)
    c["before"] = p.sb("before", [P, P], bf16)
    c["ones"] = p.sb("ones", [P, P], bf16)
    made = p.sem("routing_constants")
    with nc.Block() as block:
        @block.gpsimd
        def _(pool):
            nc.gpsimd.iota(c["count_i"][:], pattern=[[1, TILES0]], base=0, channel_multiplier=0).then_inc(made, 1)
            nc.gpsimd.memset(c["ones"][:], 1.0).then_inc(made, 1)
            nc.gpsimd.memset(c["before"][:], 1.0).then_inc(made, 1)
            pool.wait_ge(made, 3)
            nc.gpsimd.affine_select(out=c["before"][:], in_=c["before"][:], compare_op=ALU.is_gt, fill=0.0, base=0,
                                    pattern=[[1, P]], channel_multiplier=-1).then_inc(made, 1)

        @block.vector
        def _(dve):
            dve.wait_ge(made, 4)
            nc.vector.tensor_copy(c["count"][:], c["count_i"][:]).then_inc(made, 1)
            dve.wait_ge(made, 5)


def routing_results(p, c, l, E, K):
    if l == 0:
        c["xn"] = p.sb("xn_all", [P, NT, D], fp32)
        c["hot"] = p.sb("choice_expert", [P, K, NT, E], fp32)
        c["pos"] = p.sb("choice_place", [P, K, NT], fp32)
    else:
        c["xnt"] = p.sb("xn_turned", [P, KT, N], fp32)
        c["slot_read"] = p.sb("slot_read", [P, K, NT], int32)
    c["weight"] = p.sb(f"choice_weight{l}", [P, K, NT], fp32)
    c["carry"] = p.sb(f"choices_before{l}", [P, E], fp32)


class Routing:

    def __init__(self, p, c, l, E, K):
        nc = p.nc
        self.nc, self.c, self.l, self.E, self.K = nc, c, l, E, K
        self.X = c["x"]
        if l == 0:
            self.HOT, self.POS = c["hot"], c["pos"]
        self.W, self.carry = c["weight"], c["carry"]
        self.gate = p.sb(f"gate{l}", [P, KT, E], fp32)
        self.st = p.sb(f"m_stats{l}", [P, TB, 6], fp32)
        self.mv = p.sb(f"m_mean_var{l}", [P, TB, 2], fp32)
        self.ve = p.sb(f"m_var{l}", [P, TB], fp32)
        self.rs = p.sb(f"m_rstd{l}", [P, TB], fp32)
        self.hold = p.sb(f"m_hold{l}", [1, 8], fp32)
        self.hold_pool = p.sb(f"m_hold_pool{l}", [1, 2], fp32)
        self.xn = [p.sb(f"m_xn{l}{u}", [P, TB, D], fp32) for u in (0, 1)]
        self.xnt = p.sb(f"m_xnt{l}", [P, KT, S], fp32)
        self.ntop = p.sb(f"neg_top{l}", [P, TB], fp32)
        self.ex = p.sb(f"gate_exp{l}", [P, TB, E], fp32)
        self.total = p.sb(f"gate_sum{l}", [P, TB], fp32)
        self.prob = p.sb(f"gate_prob{l}", [P, TB, E], fp32)
        self.w8 = p.sb(f"choice_prob{l}", [P, TB, 8], fp32)
        self.idx = p.sb(f"choice{l}", [P, TB, 8], mybir.dt.uint32)
        self.idxf = p.sb(f"choice_f{l}", [P, K, TB], fp32)
        self.hot = p.sb(f"chosen{l}", [P, K, TB, E], fp32)
        self.M = p.sb(f"chosen_any{l}", [P, TB, E], bf16)
        self.where = p.sb(f"where{l}", [P, TB, E], fp32)
        self.picked = p.sb(f"picked{l}", [P, K, TB, E], fp32)
        if l == 1:
            self.gmax = p.sb("group_max", [P, TB, G1], fp32)
            self.g8 = p.sb("group_top", [P, TB, 8], fp32)
            self.gidx = p.sb("group_choice", [P, TB, 8], mybir.dt.uint32)
            self.gidxf = p.sb("group_choice_f", [P, TB, 8], fp32)
            self.same = p.sb("group_same", [P, TB, G1, LG1], fp32)
            self.keep = p.sb("group_kept", [P, TB, G1], fp32)
            self.drop = p.sb("group_dropped", [P, TB, G1], fp32)
            self.kept = p.sb("prob_kept", [P, TB, E], fp32)
            self.wt = p.sb("choice_share", [P, K, TB], fp32)
            self.pos = p.sb("choice_position", [P, K, TB], fp32)
            self.fits = p.sb("choice_fits", [P, K, TB], fp32)
            self.over_cap = p.sb("choice_over", [P, K, TB], fp32)
            self.slotf = p.sb("slot_f", [P, K, TB], fp32)
            self.slot = [p.sb(f"slot{u}", [P, K, TB], int32) for u in (0, 1)]
            self.scattered = p.pool_dma_sem("scattered1")
        self.gate_loaded = p.sem(f"m{l}_gate_loaded")
        self.stats_done = p.sem(f"m{l}_stats_done")
        self.aggregated = p.sem(f"m{l}_aggregated")
        self.var_done = p.sem(f"m{l}_var_done")
        self.rstd_done = p.sem(f"m{l}_rstd_done")
        self.xn_done = p.sem(f"m{l}_xn_done")
        self.xn_kept = p.sem(f"m{l}_xn_kept")
        self.xt_turned = p.sem(f"m{l}_xt_turned")
        self.xt_copied = p.sem(f"m{l}_xt_copied")
        self.xt_kept = p.sem(f"m{l}_xt_kept")
        self.logits_done = p.sem(f"m{l}_logits_done")
        self.top_done = p.sem(f"m{l}_top_done")
        self.exp_done = p.sem(f"m{l}_exp_done")
        self.step = p.sem(f"m{l}_step")
        self.chosen = p.sem(f"m{l}_chosen")
        self.counted = p.sem(f"m{l}_counted")
        self.places_read = p.sem(f"m{l}_places_read")
        self.slots_done = p.sem(f"m{l}_slots_done")
        self.STEPS = 13 if l == 0 else 26

    def begin_dve(self, dve):
        dve.sem_inc(self.xn_done, 1)
        dve.sem_inc(self.step, self.STEPS)
        self.nc.vector.memset(self.carry[:], 0.0).then_inc(self.places_read, 1)

    def begin_pe(self, pe):
        pe.sem_inc(self.xt_turned, 2)
        pe.sem_inc(self.logits_done, 1)
        pe.wait_ge(self.gate_loaded, 16)

    def begin_act(self, act):
        act.sem_inc(self.exp_done, TB)

    def begin_pool(self, pool):
        pool.sem_inc(self.rstd_done, 1)
        if self.l == 1:
            pool.sem_inc(self.xt_kept, 1)
        pool.sem_inc(self.xn_kept, 2)

    def stats(self, dve, r, t):
        nc = self.nc
        nc.vector.memset(self.hold[:, t:t + 1], 0.0)
        nc.vector.bn_stats(self.st[:, t], self.X[:, bass.ds(r * TB + t, 1), :].rearrange("p o d -> p (o d)"))\
            .then_inc(self.stats_done, 1)

    def aggregate(self, dve, r):
        nc = self.nc
        dve.wait_ge(self.stats_done, r * TB + TB)
        nc.vector.memset(self.hold[:, 2:3], 0.0)
        for t in range(TB):
            nc.vector.bn_aggr(self.mv[:, t], self.st[:, t]).then_inc(self.aggregated, 1)
        dve.wait_ge(self.aggregated, r * TB + TB)
        dve.wait_ge(self.rstd_done, r + 1)
        nc.vector.tensor_scalar(self.ve[:], self.mv[:, :, 1], EPS, None, ALU.add).then_inc(self.var_done, 1)

    def invert(self, pool, r):
        pool.wait_ge(self.var_done, r + 1)
        pool.wait_ge(self.xn_done, r + 1)
        self.nc.gpsimd.tensor_tensor(self.rs[:], self.ve[:], self.c["minus_half"][:, 0:TB], ALU.pow)\
            .then_inc(self.rstd_done, 1)

    def norm(self, dve, r, u):
        nc = self.nc
        dve.wait_ge(self.rstd_done, r + 2)
        dve.wait_ge(self.xt_turned, r + 1)
        dve.wait_ge(self.xn_kept, r + 1)
        for t in range(TB):
            ins = nc.vector.tensor_scalar(self.xn[u][:, t], self.X[:, bass.ds(r * TB + t, 1), :].rearrange("p o d -> p (o d)"),
                                          self.mv[:, t, 0:1], self.rs[:, t:t + 1], ALU.subtract, ALU.mult)
        ins.then_inc(self.xn_done, 1)

    def keep_xn(self, pool, r, u):
        pool.wait_ge(self.xn_done, r + 2)
        self.nc.gpsimd.tensor_copy(self.c["xn"][:, bass.ds(r * TB, TB), :], self.xn[u][:]).then_inc(self.xn_kept, 1)

    def turn(self, pe, r, u, bank):
        pe.wait_ge(self.xn_done, r + 2)
        pe.wait_ge(self.places_read, r + 1)
        for t in range(TB):
            for k in range(KT):
                last = self.nc.tensor.transpose(bank[:, k * S + t * P:k * S + (t + 1) * P], self.xn[u][:, t, k * P:(k + 1) * P],
                                                self.c["ident"][:])
        last.then_inc(self.xt_turned, 1)

    def copy_turned(self, act, r, bank):
        act.wait_ge(self.xt_turned, r + 3)
        act.wait_ge(self.logits_done, r + 1)
        if self.l == 1:
            act.wait_ge(self.xt_kept, r + 1)
        self.nc.scalar.activation(self.xnt[:].rearrange("p k t -> p (k t)"), bank[:], ACT.Copy).then_inc(self.xt_copied, 1)

    def keep_turned(self, pool, r):
        pool.wait_ge(self.xt_copied, r + 1)
        self.nc.gpsimd.tensor_copy(self.c["xnt"][:, :, bass.ds(r * S, S)], self.xnt[:]).then_inc(self.xt_kept, 1)

    def logits(self, pe, r, bank):
        pe.wait_ge(self.xt_copied, r + 1)
        for t in range(TB):
            for k in range(KT):
                last = self.nc.tensor.matmul(bank[:, t * self.E:(t + 1) * self.E], self.xnt[:, k, t * P:(t + 1) * P],
                                             self.gate[:, k], start=k == 0, stop=k == KT - 1)
        last.then_inc(self.logits_done, 1)

    def top(self, dve, r, bank):
        dve.wait_ge(self.logits_done, r + 2)
        dve.wait_ge(self.exp_done, r * TB + TB)
        self.nc.vector.tensor_reduce(self.ntop[:], bank[:, 0:TB * self.E].rearrange("p (t e) -> p t e", t=TB), AX.X, ALU.max,
                                     negate=True).then_inc(self.top_done, 1)

    def exp(self, act, r, bank):
        act.wait_ge(self.top_done, r + 1)
        act.wait_ge(self.step, (r + 1) * self.STEPS)
        for t in range(TB):
            self.nc.scalar.activation(self.ex[:, t], bank[:, t * self.E:(t + 1) * self.E], ACT.Exp,
                                      bias=self.ntop[:, t:t + 1]).then_inc(self.exp_done, 1)

    def chain(self, dve, r):
        def then(ins):
            ins.then_inc(self.step, 1)
            self.done += 1

        def ready():
            dve.wait_ge(self.step, (r + 1) * self.STEPS + self.done)
        return then, ready

    def choose(self, dve, r, part):
        nc, E, K, total, prob = self.nc, self.E, self.K, self.total, self.prob
        source = prob if self.l == 0 else self.kept
        if part == 0:
            self.done = 0
        then, ready = self.chain(dve, r)

        def by_group(v):
            return v[:].rearrange("p t (g e) -> p (t g) e", g=G1)

        def over_group(v):
            return v[:].rearrange("p t g -> p (t g)").unsqueeze(2).broadcast_to([P, TB * G1, GE1])

        if part == 0:
            dve.wait_ge(self.exp_done, r * TB + 2 * TB)
            then(nc.vector.tensor_reduce(total[:], self.ex[:], AX.X, ALU.add))
            ready()
            then(nc.vector.reciprocal(total[:], total[:]))
        if part == 1:
            ready()
            then(nc.vector.tensor_tensor(prob[:], self.ex[:], total[:].unsqueeze(2).broadcast_to([P, TB, E]), ALU.mult))
            if self.l == 1:
                ready()
                then(nc.vector.tensor_reduce(self.gmax[:], prob[:].rearrange("p t (g e) -> p t g e", g=G1), AX.X, ALU.max))
        if part == 2 and self.l == 1:
            ready()
            nc.vector.memset(self.hold[:, 3:4], 0.0)
            for t in range(TB):
                ins = nc.vector.max(self.g8[:, t], self.gmax[:, t])
            then(ins)
            ready()
            nc.vector.memset(self.hold[:, 4:5], 0.0)
            for t in range(TB):
                ins = nc.vector.max_index(self.gidx[:, t], self.g8[:, t], self.gmax[:, t])
            then(ins)
        if part == 3 and self.l == 1:
            ready()
            then(nc.vector.tensor_copy(self.gidxf[:], self.gidx[:]))
            ready()
            for t in range(TB):
                ins = nc.vector.tensor_tensor(self.same[:, t], self.gidxf[:, t, 0:LG1].unsqueeze(1).broadcast_to([P, G1, LG1]),
                                              self.c["count"][:, 0:G1].unsqueeze(2).broadcast_to([P, G1, LG1]), ALU.is_equal)
            then(ins)
        if part == 4 and self.l == 1:
            ready()
            then(nc.vector.tensor_reduce(self.keep[:], self.same[:], AX.X, ALU.add))
            ready()
            then(nc.vector.tensor_scalar(self.drop[:], self.keep[:], -1.0, None, ALU.add))
        if part == 5 and self.l == 1:
            ready()
            then(nc.vector.tensor_tensor(by_group(source), by_group(prob), over_group(self.keep), ALU.mult))
            ready()
            then(nc.vector.tensor_tensor(by_group(source), by_group(source), over_group(self.drop), ALU.add))
        if part == 6:
            ready()
            nc.vector.memset(self.hold[:, 5:6], 0.0)
            for t in range(TB):
                ins = nc.vector.max(self.w8[:, t], source[:, t])
            then(ins)
            ready()
            nc.vector.memset(self.hold[:, 6:7], 0.0)
            for t in range(TB):
                ins = nc.vector.max_index(self.idx[:, t], self.w8[:, t], source[:, t])
            then(ins)
        if part == 7:
            ready()
            then(nc.vector.tensor_copy(self.idxf[:], self.idx[:, :, 0:K].rearrange("p t k -> p k t")))
            ready()
            then(nc.vector.tensor_tensor(self.hot[:].rearrange("p k t e -> p (k t) e"),
                                         self.idxf[:].rearrange("p k t -> p (k t)").unsqueeze(2).broadcast_to([P, K * TB, E]),
                                         self.c["count"][:, 0:E].unsqueeze(1).broadcast_to([P, K * TB, E]), ALU.is_equal))
        if part == 8:
            ready()
            with nc.allow_low_precision(reason="the sums are 0 or 1"):
                nc.vector.tensor_reduce(self.M[:].rearrange("p t e -> p (t e)"), self.hot[:].rearrange("p k t e -> p (t e) k"),
                                        AX.X, ALU.add).then_inc(self.chosen, 1)
            then(nc.vector.tensor_reduce(total[:], self.w8[:, :, 0:K], AX.X, ALU.add))
        if part == 9:
            if self.l == 1:
                ready()
                then(nc.vector.tensor_scalar(total[:], total[:], 1e-9, None, ALU.add))
            ready()
            then(nc.vector.reciprocal(total[:], total[:]))
            ready()
            share = self.W[:, :, bass.ds(r * TB, TB)] if self.l == 0 else self.wt[:]
            then(nc.vector.tensor_tensor(share, self.w8[:, :, 0:K].rearrange("p t k -> p k t"),
                                         total[:].unsqueeze(1).broadcast_to([P, K, TB]), ALU.mult))

    def count(self, pe, r, bank):
        nc, E = self.nc, self.E
        pe.wait_ge(self.chosen, r + 1)
        nc.tensor.matmul(bank[:, 0:TB * E], self.c["before"][:], self.M[:].rearrange("p t e -> p (t e)"), start=True, stop=False)
        for t in range(TB - 1):
            nc.tensor.matmul(bank[:, (t + 1) * E:TB * E].rearrange("p (t e) -> p t e", e=E), self.c["ones"][:],
                             self.M[:, t:t + 1].broadcast_to([P, TB - 1 - t, E]), start=False, stop=t == TB - 2)
        for t in range(TB):
            last = nc.tensor.matmul(bank[:, TB * E:(TB + 1) * E], self.c["ones"][:], self.M[:, t], start=t == 0, stop=t == TB - 1)
        last.then_inc(self.counted, 1)

    def place(self, dve, r, u, bank):
        nc, E, K = self.nc, self.E, self.K
        then, ready = self.chain(dve, r)
        dve.wait_ge(self.counted, r + 1)
        dve.wait_ge(self.places_read, r + 1)
        ready()
        then(nc.vector.tensor_tensor(self.where[:], bank[:, 0:TB * E].rearrange("p (t e) -> p t e", t=TB),
                                     self.carry[:].unsqueeze(1).broadcast_to([P, TB, E]), ALU.add))
        ready()
        nc.vector.tensor_tensor(self.carry[:], self.carry[:], bank[:, TB * E:(TB + 1) * E], ALU.add)\
            .then_inc(self.places_read, 1)
        ready()
        then(nc.vector.tensor_tensor(self.picked[:].rearrange("p k t e -> p k (t e)"),
                                     self.where[:].rearrange("p t e -> p (t e)").unsqueeze(1).broadcast_to([P, K, TB * E]),
                                     self.hot[:].rearrange("p k t e -> p k (t e)"), ALU.mult))
        ready()
        at = bass.ds(r * TB, TB)
        if self.l == 0:
            nc.vector.tensor_reduce(self.POS[:, :, at], self.picked[:], AX.X, ALU.add)
            for k in range(K):
                ins = nc.vector.tensor_copy(self.HOT[:, k, at], self.hot[:, k])
            then(ins)
        else:
            then(nc.vector.tensor_reduce(self.pos[:], self.picked[:], AX.X, ALU.add))
            ready()
            nc.vector.tensor_scalar(self.fits[:], self.pos[:], float(CAP), None, ALU.is_lt)
            nc.vector.tensor_scalar(self.over_cap[:], self.pos[:], float(CAP), float(SLOTS1), ALU.is_ge, ALU.mult)
            then(nc.vector.scalar_tensor_tensor(self.slotf[:], self.idxf[:], float(CAP), self.pos[:], ALU.mult, ALU.add))
            ready()
            then(nc.vector.tensor_tensor(self.slotf[:], self.slotf[:], self.over_cap[:], ALU.add))
            ready()
            nc.vector.tensor_copy(self.slot[u][:], self.slotf[:]).then_inc(self.slots_done, 1)
            nc.vector.tensor_tensor(self.W[:, :, at], self.wt[:], self.fits[:], ALU.mult)
            then(nc.vector.tensor_scalar(self.c["slot_read"][:, :, at], self.slotf[:], float(SLOTS1 - 1), None, ALU.min))
        ready()
        assert self.done == self.STEPS, self.done

    def scatter(self, pool, r, u):
        table = self.c["slots_in1"]
        pool.wait_ge(self.slots_done, r + 1)
        one = self.c["minus_half"][0:1, 0:1]
        self.nc.gpsimd.tensor_tensor(self.hold_pool[:, u:u + 1], one, one, ALU.mult)
        for k in range(self.K):
            for t in range(TB):
                self.nc.gpsimd.indirect_dma_start(table, bass.IndirectOffsetOnAxis(ap=self.slot[u][:, k, t:t + 1], axis=0),
                                                  self.xn[u][:, t], None, bounds_check=table.shape[0] - 1,
                                                  oob_is_err=False).then_inc(self.scattered, 16)
        pool.wait_ge(self.scattered, (r + 1) * 16 * self.K * TB)
        pool.sem_inc(self.xn_kept, 1)


def place_first(p, c):
    nc = p.nc
    E, K = E0, K0
    SLOT = c["slot"] = p.sb("slot0", [P, K, NT], int32)
    TE = c["tile_expert"] = p.sb("tile_expert", [P, TILES0], int32)
    c["below_experts"] = p.top
    c["w2"] = p.sb("m0_w2", [P, E0, HT0, D], fp32)
    tables = (("b1", H0), ("ln1_b", H0), ("b2", D))
    for n, w in tables:
        c["m0_" + n] = p.sb(f"m0_{n}b", [P, E0, w], fp32)
    start = p.top
    cnt_i = p.sb("tiles_i", [P, E], int32)
    tiles = p.sb("tiles_f", [P, E], fp32)
    ends = p.sb("tile_ends", [P, E], fp32)
    base = p.sb("slot_base", [P, E], fp32)
    past = p.sb("tiles_past", [P, TILES0, E], fp32)
    te = p.sb("tile_expert_f", [P, TILES0], fp32)
    picked = p.sb("base_picked", [P, K * NT, E], fp32)
    slotf = p.sb("slot0_f", [P, K * NT], fp32)
    step, slots_done, tables_loaded = p.sem("place_step"), p.sem("slots0_done"), p.sem("m0_tables_loaded")
    scattered = p.pool_dma_sem("scattered_first")
    kv = KeysAndValues(p, c, 1)
    p.top = start
    with nc.Block() as block:
        @block.sync
        def _(sp):
            def expert(e, u):
                sp.dma_start(c["w2"][:, bass.ds(e, 1)].rearrange("p o k d -> p (o k) d"),
                             p.dram["m0_w2"][bass.ds(e, 1)].rearrange("o (k p) d -> p (o k) d", p=P)).then_inc(tables_loaded, 16)
                for n, _ in tables:
                    at = c["m0_" + n][:, bass.ds(e, 1)].rearrange("p o h -> p (o h)")
                    sp.dma_start(at, p.dram["m0_" + n][bass.ds(e, 1)].broadcast_to([P, at.shape[1]])).then_inc(tables_loaded, 16)

            in_steps(sp, B, [(0, on(sp, kv.load)), (0, expert), (2, on(sp, kv.store))])
            kv.end(sp)
            sp.wait_ge(tables_loaded, 16 * 4 * E0)

        @block.tensor
        def _(pe):
            kv.begin_pe(pe)
            in_steps(pe, B, [(0, on(pe, kv.project))])

        @block.scalar
        def _(act):
            kv.begin_act(act)
            in_steps(act, B, [(0, on(act, kv.high))])

        @block.vector
        def _(dve):
            done = [0]

            def then(ins):
                ins.then_inc(step, 1)
                done[0] += 1
                dve.wait_ge(step, done[0])

            then(nc.vector.tensor_scalar(cnt_i[:], c["carry"][:], float(P - 1), None, ALU.add))
            then(nc.vector.tensor_scalar(cnt_i[:], cnt_i[:], 7, None, ALU.arith_shift_right))
            then(nc.vector.tensor_copy(tiles[:], cnt_i[:]))
            then(nc.vector.tensor_copy(ends[:, 0:1], tiles[:, 0:1]))
            for e in range(1, E):
                then(nc.vector.tensor_tensor(ends[:, e:e + 1], ends[:, e - 1:e], tiles[:, e:e + 1], ALU.add))
            then(nc.vector.tensor_tensor(base[:], ends[:], tiles[:], ALU.subtract))
            then(nc.vector.tensor_scalar(base[:], base[:], float(P), None, ALU.mult))
            then(nc.vector.tensor_tensor(picked[:], c["hot"][:].rearrange("p k t e -> p (k t) e"),
                                         base[:].unsqueeze(1).broadcast_to([P, K * NT, E]), ALU.mult))
            then(nc.vector.tensor_reduce(slotf[:], picked[:], AX.X, ALU.add))
            then(nc.vector.tensor_tensor(slotf[:], slotf[:], c["pos"][:].rearrange("p k t -> p (k t)"), ALU.add))
            nc.vector.tensor_copy(SLOT[:].rearrange("p k t -> p (k t)"), slotf[:]).then_inc(slots_done, 1)
            then(nc.vector.tensor_tensor(past[:], c["count"][:].unsqueeze(2).broadcast_to([P, TILES0, E]),
                                         ends[:].unsqueeze(1).broadcast_to([P, TILES0, E]), ALU.is_ge))
            then(nc.vector.tensor_reduce(te[:], past[:], AX.X, ALU.add))
            then(nc.vector.tensor_scalar(TE[:], te[:], float(E - 1), None, ALU.min))
            kv.begin_dve(dve)
            in_steps(dve, B, [(0, on(dve, kv.low))])

        @block.gpsimd
        def _(pool):
            table = c["slots_in0"]
            pool.wait_ge(slots_done, 1)
            for k in range(K):
                for t in range(NT):
                    nc.gpsimd.indirect_dma_start(table, bass.IndirectOffsetOnAxis(ap=SLOT[:, k, t:t + 1], axis=0),
                                                 c["xn"][:, t, :], None, bounds_check=table.shape[0] - 1,
                                                 oob_is_err=False).then_inc(scattered, 16)
            pool.wait_ge(scattered, 16 * K * NT)
    kv.psum.close()


def experts_first(p, c):
    nc = p.nc
    W1, W2, TE = c["w1"], c["w2"], c["tile_expert"]
    start = p.top
    B1, G, BB, B2 = (c["m0_" + n] for n in ("b1", "ln1_g", "ln1_b", "b2"))
    NB = 4
    xg = [p.sb(f"xg{u}", [P, D], fp32) for u in range(NB)]
    xt = [p.sb(f"xgt{u}", [P, KT, P], fp32) for u in (0, 1)]
    hs = [p.sb(f"hs{u}", [P, H0], fp32) for u in range(NB)]
    gs = [p.sb(f"gs{u}", [P, H0], fp32) for u in (0, 1)]
    ht = [p.sb(f"ht{u}", [P, HT0, P], fp32) for u in (0, 1)]
    ys = [p.sb(f"ys{u}", [P, D], fp32) for u in range(NB)]
    st = p.sb("h_stats", [P, NB, 6], fp32)
    mv = p.sb("h_mean_var", [P, NB, 2], fp32)
    ve = p.sb("h_var", [P, NB], fp32)
    hold = p.sb("hold", [1, 1], fp32)
    rs = p.sb("h_rstd", [P, NB], fp32)
    p.top = start
    psum = ExitStack()
    ps_x, ps_h, ps_t, ps_y = ([psum.enter_context(nc.psum_tensor(f"ps_m0{n}{u}", [P, 512], fp32)) for u in (0, 1)]
                              for n in ("xg", "h", "ht", "y"))
    x_loaded = [p.sem(f"xg_loaded{u}") for u in range(NB)]
    y_stored = [p.sem(f"yg_stored{u}") for u in range(NB)]
    x_turned, x_copied = p.sem("xg_turned"), p.sem("xg_copied")
    h_made, h_biased, h_stats = p.sem("h_made"), p.sem("h_biased"), p.sem("h_stats_done")
    h_var, h_rstd, h_normed = p.sem("h_var_done"), p.sem("h_rstd_done"), p.sem("h_normed")
    h_scaled, h_gelu = p.sem("h_scaled"), p.sem("h_gelu")
    h_turned, h_copied = p.sem("h_turned"), p.sem("h_copied")
    y_made, y_biased = p.sem("yg_made"), p.sem("yg_biased")
    LAG_UP, LAG_NORM, LAG_GELU, LAG_DOWN, LAG_STORE = 1, 2, 3, 4, 5

    with nc.Block() as block:
        @block.sync
        def _(sp):
            def load(j, u):
                sp.wait_ge(x_turned, j + 1)
                sp.dma_start(xg[u][:], c["slots_in0"][bass.ds(j * P, P), :]).then_inc(x_loaded[u], 16)

            in_steps(sp, TILES0, [(0, load)], NB)
            for u in range(NB):
                sp.wait_ge(y_stored[u], 16 * (TILES0 // NB + 1))

        @block.tensor
        def _(pe):
            pe.sem_inc(x_turned, NB)
            pe.sem_inc(h_turned, 2)
            pe.sem_inc(h_made, 2)
            pe.sem_inc(y_made, 2)

            def turn_x(j, u):
                pe.wait_ge(x_loaded[u], use_of(j, u, NB) * 16 + 16)
                pe.wait_ge(x_copied, j + 1)
                for k in range(KT):
                    last = nc.tensor.transpose(ps_x[u % 2][:, k * P:(k + 1) * P], xg[u][:, k * P:(k + 1) * P], c["ident"][:])
                last.then_inc(x_turned, 1)

            def up(j, u):
                e = pe.value_load(TE[0:1, bass.ds(j, 1)], min_val=0, max_val=E0 - 1)
                pe.wait_ge(x_copied, j + 3)
                pe.wait_ge(h_biased, j + 1)
                for k in range(KT):
                    last = nc.tensor.matmul(ps_h[u % 2][:], xt[u % 2][:, k], W1[:, bass.ds(e, 1), k].rearrange("p o h -> p (o h)"),
                                            start=k == 0, stop=k == KT - 1)
                last.then_inc(h_made, 1)

            def turn_h(j, u):
                pe.wait_ge(h_gelu, j + 1 + NB)
                pe.wait_ge(h_copied, j + 1)
                for k in range(HT0):
                    last = nc.tensor.transpose(ps_t[u % 2][:, k * P:(k + 1) * P], gs[u % 2][:, k * P:(k + 1) * P], c["ident"][:])
                last.then_inc(h_turned, 1)

            def down(j, u):
                e = pe.value_load(TE[0:1, bass.ds(j, 1)], min_val=0, max_val=E0 - 1)
                pe.wait_ge(h_copied, j + 3)
                pe.wait_ge(y_biased, j + 1)
                for k in range(HT0):
                    last = nc.tensor.matmul(ps_y[u % 2][:, 0:D], ht[u % 2][:, k], W2[:, bass.ds(e, 1), k].rearrange("p o h -> p (o h)"),
                                            start=k == 0, stop=k == HT0 - 1)
                last.then_inc(y_made, 1)

            in_steps(pe, TILES0, [(0, turn_x), (LAG_DOWN, turn_h), (LAG_UP, up), (LAG_DOWN, down)], NB)

        @block.scalar
        def _(act):
            act.sem_inc(x_copied, 2)
            act.sem_inc(h_gelu, NB)
            act.sem_inc(h_copied, 2)

            def copy_x(j, u):
                act.wait_ge(x_turned, j + 1 + NB)
                act.wait_ge(h_made, j + 1)
                nc.scalar.activation(xt[u % 2][:].rearrange("p k t -> p (k t)"), ps_x[u % 2][:, 0:D], ACT.Copy).then_inc(x_copied, 1)

            def gelu(j, u):
                act.wait_ge(h_scaled, j * 2 + 2)
                act.wait_ge(h_turned, j + 1)
                nc.scalar.activation(gs[u % 2][:], hs[u][:], ACT.Gelu).then_inc(h_gelu, 1)

            def copy_h(j, u):
                act.wait_ge(h_turned, j + 3)
                act.wait_ge(y_made, j + 1)
                nc.scalar.activation(ht[u % 2][:].rearrange("p k t -> p (k t)"), ps_t[u % 2][:], ACT.Copy).then_inc(h_copied, 1)

            def store(j, u):
                act.wait_ge(y_biased, j + 3)
                act.dma_start(c["slots_out0"][bass.ds(j * P, P), :], ys[u][:]).then_inc(y_stored[u], 16)

            for u in range(NB):
                act.sem_inc(y_stored[u], 16)
            in_steps(act, TILES0, [(0, copy_x), (LAG_DOWN, copy_h), (LAG_GELU, gelu), (LAG_STORE, store)], NB)

        @block.vector
        def _(dve):
            dve.sem_inc(h_biased, 2)
            dve.sem_inc(y_biased, 2)

            def stats(j, u):
                e = dve.value_load(TE[0:1, bass.ds(j, 1)], min_val=0, max_val=E0 - 1)
                dve.wait_ge(h_made, j + 3)
                dve.wait_ge(h_gelu, j + 1)
                nc.vector.tensor_tensor(hs[u][:], ps_h[u % 2][:], B1[:, bass.ds(e, 1), :].rearrange("p o h -> p (o h)"),
                                        ALU.add).then_inc(h_biased, 1)
                dve.wait_ge(h_biased, j + 3)
                nc.vector.bn_stats(st[:, u], hs[u][:]).then_inc(h_stats, 1)
                dve.wait_ge(h_stats, j * 2 + 1)
                nc.vector.memset(hold[:], 0.0)
                nc.vector.bn_aggr(mv[:, u], st[:, u]).then_inc(h_stats, 1)
                dve.wait_ge(h_stats, j * 2 + 2)
                nc.vector.tensor_scalar(ve[:, u:u + 1], mv[:, u, 1:2], EPS, None, ALU.add).then_inc(h_var, 1)

            def norm(j, u):
                dve.wait_ge(h_rstd, j + 1)
                nc.vector.tensor_scalar(hs[u][:], hs[u][:], mv[:, u, 0:1], rs[:, u:u + 1], ALU.subtract, ALU.mult)\
                    .then_inc(h_normed, 1)

            def bias_y(j, u):
                e = dve.value_load(TE[0:1, bass.ds(j, 1)], min_val=0, max_val=E0 - 1)
                dve.wait_ge(y_made, j + 3)
                dve.wait_ge(y_stored[u], use_of(j, u, NB) * 16 + 16)
                nc.vector.tensor_tensor(ys[u][:], ps_y[u % 2][:, 0:D], B2[:, bass.ds(e, 1), :].rearrange("p o h -> p (o h)"),
                                        ALU.add).then_inc(y_biased, 1)

            in_steps(dve, TILES0, [(LAG_NORM, norm), (LAG_UP, stats), (LAG_DOWN, bias_y)], NB)

        @block.gpsimd
        def _(pool):
            def inverse(j, u):
                pool.wait_ge(h_var, j + 1)
                nc.gpsimd.tensor_tensor(rs[:, u:u + 1], ve[:, u:u + 1], c["minus_half"][:, 0:1], ALU.pow).then_inc(h_rstd, 1)

            def scale(j, u):
                e = pool.value_load(TE[0:1, bass.ds(j, 1)], min_val=0, max_val=E0 - 1)
                pool.wait_ge(h_normed, j + 1)
                nc.gpsimd.tensor_tensor(hs[u][:], hs[u][:], G[:, bass.ds(e, 1), :].rearrange("p o h -> p (o h)"), ALU.mult)\
                    .then_inc(h_scaled, 1)
                pool.wait_ge(h_scaled, j * 2 + 1)
                nc.gpsimd.tensor_tensor(hs[u][:], hs[u][:], BB[:, bass.ds(e, 1), :].rearrange("p o h -> p (o h)"), ALU.add)\
                    .then_inc(h_scaled, 1)

            in_steps(pool, TILES0, [(LAG_NORM, scale), (LAG_UP, inverse)], NB)
    psum.close()


def use_of(j, u, buffers=2):
    return (j - u) // buffers


def combine_first(p, c):
    nc = p.nc
    X, XN, W, SLOT = c["x"], c["xn"], c["weight"], c["slot"]
    start = p.top
    NB = 4
    NF = 8
    LAG_POW, LAG_NORM = 3, 5
    LAG_POW_Q, LAG_NORM_Q, LAG_LOW_Q = 7, 8, 14
    yk = [p.sb(f"y_rows{n}", [P, K0, D], fp32) for n in range(NB)]
    f = [p.sb(f"ffn{n}", [P, D], fp32) for n in range(NF)]
    gb = [p.sb(f"m0_{n}", [P, D], fp32) for n in ("ln_gb", "ln_bb")]
    st = p.sb("f_stats", [P, NF, 6], fp32)
    mv = p.sb("f_mean_var", [P, NF, 2], fp32)
    ve = p.sb("f_var", [P, NF], fp32)
    rs = p.sb("f_rstd", [P, NF], fp32)
    q = Queries(p, c, 1)
    p.top = start
    loaded = p.sem("ln_loaded")
    gathered = [p.pool_dma_sem(f"y_gathered{n}") for n in range(NB)]
    first, used = p.sem("y_first_used"), p.sem("y_rows_used")
    stats_done, aggregated, var_done, rstd_done = (p.sem("f_" + n) for n in ("stats_done", "aggregated", "var_done", "rstd_done"))
    normed, scaled, added = p.sem("f_normed"), p.sem("f_scaled"), p.sem("f_added")
    done, done_stats = p.sem("x_mixture_added"), p.sem("x_new_stats")
    with nc.Block() as block:
        @block.sync
        def _(sp):
            for buf, n in zip(gb, ("ln_g", "ln_b")):
                sp.dma_start(buf[:], across_partitions(p.dram["m0_" + n], D)).then_inc(loaded, 16)
            for b in range(B):
                q.store(sp, b, b % 2)
            q.end(sp)

        @block.tensor
        def _(pe):
            q.begin_pe(pe)
            in_steps(pe, B, [(0, on(pe, q.transposes)), (1, on(pe, q.project))])

        @block.scalar
        def _(act):
            q.begin_act(act)
            in_steps(act, B, [(0, on(act, q.copy)), (1, on(act, q.high))])

        @block.gpsimd
        def _(pool):
            table = c["slots_out0"]
            for t in range(NT + LAG_POW_Q):
                if t < NT:
                    if t >= NB:
                        pool.wait_ge(used, t - NB + 1)
                    for k in range(K0):
                        nc.gpsimd.indirect_dma_start(yk[t % NB][:, k], None, table,
                                                     bass.IndirectOffsetOnAxis(ap=SLOT[:, k, t:t + 1], axis=0))\
                            .then_inc(gathered[t % NB], 16)
                if LAG_POW <= t < NT + LAG_POW:
                    u = (t - LAG_POW) % NF
                    pool.wait_ge(var_done, t - LAG_POW + 1)
                    nc.gpsimd.tensor_tensor(rs[:, u:u + 1], ve[:, u:u + 1], c["minus_half"][:, 0:1], ALU.pow)\
                        .then_inc(rstd_done, 1)
                b = (t - LAG_POW_Q) // TB
                if t >= LAG_POW_Q and (t - LAG_POW_Q) % TB == TB - 1:
                    q.invert(pool, b + 1, range(b * TB, (b + 1) * TB))

        @block.vector
        def _(dve):
            dve.wait_ge(loaded, 32)
            def weigh(t):
                dve.wait_ge(gathered[t % NB], 16 * K0 * (t // NB + 1))
                nc.vector.scalar_tensor_tensor(f[t % NF][:], yk[t % NB][:, 0], W[:, 0, t:t + 1], XN[:, t], ALU.mult, ALU.add)\
                    .then_inc(first, 1)

            def weigh_second(t):
                dve.wait_ge(first, t + 1)
                nc.vector.scalar_tensor_tensor(f[t % NF][:], yk[t % NB][:, 1], W[:, 1, t:t + 1], f[t % NF][:], ALU.mult, ALU.add)\
                    .then_inc(used, 1)

            def stats(t):
                dve.wait_ge(used, t + 1)
                nc.vector.bn_stats(st[:, t % NF], f[t % NF][:]).then_inc(stats_done, 1)

            def aggregate(t):
                dve.wait_ge(stats_done, t + 1)
                nc.vector.bn_aggr(mv[:, t % NF], st[:, t % NF]).then_inc(aggregated, 1)

            def variance(t):
                dve.wait_ge(aggregated, t + 1)
                nc.vector.tensor_scalar(ve[:, t % NF:t % NF + 1], mv[:, t % NF, 1:2], EPS, None, ALU.add).then_inc(var_done, 1)

            def norm(t):
                dve.wait_ge(rstd_done, t + 1)
                nc.vector.tensor_scalar(f[t % NF][:], f[t % NF][:], mv[:, t % NF, 0:1], rs[:, t % NF:t % NF + 1],
                                        ALU.subtract, ALU.mult).then_inc(normed, 1)

            def scale(t):
                dve.wait_ge(normed, t + 1)
                nc.vector.tensor_tensor(f[t % NF][:], f[t % NF][:], gb[0][:], ALU.mult).then_inc(scaled, 1)

            def add(t):
                dve.wait_ge(scaled, t + 1)
                nc.vector.tensor_tensor(f[t % NF][:], f[t % NF][:], X[:, t], ALU.add).then_inc(added, 1)

            def shift(t):
                dve.wait_ge(added, t + 1)
                nc.vector.tensor_tensor(X[:, t], f[t % NF][:], gb[1][:], ALU.add).then_inc(done, 1)

            def new_stats(t):
                dve.wait_ge(done, t + 1)
                nc.vector.bn_stats(c["stats"][:, t], X[:, t]).then_inc(done_stats, 1)

            stages = [(0, weigh), (LAG_NORM, norm), (0, weigh_second), (LAG_NORM, scale), (1, stats), (LAG_NORM, add), (1, aggregate),
                      (LAG_NORM, shift), (1, variance), (LAG_NORM, new_stats)]
            q.begin_dve(dve)

            def batch_of(t):
                return t // TB if 0 <= t < NT and t % TB == TB - 1 else None

            for s in range(NT + LAG_LOW_Q):
                for lag, f_ in stages:
                    if 0 <= s - lag < NT:
                        f_(s - lag)
                b = batch_of(s - LAG_NORM_Q + 2)
                if b is not None:
                    dve.wait_ge(done_stats, (b + 1) * TB)
                    q.aggregate(dve, range(b * TB, (b + 1) * TB))
                b = batch_of(s - LAG_NORM_Q)
                if b is not None:
                    dve.wait_ge(q.rstd_done, b + 1)
                    q.norm(dve, b, b % 2)
                b = batch_of(s - LAG_LOW_Q)
                if b is not None:
                    q.low(dve, b, b % 2)
    q.psum.close()


class Gated:

    def __init__(self, p):
        nc = self.nc = p.nc
        self.p = p
        self.shared = p.sb("m1_shared", [P, 3, KT, D], fp32)
        self.shared_parts = [p.sb(f"m1_shared_{part}", [P, 3, KT, D], fp32r) for part in ("high", "low")]
        self.xp = self.parts("xet", [P, KT, CAP], 2)
        self.sl = [p.sb(f"silu{u}", [P, HT1, CAP], fp32) for u in (0, 1)]
        self.gt = [p.sb(f"gated{u}", [P, HT1, CAP], fp32) for u in (0, 1)]
        self.gp = self.parts("gated", [P, HT1, CAP], 2)
        self.psum = ExitStack()
        self.ps_a, self.ps_b, self.ps_y = (self.psum.enter_context(nc.psum_tensor(f"ps_m1{n}", [P, 2, 512], fp32)) for n in "aby")
        self.shared_loaded, self.shared_high, self.shared_low = (p.sem("shared_w_" + n) for n in ("loaded", "high", "low"))
        self.x_high, self.x_low = p.sem("xe_high"), p.sem("xe_low")
        self.up_made = p.sem("m1_up_made")
        self.silu_done = p.sem("m1_silu_done")
        self.gated = p.sem("m1_gated")
        self.g_high, self.g_low = p.sem("m1_g_high"), p.sem("m1_g_low")
        self.down_made = p.sem("m1_down_made")
        self.y_copied = p.sem("m1_y_copied")
        self.NB = 4

    def parts(self, name, shape, n):
        return [[self.p.sb(f"{name}_{part}{u}", shape, fp32r) for u in range(n)] for part in ("high", "low")]

    def begin_pe(self, pe):
        pe.sem_inc(self.up_made, 2 * HT1)
        pe.sem_inc(self.down_made, self.NB)

    def begin_dve(self, dve):
        dve.sem_inc(self.x_low, 1)
        dve.sem_inc(self.gated, 2 * HT1)
        dve.sem_inc(self.g_low, 2)
        dve.sem_inc(self.y_copied, 2)

    def product(self, out, left, right):
        steps = [(a, b, k) for k in range(KT) for a, b in ((0, 0), (0, 1), (1, 0))]
        for n, (a, b, k) in enumerate(steps):
            last = self.nc.tensor.matmul(out, left(a, k), right(b, k), start=n == 0, stop=n == len(steps) - 1)
        return last

    def up(self, pe, item, u, weight, n):
        pe.wait_ge(self.x_low, item + 2)
        for m in range(HT1):
            pe.wait_ge(self.gated, (item + 1) * HT1 + m + 1)
            for i, ps in enumerate((self.ps_a, self.ps_b)):
                last = self.product(ps[:, m, 0:n], lambda part, k: weight(part)[:, i, k, m * P:(m + 1) * P],
                                    lambda part, k: self.xp[part][u][:, k, 0:n])
            last.then_inc(self.up_made, 1)

    def down(self, pe, item, u, weight, tiles):
        pe.wait_ge(self.g_low, item + 3)
        pe.wait_ge(self.y_copied, item + 2)
        for s, (at, n) in enumerate(tiles):
            last = self.product(self.ps_y[0:n, s // 2, s % 2 * D:s % 2 * D + D],
                                lambda part, k: self.gp[part][u][:, k, at:at + n], lambda part, k: weight(part)[:, k])
        last.then_inc(self.down_made, 1)

    def high_x(self, act, item, u, x, n):
        act.wait_ge(self.up_made, (item + 1) * HT1)
        self.nc.scalar.activation(self.xp[0][u][:, :, 0:n], x, ACT.Copy).then_inc(self.x_high, 1)

    def silu(self, act, item, u, n):
        for m in range(HT1):
            act.wait_ge(self.up_made, (item + 2) * HT1 + m + 1)
            act.wait_ge(self.gated, item * HT1 + m + 1)
            self.nc.scalar.activation(self.sl[u][:, m, 0:n], self.ps_a[:, m, 0:n], ACT.Silu).then_inc(self.silu_done, 1)

    def high_gated(self, act, item, u, n):
        act.wait_ge(self.down_made, item - 1 + self.NB)
        act.wait_ge(self.gated, (item + 3) * HT1)
        self.nc.scalar.activation(self.gp[0][u][:, :, 0:n], self.gt[u][:, :, 0:n], ACT.Copy).then_inc(self.g_high, 1)

    def low_x(self, dve, item, u, x, n):
        dve.wait_ge(self.x_high, item + 1)
        self.nc.vector.tensor_tensor(self.xp[1][u][:, :, 0:n], x, self.xp[0][u][:, :, 0:n].bitcast(fp32), ALU.subtract)\
            .then_inc(self.x_low, 1)

    def gate(self, dve, item, u, n):
        dve.wait_ge(self.g_low, item + 1)
        for m in range(HT1):
            dve.wait_ge(self.silu_done, item * HT1 + m + 1)
            self.nc.vector.tensor_tensor(self.gt[u][:, m, 0:n], self.ps_b[:, m, 0:n], self.sl[u][:, m, 0:n], ALU.mult)\
                .then_inc(self.gated, 1)

    def low_gated(self, dve, item, u, n):
        dve.wait_ge(self.g_high, item + 1)
        self.nc.vector.tensor_tensor(self.gp[1][u][:, :, 0:n], self.gt[u][:, :, 0:n], self.gp[0][u][:, :, 0:n].bitcast(fp32),
                                     ALU.subtract).then_inc(self.g_low, 1)


def experts_second(p, c, R, F):
    nc, d = p.nc, p.dram
    NS = len(SLOT_TILES)
    FULL = sum(n == P for _, n in SLOT_TILES)
    LAST = SLOT_TILES[-1][1] % P
    NB = F.NB
    start = p.top
    w = [p.sb(f"m1_w{u}", [P, 3, KT, D], fp32) for u in range(NB)]
    upw = F.parts("m1_w13", [P, 2, KT, D], 2)
    dnw = F.parts("m1_w2", [P, KT, D], NB)
    xe = [p.sb(f"xe{u}", [P, NS, D], fp32) for u in range(NB)]
    ys = [p.sb(f"ye{u}", [P, NS, D], fp32) for u in range(NB)]
    p.top = start
    psum = ExitStack()
    ps_x = psum.enter_context(nc.psum_tensor("ps_m1x", [P, 2, 512], fp32))
    w_loaded = [p.sem(f"w_loaded{u}") for u in range(NB)]
    x_loaded = [p.sem(f"xe_loaded{u}") for u in range(NB)]
    y_stored = [p.sem(f"ye_stored{u}") for u in range(NB)]
    w_high, w_low = p.sem("m1_w_high"), p.sem("m1_w_low")
    x_turned, y_half = p.sem("xe_turned"), p.sem("m1_y_half")

    with nc.Block() as block:
        @block.sync
        def _(sp):
            def load_weights(e, u):
                sp.wait_ge(w_low, e * 2 + 2)
                for n, name in enumerate(("w1", "w3", "w2")):
                    sp.dma_start(w[u][:, n], d["m1_" + name][bass.ds(e, 1)].rearrange("o (k p) h -> p (o k) h", p=P))\
                        .then_inc(w_loaded[u], 16)

            def load_rows(e, u):
                if isinstance(e, int) and e == 0:
                    sp.wait_ge(R.xn_kept, B + 2)
                sp.wait_ge(x_turned, e + 1)
                sp.dma_start(xe[u][:, 0:FULL], c["slots_in1"][bass.ds(e * CAP, FULL * P), :].rearrange("(s p) d -> p s d", p=P))\
                    .then_inc(x_loaded[u], 16)
                sp.dma_start(xe[u][0:LAST, FULL], c["slots_in1"][bass.ds(e * CAP + FULL * P, LAST), :])\
                    .then_inc(x_loaded[u], 16)

            in_steps(sp, E1, [(1, load_rows), (0, load_weights)], NB)
            for n, name in enumerate(("sw1", "sw3", "sw2")):
                sp.dma_start(F.shared[:, n], d["m1_" + name].rearrange("(k p) h -> p k h", p=P)).then_inc(F.shared_loaded, 16)
            for u in range(NB):
                sp.wait_ge(y_stored[u], 32 * (E1 // NB + 1))

        @block.gpsimd
        def _(pool):
            R.scatter(pool, B - 1, (B - 1) % 2)
            pool.sem_inc(w_low, 2 * NB)

            def split(e, u):
                pool.wait_ge(w_high, e * 2 + 1)
                nc.gpsimd.tensor_tensor(upw[1][u % 2][:], w[u][:, 0:2], upw[0][u % 2][:].bitcast(fp32), ALU.subtract)\
                    .then_inc(w_low, 1)
                pool.wait_ge(w_high, e * 2 + 2)
                nc.gpsimd.tensor_tensor(dnw[1][u][:], w[u][:, 2], dnw[0][u][:].bitcast(fp32), ALU.subtract).then_inc(w_low, 1)

            in_steps(pool, E1, [(0, split)], NB)
            pool.wait_ge(F.shared_high, 1)
            nc.gpsimd.tensor_tensor(F.shared_parts[1][:], F.shared[:], F.shared_parts[0][:].bitcast(fp32), ALU.subtract)\
                .then_inc(F.shared_low, 1)

        @block.tensor
        def _(pe):
            F.begin_pe(pe)
            pe.sem_inc(x_turned, NB)

            def turn(e, u):
                pe.wait_ge(x_loaded[u], use_of(e, u, NB) * 32 + 32)
                pe.wait_ge(F.x_low, e + 1)
                for k in range(KT):
                    for s, (at, n) in enumerate(SLOT_TILES):
                        last = nc.tensor.transpose(ps_x[:, k, at:at + n], xe[u][0:n, s, k * P:(k + 1) * P],
                                                   c["ident"][0:n, 0:n])
                last.then_inc(x_turned, 1)

            def up(e, u):
                pe.wait_ge(w_low, e * 2 + 1 + 2 * NB)
                F.up(pe, e, u % 2, lambda part: upw[part][u % 2], CAP)

            def down(e, u):
                pe.wait_ge(w_low, e * 2 + 2 + 2 * NB)
                F.down(pe, e, u % 2, lambda part: dnw[part][u], SLOT_TILES)

            in_steps(pe, E1, [(0, turn), (1, up), (2, down)], NB)

        @block.scalar
        def _(act):
            def high_slots(e, u):
                act.wait_ge(x_turned, e + 1 + NB)
                F.high_x(act, e, u % 2, ps_x[:, :, 0:CAP], CAP)

            def high_weights(e, u):
                act.wait_ge(w_loaded[u], use_of(e, u, NB) * 48 + 48)
                act.wait_ge(F.up_made, (e + 1) * HT1)
                nc.scalar.activation(upw[0][u % 2][:], w[u][:, 0:2], ACT.Copy).then_inc(w_high, 1)
                act.wait_ge(F.down_made, e + 1)
                nc.scalar.activation(dnw[0][u][:], w[u][:, 2], ACT.Copy).then_inc(w_high, 1)

            def store(e, u):
                act.wait_ge(F.y_copied, e + 1 + 2)
                act.dma_start(c["slots_out1"][bass.ds(e * CAP, FULL * P), :].rearrange("(s p) d -> p s d", p=P), ys[u][:, 0:FULL])\
                    .then_inc(y_stored[u], 16)
                act.dma_start(c["slots_out1"][bass.ds(e * CAP + FULL * P, LAST), :], ys[u][0:LAST, FULL])\
                    .then_inc(y_stored[u], 16)

            for u in range(NB):
                act.sem_inc(y_stored[u], 32)
            in_steps(act, E1, [(0, high_slots), (0, high_weights), (1, lambda e, u: F.silu(act, e, u % 2, CAP)),
                               (1, lambda e, u: F.high_gated(act, e, u % 2, CAP)), (3, store)], NB)
            act.wait_ge(F.shared_loaded, 48)
            nc.scalar.activation(F.shared_parts[0][:], F.shared[:], ACT.Copy).then_inc(F.shared_high, 1)

        @block.vector
        def _(dve):
            F.begin_dve(dve)

            def copy_y(e, u):
                dve.wait_ge(F.down_made, e + 1 + NB)
                dve.wait_ge(y_stored[u], use_of(e, u, NB) * 32 + 32)
                nc.vector.tensor_copy(ys[u][:, 0:FULL], F.ps_y[:, 0].rearrange("p (t d) -> p t d", t=FULL)).then_inc(y_half, 1)
                nc.vector.tensor_copy(ys[u][0:LAST, FULL], F.ps_y[0:LAST, 1, 0:D]).then_inc(F.y_copied, 1)

            in_steps(dve, E1, [(0, lambda e, u: F.low_x(dve, e, u % 2, ps_x[:, :, 0:CAP], CAP)),
                               (1, lambda e, u: F.gate(dve, e, u % 2, CAP)), (1, lambda e, u: F.low_gated(dve, e, u % 2, CAP)),
                               (2, copy_y)], NB)
    psum.close()


def combine_second(p, c, F):
    nc = p.nc
    X, XNT, W, SLOT = c["x"], c["xnt"], c["weight"], c["slot_read"]
    start = p.top
    NB = 8
    yk = [p.sb(f"z_rows{n}", [P, K1, D], fp32) for n in range(NB)]
    p.top = start
    gathered = [p.pool_dma_sem(f"z_gathered{n}") for n in range(NB)]
    added, done = p.sem("z_added"), p.sem("out_stored")
    out = p.dram["out"].rearrange("(t p) d -> t p d", p=P)
    with nc.Block() as block:
        @block.sync
        def _(sp):
            for t in range(NT):
                sp.wait_ge(added, K1 * (t + 1))
                sp.dma_start(out[t], X[:, t]).then_inc(done, 16)
            sp.wait_ge(done, 16 * NT)

        @block.gpsimd
        def _(pool):
            for t in range(NT):
                if t >= NB:
                    pool.wait_ge(added, K1 * (t - NB + 1))
                for k in range(K1):
                    nc.gpsimd.indirect_dma_start(yk[t % NB][:, k], None, c["slots_out1"],
                                                 bass.IndirectOffsetOnAxis(ap=SLOT[:, k, t:t + 1], axis=0))\
                        .then_inc(gathered[t % NB], 16)

        @block.tensor
        def _(pe):
            pe.wait_ge(F.shared_low, 1)
            in_steps(pe, B, [(0, lambda b, u: F.up(pe, E1 + b, u, lambda part: F.shared_parts[part][:, 0:2], S)),
                             (2, lambda b, u: F.down(pe, E1 + b, u, lambda part: F.shared_parts[part][:, 2], [(0, P), (P, P)]))])

        @block.scalar
        def _(act):
            in_steps(act, B, [(0, lambda b, u: F.high_x(act, E1 + b, u, XNT[:, :, bass.ds(b * S, S)], S)),
                              (1, lambda b, u: F.silu(act, E1 + b, u, S)), (1, lambda b, u: F.high_gated(act, E1 + b, u, S))])

        @block.vector
        def _(dve):
            def add_shared(b):
                dve.wait_ge(F.down_made, E1 + b + 1 + F.NB)
                at = X[:, b * TB:(b + 1) * TB]
                nc.vector.tensor_tensor(at, F.ps_y[:, 0].rearrange("p (t d) -> p t d", t=TB), at, ALU.add).then_inc(F.y_copied, 1)
                dve.wait_ge(F.y_copied, E1 + b + 3)

            def add_chosen(t):
                dve.wait_ge(gathered[t % NB], 16 * K1 * (t // NB + 1))
                for k in range(K1):
                    nc.vector.scalar_tensor_tensor(X[:, t], yk[t % NB][:, k], W[:, k, t:t + 1], X[:, t], ALU.mult, ALU.add)\
                        .then_inc(added, 1)
                    dve.wait_ge(added, K1 * t + k + 1)

            for s in range(B + 3):
                if s < B:
                    F.low_x(dve, E1 + s, s % 2, XNT[:, :, s * S:(s + 1) * S], S)
                if s >= 3:
                    add_shared(s - 3)
                if 1 <= s <= B:
                    F.gate(dve, E1 + s - 1, (s - 1) % 2, S)
                    F.low_gated(dve, E1 + s - 1, (s - 1) % 2, S)
                if s >= 3:
                    for t in range((s - 3) * TB, (s - 2) * TB):
                        add_chosen(t)
    F.psum.close()


def prepare_mixtures(p, c):
    c["w1"] = p.sb("m0_w1", [P, E0, KT, H0], fp32)
    c["m0_ln1_g"] = p.sb("m0_ln1_gb", [P, E0, H0], fp32)
    for l, n in ((0, TILES0 * P), (1, SLOTS1)):
        c[f"slots_in{l}"] = p.scratch(f"slots_in{l}", [n, D], fp32)
        c[f"slots_out{l}"] = p.scratch(f"slots_out{l}", [n, D], fp32)
    c["filled"] = p.sem("mixtures_filled")
    assert E0 == B
    c["FILLS"] = 4

    def fill(sp, b):
        for l in (0, 1):
            rows = c[f"slots_in{l}"].rearrange("(b p n) d -> b p n d", b=B, p=P)
            sp.dma_start(rows[bass.ds(b, 1)].rearrange("o p n d -> p (o n) d"),
                         c["zero_row"][:].unsqueeze(1).broadcast_to([P, rows.shape[2], D])).then_inc(c["filled"], 16)
        sp.dma_start(c["w1"][:, bass.ds(b, 1)].rearrange("p o k h -> p (o k) h"),
                     p.dram["m0_w1"][bass.ds(b, 1)].rearrange("o (k p) h -> p (o k) h", p=P)).then_inc(c["filled"], 16)
        sp.dma_start(c["m0_ln1_g"][:, bass.ds(b, 1)].rearrange("p o h -> p (o h)"),
                     p.dram["m0_ln1_g"][bass.ds(b, 1)].broadcast_to([P, H0])).then_inc(c["filled"], 16)
    return fill


def program(nc, dram):
    p = Program(nc, dram)
    with p.lasting:
        c = load_constants(p)
        routing_constants(p, c)
        lasting = p.top
        routing_results(p, c, 0, E0, K0)
        fill = prepare_mixtures(p, c)
        kept = p.top
        first_projections(p, c)
        attention(p, c, 0, Routing(p, c, 0, E0, K0), fill)
        p.top = kept
        place_first(p, c)
        experts_first(p, c)
        p.top = c["below_experts"]
        combine_first(p, c)
        p.top = lasting
        p.renew_semaphores()
        routing_results(p, c, 1, E1, K1)
        routing = Routing(p, c, 1, E1, K1)
        kept = p.top
        attention(p, c, 1, routing, None)
        p.top = kept
        shared = Gated(p)
        experts_second(p, c, routing, shared)
        combine_second(p, c, shared)
        p.stack.close()


def laid_out(inputs):
    def w_t(w):
        return w.T.reshape(KT, P, -1).transpose(1, 0, 2)

    a = {}
    a["x"] = inputs["x"].reshape(N, D)
    a["ctx"] = inputs["ctx_1024"].transpose(0, 2, 1).reshape(B, KT, P, S).transpose(0, 2, 1, 3)
    mask = inputs["mask_1x1xSxS2_ik0"].reshape(S, S)
    a["mask_qk"] = mask.reshape(TB, P, S).transpose(1, 0, 2)
    a["mask_kq"] = mask.T.reshape(TB, P, S).transpose(1, 0, 2)
    for l, names in ((0, ("Wq", "Wk", "Wv", "Wo")), (1, ("Wq", "Wk", "Wv", "Wu"))):
        for n, w in zip("qkvo", names):
            a[f"w{n}{l}"] = w_t(inputs[f"L{l}_xattn_{w}"])
    for n in ("bq", "bk"):
        a[n + "0"] = inputs[f"L0_xattn_{n}"].reshape(KT, P).T
    a["bv0"], a["bo0"], a["bo1"] = inputs["L0_xattn_bv"], inputs["L0_xattn_bo"], inputs["L1_xattn_bu"]
    for n in ("gate_w", "w1", "b1", "ln1_g", "ln1_b", "w2", "b2", "ln_g", "ln_b"):
        a["m0_" + n] = inputs["L0_ffn_" + n]
    for n in ("w1", "w2", "w3", "sw1", "sw2", "sw3"):
        a["m1_" + n] = inputs["L1_ffn_" + n]
    a["m0_gate_w"] = a["m0_gate_w"].reshape(KT, P, E0).transpose(1, 0, 2)
    a["m1_gate_w"] = w_t(inputs["L1_ffn_wg"])
    return {n: np.ascontiguousarray(v) for n, v in a.items()}


def kernel(**inputs):
    import concourse.bacc as bacc
    from concourse.bass_utils import run_bass_kernel_spmd

    arrays = laid_out({n: np.asarray(v) for n, v in inputs.items()})
    nc = bacc.Bacc("TRN2", target_bir_lowering=False, num_devices=1)
    dram = {n: nc.dram_tensor(f"in_{n}", v.shape, mybir.dt.from_np(v.dtype), kind="ExternalInput").ap()
            for n, v in arrays.items()}
    dram["out"] = nc.dram_tensor("out_x", [N, D], fp32, kind="ExternalOutput").ap()
    program(nc, dram)
    result = run_bass_kernel_spmd(nc, [{f"in_{n}": v for n, v in arrays.items()}], core_ids=[0])
    return result.results[0]["out_x"].reshape(B, S, D)
```
